# Optimizing a Trainium2 kernel written in Bass

```python
import numpy as np
import jax
import jax.numpy as jnp

def _softmax(x, axis=-1):
    return jax.nn.softmax(x, axis=axis)

def _gelu(x):
    return jax.nn.gelu(x, approximate=True)

def _silu(x):
    return jax.nn.silu(x)

def _sigmoid(x):
    return jax.nn.sigmoid(x)

def _layernorm(x, axis=-1, eps=1e-05):
    m = jnp.mean(x, axis=axis, keepdims=True)
    v = jnp.var(x, axis=axis, keepdims=True)
    return (x - m) / jnp.sqrt(v + eps)

def _scatter_add(tgt, idx, src, axis=0):
    return tgt.at[idx].add(src)

def _segment_sum(src, seg, n):
    return jax.ops.segment_sum(src, seg, n)
kernel_name = 'mk_decoder_postln_d2_seqx_r8_bf3cfc'

def setup_inputs(seed: int=0):
    np.random.seed(seed)
    _w = jnp.asarray

    def _rec_inputs():
        import jax
        import jax.numpy as jnp
        _rk = jax.random.key(seed)
        x = 7.22e-05 + 1 * jax.random.normal(jax.random.fold_in(_rk, 1), (32, 64, 128), jnp.float32)
        _lenS = 64 - jax.random.randint(jax.random.fold_in(_rk, 7), (32,), 0, max(1, 64 // 4) + 1, jnp.int32)
        _lenS2 = 64 - jax.random.randint(jax.random.fold_in(_rk, 8), (32,), 0, max(1, 64 // 4) + 1, jnp.int32)
        _ctx_1024P = jax.random.normal(jax.random.fold_in(_rk, 11), (32, 16, 128), jnp.float32)
        _ctx_1024c = jax.random.dirichlet(jax.random.fold_in(_rk, 511), 0.3 * jnp.ones((16,), jnp.float32), (32, 64))
        _ctx_1024t = jnp.einsum('bsk,bkd->bsd', _ctx_1024c, _ctx_1024P)
        _ctx_1024t = _ctx_1024t * jax.lax.rsqrt(jnp.mean(jnp.square(_ctx_1024t)) + 1e-12) * 0.953939
        ctx_1024 = 4.13588e-05 + 0.999923 * (_ctx_1024t + 0.3 * jax.random.normal(jax.random.fold_in(_rk, 611), (32, 64, 128), jnp.float32))
        _validS = jnp.arange(64)[None, :] < _lenS[:, None]
        _validS2 = jnp.arange(64)[None, :] < _lenS2[:, None]
        _causal = jnp.tril(jnp.ones((64, 64), dtype=bool))
        mask_Bx1x1xS2_bk0 = jnp.logical_not(jnp.broadcast_to(_validS2[:, None, None, :], (32, 1, 1, 64)))
        return (x, ctx_1024, mask_Bx1x1xS2_bk0)
    x, ctx_1024, mask_Bx1x1xS2_bk0 = _rec_inputs()

    def _L0_attn_setup():
        import jax, jax.numpy as jnp
        import numpy as np
        B, S, E, H = (4, 512, 128, 16)
        D = E // H

        def _phi(x):
            return jax.nn.elu(x) + 1.0
        key = jax.random.key(seed)
        k1, k2, k3 = jax.random.split(key, 3)
        x = jax.random.normal(k1, (B, S, E), dtype=jnp.float32)
        W_qkv = jax.random.normal(k2, (E, 3 * E), dtype=jnp.float32) * E ** (-0.5)
        b_qkv = jnp.zeros((3 * E,), dtype=jnp.float32)
        W_proj = jax.random.normal(k3, (E, E), dtype=jnp.float32) * E ** (-0.5)
        b_proj = jnp.zeros((E,), dtype=jnp.float32)
        return {'x': x, 'W_qkv': W_qkv, 'b_qkv': b_qkv, 'W_proj': W_proj, 'b_proj': b_proj}
    _L0_attn_all = _L0_attn_setup()
    _L0_attn_in = {k: v for k, v in _L0_attn_all.items() if k in ('W_qkv', 'b_qkv', 'W_proj', 'b_proj')}
    del _L0_attn_all

    def _L0_xattn_setup():
        import jax, jax.numpy as jnp
        import numpy as np
        B, S, D, H = (4, 256, 128, 16)
        DEPTH = D // H
        NEG = 10000000000.0

        def _split_heads(x):
            b, s, _ = x.shape
            return x.reshape(b, s, H, DEPTH).transpose(0, 2, 1, 3)
        key = jax.random.key(seed)
        ks = jax.random.split(key, 11)
        sc = 0.02
        return {'q': jax.random.normal(ks[0], (B, S, D), jnp.float32), 'v': jax.random.normal(ks[1], (B, S, D), jnp.float32), 'k': jax.random.normal(ks[2], (B, S, D), jnp.float32), 'Wq': jax.random.normal(ks[3], (D, D), jnp.float32) * sc, 'bq': jnp.zeros((D,), jnp.float32), 'Wk': jax.random.normal(ks[4], (D, D), jnp.float32) * sc, 'bk': jnp.zeros((D,), jnp.float32), 'Wv': jax.random.normal(ks[5], (D, D), jnp.float32) * sc, 'bv': jnp.zeros((D,), jnp.float32), 'Wo': jax.random.normal(ks[6], (D, D), jnp.float32) * sc, 'bo': jnp.zeros((D,), jnp.float32), 'mask': 1}
    _L0_xattn_all = _L0_xattn_setup()
    _L0_xattn_in = {k: v for k, v in _L0_xattn_all.items() if k in ('Wq', 'bq', 'Wk', 'bk', 'Wv', 'bv', 'Wo', 'bo')}
    del _L0_xattn_all

    def _L0_ffn_setup():
        import jax, jax.numpy as jnp
        import numpy as np
        B, S, D, F, O = (4, 256, 128, 512, 128)
        E, NS, K = (4, 2, 2)
        key = jax.random.key(seed)
        ks = jax.random.split(key, 6)

        def w(k, shape, fan_in):
            return jax.random.normal(k, shape, jnp.float32) * fan_in ** (-0.5)
        return {'x': jax.random.normal(ks[0], (B, S, D), jnp.float32), 'gate_w': w(ks[1], (D, E), D), 'gate_b': jnp.zeros((E,), jnp.float32), 'sw1': w(ks[2], (NS, D, F), D), 'sb1': jnp.zeros((NS, F), jnp.float32), 'sw2': w(ks[3], (NS, F, O), F), 'sb2': jnp.zeros((NS, O), jnp.float32), 'rw1': w(ks[4], (E, D, F), D), 'rb1': jnp.zeros((E, F), jnp.float32), 'rw2': w(ks[5], (E, F, O), F), 'rb2': jnp.zeros((E, O), jnp.float32)}
    _L0_ffn_all = _L0_ffn_setup()
    _L0_ffn_in = {k: v for k, v in _L0_ffn_all.items() if k in ('gate_w', 'gate_b', 'sw1', 'sb1', 'sw2', 'sb2', 'rw1', 'rb1', 'rw2', 'rb2')}
    del _L0_ffn_all

    def _L1_attn_setup():
        import jax, jax.numpy as jnp
        import numpy as np
        import math
        N_HEAD = 16
        N_EMBD = 128
        HEAD_D = N_EMBD // N_HEAD
        BASE = 1250

        def rope(Y):
            d = Y.shape[-1]
            t = Y.shape[-2]
            theta = BASE ** (-2.0 * jnp.arange(d // 2, dtype=Y.dtype) / d)
            theta2 = jnp.concatenate([theta, theta], axis=0)
            pos = jnp.arange(1, t + 1, dtype=Y.dtype)
            C = pos[:, None] * theta2[None, :]
            cos, sin = (jnp.cos(C), jnp.sin(C))
            Y2 = jnp.concatenate([-Y[..., d // 2:], Y[..., :d // 2]], axis=-1)
            return Y * cos + Y2 * sin
        key = jax.random.key(seed)
        ks = jax.random.split(key, 9)
        s = 0.02
        x = jax.random.normal(ks[0], (4, 256, N_EMBD), dtype=jnp.float32)
        Wq = jax.random.normal(ks[1], (N_EMBD, N_EMBD), dtype=jnp.float32) * s
        bq = jnp.zeros((N_EMBD,), dtype=jnp.float32)
        Wk = jax.random.normal(ks[2], (N_EMBD, N_EMBD), dtype=jnp.float32) * s
        bk = jnp.zeros((N_EMBD,), dtype=jnp.float32)
        Wv = jax.random.normal(ks[3], (N_EMBD, N_EMBD), dtype=jnp.float32) * s
        bv = jnp.zeros((N_EMBD,), dtype=jnp.float32)
        Wo = jax.random.normal(ks[4], (N_EMBD, N_EMBD), dtype=jnp.float32) * s
        bo = jnp.zeros((N_EMBD,), dtype=jnp.float32)
        return {'x': x, 'Wq': Wq, 'bq': bq, 'Wk': Wk, 'bk': bk, 'Wv': Wv, 'bv': bv, 'Wo': Wo, 'bo': bo}
    _L1_attn_all = _L1_attn_setup()
    _L1_attn_in = {k: v for k, v in _L1_attn_all.items() if k in ('Wq', 'bq', 'Wk', 'bk', 'Wv', 'bv', 'Wo', 'bo')}
    del _L1_attn_all

    def _L1_xattn_setup():
        import math
        import jax, jax.numpy as jnp
        import numpy as np
        NUM_BUCKETS = 32
        MAX_DISTANCE = 128
        H = 16
        D_MODEL = 128
        D_K = D_MODEL // H

        def _relative_position_bucket(relative_position):
            nb = NUM_BUCKETS // 2
            buckets = (relative_position > 0).astype(jnp.int32) * nb
            rp = jnp.abs(relative_position)
            max_exact = nb // 2
            is_small = rp < max_exact
            rp_large = max_exact + (jnp.log(jnp.maximum(rp, 1).astype(jnp.float32) / max_exact) / math.log(MAX_DISTANCE / max_exact) * (nb - max_exact)).astype(jnp.int32)
            rp_large = jnp.minimum(rp_large, nb - 1)
            return buckets + jnp.where(is_small, rp, rp_large)
        key = jax.random.key(seed)
        ks = jax.random.split(key, 8)
        B, T_k, T_q = (4, 256, 128)
        std = D_MODEL ** (-0.5)
        inp = {'src': jax.random.normal(ks[0], (B, T_k, D_MODEL), dtype=jnp.float32), 'dst': jax.random.normal(ks[1], (B, T_q, D_MODEL), dtype=jnp.float32), 'mask': jax.random.randint(ks[2], (B, 1, 1, T_k), 0, 2).astype(bool), 'Wq': jax.random.normal(ks[3], (D_MODEL, D_MODEL), dtype=jnp.float32) * std, 'Wk': jax.random.normal(ks[4], (D_MODEL, D_MODEL), dtype=jnp.float32) * std, 'Wv': jax.random.normal(ks[5], (D_MODEL, D_MODEL), dtype=jnp.float32) * std, 'Wo': jax.random.normal(ks[6], (D_MODEL, D_MODEL), dtype=jnp.float32) * std, 'rel_bias': jax.random.normal(ks[7], (H, NUM_BUCKETS), dtype=jnp.float32) * NUM_BUCKETS ** (-0.5)}
        return inp
    _L1_xattn_all = _L1_xattn_setup()
    _L1_xattn_in = {k: v for k, v in _L1_xattn_all.items() if k in ('Wq', 'Wk', 'Wv', 'Wo', 'rel_bias')}
    del _L1_xattn_all

    def _L1_ffn_setup():
        import jax, jax.numpy as jnp
        import numpy as np
        E = 8
        key = jax.random.key(seed)
        k0, k1, k2, k3 = jax.random.split(key, 4)
        B, S, H, F = (4, 512, 128, 512)
        x = jax.random.normal(k0, (B, S, H), jnp.float32)
        Wr = jax.random.normal(k1, (E, H), jnp.float32) * 0.02
        W1 = jax.random.normal(k2, (E, H, F), jnp.float32) * 0.02
        b1 = jnp.zeros((E, F), jnp.float32)
        W2 = jax.random.normal(k3, (E, F, H), jnp.float32) * 0.02
        b2 = jnp.zeros((E, H), jnp.float32)
        return {'x': x, 'Wr': Wr, 'W1': W1, 'b1': b1, 'W2': W2, 'b2': b2}
    _L1_ffn_all = _L1_ffn_setup()
    _L1_ffn_in = {k: v for k, v in _L1_ffn_all.items() if k in ('Wr', 'W1', 'b1', 'W2', 'b2')}
    del _L1_ffn_all
    return {'x': x, 'ctx_1024': ctx_1024, 'mask_Bx1x1xS2_bk0': mask_Bx1x1xS2_bk0, 'L0_attn_W_qkv': _L0_attn_in['W_qkv'], 'L0_attn_b_qkv': _L0_attn_in['b_qkv'], 'L0_attn_W_proj': _L0_attn_in['W_proj'], 'L0_attn_b_proj': _L0_attn_in['b_proj'], 'L0_xattn_Wq': _L0_xattn_in['Wq'], 'L0_xattn_bq': _L0_xattn_in['bq'], 'L0_xattn_Wk': _L0_xattn_in['Wk'], 'L0_xattn_bk': _L0_xattn_in['bk'], 'L0_xattn_Wv': _L0_xattn_in['Wv'], 'L0_xattn_bv': _L0_xattn_in['bv'], 'L0_xattn_Wo': _L0_xattn_in['Wo'], 'L0_xattn_bo': _L0_xattn_in['bo'], 'L0_ffn_gate_w': _L0_ffn_in['gate_w'], 'L0_ffn_gate_b': _L0_ffn_in['gate_b'], 'L0_ffn_sw1': _L0_ffn_in['sw1'], 'L0_ffn_sb1': _L0_ffn_in['sb1'], 'L0_ffn_sw2': _L0_ffn_in['sw2'], 'L0_ffn_sb2': _L0_ffn_in['sb2'], 'L0_ffn_rw1': _L0_ffn_in['rw1'], 'L0_ffn_rb1': _L0_ffn_in['rb1'], 'L0_ffn_rw2': _L0_ffn_in['rw2'], 'L0_ffn_rb2': _L0_ffn_in['rb2'], 'L1_attn_Wq': _L1_attn_in['Wq'], 'L1_attn_bq': _L1_attn_in['bq'], 'L1_attn_Wk': _L1_attn_in['Wk'], 'L1_attn_bk': _L1_attn_in['bk'], 'L1_attn_Wv': _L1_attn_in['Wv'], 'L1_attn_bv': _L1_attn_in['bv'], 'L1_attn_Wo': _L1_attn_in['Wo'], 'L1_attn_bo': _L1_attn_in['bo'], 'L1_xattn_Wq': _L1_xattn_in['Wq'], 'L1_xattn_Wk': _L1_xattn_in['Wk'], 'L1_xattn_Wv': _L1_xattn_in['Wv'], 'L1_xattn_Wo': _L1_xattn_in['Wo'], 'L1_xattn_rel_bias': _L1_xattn_in['rel_bias'], 'L1_ffn_Wr': _L1_ffn_in['Wr'], 'L1_ffn_W1': _L1_ffn_in['W1'], 'L1_ffn_b1': _L1_ffn_in['b1'], 'L1_ffn_W2': _L1_ffn_in['W2'], 'L1_ffn_b2': _L1_ffn_in['b2']}

def reference(x, ctx_1024, mask_Bx1x1xS2_bk0, L0_attn_W_qkv, L0_attn_b_qkv, L0_attn_W_proj, L0_attn_b_proj, L0_xattn_Wq, L0_xattn_bq, L0_xattn_Wk, L0_xattn_bk, L0_xattn_Wv, L0_xattn_bv, L0_xattn_Wo, L0_xattn_bo, L0_ffn_gate_w, L0_ffn_gate_b, L0_ffn_sw1, L0_ffn_sb1, L0_ffn_sw2, L0_ffn_sb2, L0_ffn_rw1, L0_ffn_rb1, L0_ffn_rw2, L0_ffn_rb2, L1_attn_Wq, L1_attn_bq, L1_attn_Wk, L1_attn_bk, L1_attn_Wv, L1_attn_bv, L1_attn_Wo, L1_attn_bo, L1_xattn_Wq, L1_xattn_Wk, L1_xattn_Wv, L1_xattn_Wo, L1_xattn_rel_bias, L1_ffn_Wr, L1_ffn_W1, L1_ffn_b1, L1_ffn_W2, L1_ffn_b2):
    import jax
    import jax.numpy as jnp

    def _L0_attn_ref(x, W_qkv, b_qkv, W_proj, b_proj):
        import jax, jax.numpy as jnp
        import numpy as np
        B, S, E, H = (4, 512, 128, 16)
        D = E // H

        def _phi(x):
            return jax.nn.elu(x) + 1.0
        b, s, _ = x.shape
        qkv = (x @ W_qkv + b_qkv).reshape(b, s, 3, H, D)
        q, k, v = (qkv[:, :, 0], qkv[:, :, 1], qkv[:, :, 2])
        pq, pk = (_phi(q), _phi(k))
        kv = jnp.einsum('bshd,bshm->bhmd', pk, v)
        z = 1.0 / (jnp.einsum('bshd,bhd->bsh', pq, pk.sum(axis=1)) + 1e-06)
        attn = jnp.einsum('bshd,bhmd,bsh->bshm', pq, kv, z)
        attn = attn.reshape(b, s, H * D)
        _proj = attn @ W_proj + b_proj
        return attn

    def _L0_xattn_ref(q, v, k, Wq, bq, Wk, bk, Wv, bv, Wo, bo, mask):
        import jax, jax.numpy as jnp
        import numpy as np
        B, S, D, H = (4, 256, 128, 16)
        DEPTH = D // H
        NEG = 10000000000.0

        def _split_heads(x):
            b, s, _ = x.shape
            return x.reshape(b, s, H, DEPTH).transpose(0, 2, 1, 3)
        qh = _split_heads(q @ Wq + bq)
        kh = _split_heads(k @ Wk + bk)
        vh = _split_heads(v @ Wv + bv)
        scale = 1.0 / jnp.sqrt(jnp.asarray(DEPTH, jnp.float32))
        logits = jnp.einsum('bhqd,bhkd->bhqk', qh, kh) * scale
        if mask:
            nd, ns = (logits.shape[-2], logits.shape[-1])
            i = jnp.arange(nd)[:, None]
            j = jnp.arange(ns)[None, :]
            b = (i >= j - ns + nd).astype(logits.dtype)
            logits = logits * b - NEG * (1.0 - b)
        attn = jax.nn.softmax(logits, axis=-1)
        out = jnp.einsum('bhqk,bhkd->bhqd', attn, vh)
        out = out.transpose(0, 2, 1, 3).reshape(q.shape[0], -1, D)
        return out @ Wo + bo

    def _L0_ffn_ref(x, gate_w, gate_b, sw1, sb1, sw2, sb2, rw1, rb1, rw2, rb2):
        import jax, jax.numpy as jnp
        import numpy as np
        B, S, D, F, O = (4, 256, 128, 512, 128)
        E, NS, K = (4, 2, 2)
        weights = jax.nn.softmax(x @ gate_w + gate_b, axis=-1)
        topk_w, topk_i = jax.lax.top_k(weights, K)
        sh = jax.nn.relu(jnp.einsum('bsd,ndf->bsnf', x, sw1) + sb1)
        shared = (jnp.einsum('bsnf,nfo->bsno', sh, sw2) + sb2).sum(axis=2) / NS
        rh = jax.nn.relu(jnp.einsum('bsd,edf->bsef', x, rw1) + rb1)
        eo = jnp.einsum('bsef,efo->bseo', rh, rw2) + rb2
        gathered = jnp.take_along_axis(eo, topk_i[..., None], axis=2)
        routed = (gathered * topk_w[..., None]).sum(axis=2)
        return shared + routed

    def _L1_attn_ref(x, Wq, bq, Wk, bk, Wv, bv, Wo, bo):
        import jax, jax.numpy as jnp
        import numpy as np
        import math
        N_HEAD = 16
        N_EMBD = 128
        HEAD_D = N_EMBD // N_HEAD
        BASE = 1250

        def rope(Y):
            d = Y.shape[-1]
            t = Y.shape[-2]
            theta = BASE ** (-2.0 * jnp.arange(d // 2, dtype=Y.dtype) / d)
            theta2 = jnp.concatenate([theta, theta], axis=0)
            pos = jnp.arange(1, t + 1, dtype=Y.dtype)
            C = pos[:, None] * theta2[None, :]
            cos, sin = (jnp.cos(C), jnp.sin(C))
            Y2 = jnp.concatenate([-Y[..., d // 2:], Y[..., :d // 2]], axis=-1)
            return Y * cos + Y2 * sin
        b, t, _ = x.shape

        def split_heads(y):
            return y.reshape(b, t, N_HEAD, HEAD_D).transpose(0, 2, 1, 3)
        q = split_heads(x @ Wq.T + bq)
        k = split_heads(x @ Wk.T + bk)
        v = split_heads(x @ Wv.T + bv)
        q, k = (rope(q), rope(k))
        scale = math.sqrt(HEAD_D)
        att = jnp.einsum('bhqd,bhkd->bhqk', q, k) / scale
        mask = jnp.tril(jnp.ones((t, t), dtype=bool))
        att = jnp.where(mask, att, -jnp.inf)
        att = jax.nn.softmax(att, axis=-1)
        y = jnp.einsum('bhqk,bhkd->bhqd', att, v)
        y = y.transpose(0, 2, 1, 3).reshape(b, t, N_EMBD)
        return y @ Wo.T + bo

    def _L1_xattn_ref(src, dst, mask, Wq, Wk, Wv, Wo, rel_bias):
        import math
        import jax, jax.numpy as jnp
        import numpy as np
        NUM_BUCKETS = 32
        MAX_DISTANCE = 128
        H = 16
        D_MODEL = 128
        D_K = D_MODEL // H

        def _relative_position_bucket(relative_position):
            nb = NUM_BUCKETS // 2
            buckets = (relative_position > 0).astype(jnp.int32) * nb
            rp = jnp.abs(relative_position)
            max_exact = nb // 2
            is_small = rp < max_exact
            rp_large = max_exact + (jnp.log(jnp.maximum(rp, 1).astype(jnp.float32) / max_exact) / math.log(MAX_DISTANCE / max_exact) * (nb - max_exact)).astype(jnp.int32)
            rp_large = jnp.minimum(rp_large, nb - 1)
            return buckets + jnp.where(is_small, rp, rp_large)
        B, T_k, _ = src.shape
        T_q = dst.shape[1]
        q = (dst @ Wq.T).reshape(B, T_q, H, D_K)
        k = (src @ Wk.T).reshape(B, T_k, H, D_K)
        v = (src @ Wv.T).reshape(B, T_k, H, D_K)
        scores = jnp.einsum('bqhd,bkhd->bhqk', q, k)
        rel_pos = jnp.arange(T_k)[None, :] - jnp.arange(T_q)[:, None]
        rp_bucket = _relative_position_bucket(rel_pos)
        bias = rel_bias[:, rp_bucket]
        scores = scores + bias[None]
        scores = jnp.where(mask, scores, -1000000000.0)
        attn = jax.nn.softmax(scores, axis=-1)
        out = jnp.einsum('bhqk,bkhd->bqhd', attn, v).reshape(B, T_q, H * D_K)
        return out @ Wo.T

    def _L1_ffn_ref(x, Wr, W1, b1, W2, b2):
        import jax, jax.numpy as jnp
        import numpy as np
        E = 8
        B, S, H = x.shape
        xf = x.reshape(-1, H)
        probs = jax.nn.softmax(xf @ Wr.T, axis=-1)
        eid = E - 1
        h = jax.nn.gelu(xf @ W1[eid] + b1[eid], approximate=False)
        y = (h @ W2[eid] + b2[eid]) * probs[:, eid:eid + 1]
        return y.reshape(B, S, H)
    x = _layernorm(x + _L0_attn_ref(x, L0_attn_W_qkv, L0_attn_b_qkv, L0_attn_W_proj, L0_attn_b_proj), axis=-1)
    x = _layernorm(x + _L0_xattn_ref(x, ctx_1024, ctx_1024, L0_xattn_Wq, L0_xattn_bq, L0_xattn_Wk, L0_xattn_bk, L0_xattn_Wv, L0_xattn_bv, L0_xattn_Wo, L0_xattn_bo, 1), axis=-1)
    x = _layernorm(x + _L0_ffn_ref(x, L0_ffn_gate_w, L0_ffn_gate_b, L0_ffn_sw1, L0_ffn_sb1, L0_ffn_sw2, L0_ffn_sb2, L0_ffn_rw1, L0_ffn_rb1, L0_ffn_rw2, L0_ffn_rb2), axis=-1)
    x = _layernorm(x + _L1_attn_ref(x, L1_attn_Wq, L1_attn_bq, L1_attn_Wk, L1_attn_bk, L1_attn_Wv, L1_attn_bv, L1_attn_Wo, L1_attn_bo), axis=-1)
    x = _layernorm(x + _L1_xattn_ref(ctx_1024, x, mask_Bx1x1xS2_bk0, L1_xattn_Wq, L1_xattn_Wk, L1_xattn_Wv, L1_xattn_Wo, L1_xattn_rel_bias), axis=-1)
    x = _layernorm(x + _L1_ffn_ref(x, L1_ffn_Wr, L1_ffn_W1, L1_ffn_b1, L1_ffn_W2, L1_ffn_b2), axis=-1)
    return x

_drawn_inputs = setup_inputs


def setup_inputs(seed=0):
    import zlib

    import numpy as np

    out = dict(_drawn_inputs(seed))
    spreads = {'L0_attn_b_qkv': (0.0, 0.1),
     'L0_attn_b_proj': (0.0, 0.1),
     'L0_xattn_bq': (0.0, 2.0),
     'L0_xattn_bk': (0.0, 2.0),
     'L0_xattn_bv': (0.0, 0.1),
     'L0_xattn_bo': (0.0, 0.1),
     'L0_ffn_gate_b': (0.0, 0.1),
     'L0_ffn_sb1': (0.0, 0.1),
     'L0_ffn_sb2': (0.0, 0.1),
     'L0_ffn_rb1': (0.0, 0.1),
     'L0_ffn_rb2': (0.0, 0.1),
     'L1_attn_bq': (0.0, 0.8),
     'L1_attn_bk': (0.0, 0.8),
     'L1_attn_bv': (0.0, 0.366),
     'L1_attn_bo': (0.0, 0.1),
     'L1_ffn_b1': (0.0, 0.8),
     'L1_ffn_b2': (0.0, 0.656)}
    factors = {'L0_xattn_Wq': 8.0,
     'L0_xattn_Wk': 8.0,
     'L1_attn_Wq': 8.0,
     'L1_attn_Wk': 8.0,
     'L1_attn_Wv': 2.986,
     'L1_ffn_Wr': 8.0,
     'L1_ffn_W1': 8.0,
     'L1_ffn_W2': 7.949}
    for name, (base, spread) in spreads.items():
        noise = np.random.default_rng([zlib.crc32(name.encode()), seed]).standard_normal(out[name].shape)
        drawn = base * np.exp(spread * noise) if base else spread * noise
        out[name] = jnp.asarray(drawn.astype(out[name].dtype))
    for name, factor in factors.items():
        out[name] = (out[name] * factor).astype(out[name].dtype)
    return out
```

```python
from contextlib import ExitStack

import concourse.bass as bass
import numpy as np
from concourse import mybir

ALU = mybir.AluOpType
ACT = mybir.ActivationFunctionType
AX = mybir.AxisListType
F32 = mybir.dt.float32
F32R = mybir.dt.float32r
BF16 = mybir.dt.bfloat16

B, S, D, H = 32, 64, 128, 16
HD = D // H
P = 128
BT = P // S
T = B * S // P
CH = 4
NCH = T // CH
N = CH * P
F = 512
FB = F // P
NS, NE = 2, 4
NR1 = 8
BUCKETS = 32
EPS = 1e-5
NEG = -1e30
DEPTH = 3

def _columns(widths):
    at, out = 0, {}
    for name, width in widths:
        out[name] = slice(at, at + width)
        at += width
    return out, at


PACK_A, WIDTH_A = _columns([
    ("wq_lin", D), ("wkv_lin", 2 * D), ("bkv_lin", 2 * D), ("bq_lin", 1),
    ("ident", P), ("head_mask", H), ("block_mask", D)])
PACK_B, WIDTH_B = _columns([
    ("B_wq", D), ("B_wk", D), ("B_wv", D), ("B_wo", D), ("B_bo", D),
    ("D_wq", D), ("D_wk", D), ("D_wq_turned", D), ("D_wk_turned", D), ("D_wv", D), ("D_wo", D), ("D_bo", D),
    ("E_wq", D), ("E_wk", D), ("E_wv", D), ("E_wo", D),
    ("B_bq", 1), ("B_bk", 1), ("B_bv", 1),
    ("D_bq", 1), ("D_bk", 1), ("D_bq_turned", 1), ("D_bk_turned", 1), ("D_bv", 1),
    ("C_b1", (NS + NE) * FB), ("F_b1", FB), ("C_b2", NS + NE), ("F_b2", 1),
    ("C_gate", NE), ("F_gate", NR1), ("C_gate_bias", 1),
    ("value_mask", 2 * D), ("cos", S), ("sin", S), ("lower", NE * NE),
    ("rel_bias", H), ("buckets", P), ("causal", S), ("select", P)])
EXPERT_COLS = 2 * F
W_COLS = (NS + NE + 1) * EXPERT_COLS
W_CHUNK = W_COLS // T


def w1_block(expert, f):
    at = expert * EXPERT_COLS + f * P
    return slice(at, at + P)


def w2_block(expert, f):
    at = expert * EXPERT_COLS + F + f * P
    return slice(at, at + P)


def after(engine, semaphore, count):
    if not isinstance(count, int) or count > 0:
        engine.wait_ge(semaphore, count)


def sweep(engine, step):
    for k in range(DEPTH + 1):
        step(k, k)
    with engine.Fori(0, (T - DEPTH - 1) // 2) as i:
        step(2 * i + (DEPTH + 1), DEPTH + 1)
        step(2 * i + (DEPTH + 2), DEPTH + 2)
    for k in range(T, T + DEPTH):
        step(k, k)


def active(kk, behind):
    return 0 <= kk - behind < T


def previous_user(j, buffers, per_chunk):
    if j >= buffers:
        return j - buffers
    last = max(x for x in range(per_chunk) if x % buffers == j % buffers)
    return last - per_chunk


def build(nc, x, xT_in, ctxT_in, pack_a, pack_b, w_experts, key_mask, out):
    with ExitStack() as ctx:
        def sb(name, shape, dt=F32):
            return ctx.enter_context(nc.sbuf_tensor(name, shape, dt))

        def bank(name, banks=1):
            return ctx.enter_context(nc.psum_tensor(name, [P, 512 * banks], F32))

        def sem(name):
            return ctx.enter_context(nc.semaphore(name))

        x_nat = sb("x_nat", [P, T, D])
        xT = sb("xT", [P, T * P])
        ctxT = sb("ctxT", [P, T * P])
        pa = sb("pa", [P, WIDTH_A])
        pb = sb("pb", [P, WIDTH_B])
        w_raw = sb("w_raw", [P, 2, W_CHUNK])
        w_hi = sb("w_hi", [P, W_COLS], F32R)
        w_lo = sb("w_lo", [P, W_COLS], F32R)
        id16 = sb("id16", [P, P], BF16)
        causal = sb("causal", [P, S], BF16)
        select = sb("select", [BT, P], BF16)
        key_neg = sb("key_neg", [BT, T, S], BF16)
        rel_bias = sb("rel_bias", [P, H, S])
        bo_B = sb("bo_B", [P, D])
        bo_D = sb("bo_D", [P, D])
        b2_shared = sb("b2_shared", [P, 1])
        minus_half = sb("minus_half", [P, 1])
        x_stage = sb("x_stage", [P, 2, P])
        z = sb("z", [P, 2, 3 * D + 1])
        e_z = sb("e_z", [P, 2, 2 * D])
        r_z = sb("r_z", [P, 2, 2 * D])
        phi = sb("phi", [P, 2, 2 * D])
        kv_masked = sb("kv_masked", [P, 2, BT, D + H])
        den = sb("den", [P, H])
        den_inv = sb("den_inv", [P, H])
        o_lin = sb("o_lin", [P, D])
        kv_stage = sb("kv_stage", [P, 2, BT, 2, S])
        qk = sb("qk", [P, 2, 2 * P])
        qk_raw = sb("qk_raw", [P, 2, 4 * P])
        turned = sb("turned", [P, 2, 2 * P])
        straight = sb("straight", [P, 2, 2 * P])
        k_heads = sb("k_heads", [P, 2, BT, H, S])
        v_heads = sb("v_heads", [P, 2, BT, 2, D])
        row_max = sb("row_max", [P, H])
        shifted = sb("shifted", [P, H, S])
        probs = sb("probs", [P, 2, H, S])
        probsT = sb("probsT", [P, 2, H // 2, P])
        row_sum = sb("row_sum", [P, H])
        row_inv = sb("row_inv", [P, H])
        inv_nat = sb("inv_nat", [P, H, HD])
        invT = sb("invT", [P, 2, P])
        attnT = sb("attnT", [P, 2, P])
        mask_in = k_heads[0:BT, 1, 0, :, :].bitcast(mybir.dt.int32)
        y = sb("y", [P, CH, D])
        x_new = sb("x_new", [P, CH, D])
        stats = sb("stats", [P, CH, 6])
        mean_var = sb("mean_var", [P, CH, 2])
        var_eps = sb("var_eps", [P, CH, 1])
        rstd = sb("rstd", [P, CH, 1])
        x_hi = sb("x_hi", [P, T * P], F32R)
        x_lo = sb("x_lo", [P, T * P], F32R)
        h = probsT[:, 0, :, :].rearrange("p (i a) b -> p i (a b)", i=2)
        h_hi = sb("h_hi", [P, 2, N], F32R)
        h_lo = sb("h_lo", [P, 2, N], F32R)
        yT = probs[:, 0, :, :].rearrange("p (i a) b -> p i (a b)", i=2)
        logitsT = k_heads[0:NR1, 0, :, :, :].rearrange("p b h s -> p (b h s)")
        gates = {n: sb(n, [P, T, NR1]) for n in ("g_shifted", "g_exp", "g_probs", "g_rank", "g_weights")}
        g_max = sb("g_max", [P, T])
        g_sum = sb("g_sum", [P, T])
        g_inv = sb("g_inv", [P, T])
        g_above, g_equal, g_tied, g_before = (
            shifted[:, i * H // 4:(i + 1) * H // 4, :].rearrange("p a (b e j) -> p (a b) e j", e=NE, j=NE)
            for i in range(4))

        ps_scores = bank("ps_scores", 2)
        ps_probsT = bank("ps_probsT", 2)
        ps_qk = bank("ps_qk")
        ps_tr = bank("ps_tr")
        ps_vo = bank("ps_vo")
        ps_y = bank("ps_y")

        def names(*which):
            return [sem(f"s_{n}") for n in which]

        s_pa, s_pb, s_xT_in, s_x_in, s_ctx_in, s_mask_in, s_out = names(
            "pa", "pb", "xT_in", "x_in", "ctx_in", "mask_in", "out")
        s_w_in = [sem("s_w_in0"), sem("s_w_in1")]
        s_const, s_bias_mm, s_bo_mm, s_w_split, s_prep, s_half, s_ones, s_w_hi = names(
            "const", "bias_mm", "bo_mm", "w_split", "prep", "half", "ones", "w_hi")
        s_x_stage, s_lin_proj, s_lin_q, s_lin_kv, s_lin_exp, s_lin_phi = names(
            "x_stage", "lin_proj", "lin_q", "lin_kv", "lin_exp", "lin_phi")
        s_lin_state, s_lin_masked, s_lin_out, s_lin_den, s_lin_inv, s_lin_norm, s_lin_min = names(
            "lin_state", "lin_masked", "lin_out", "lin_den", "lin_inv", "lin_norm", "lin_min")
        s_kv_stage, s_qk_mm, s_qk, s_rope_mul, s_rope, s_k_heads, s_v_mm, s_v_heads = names(
            "kv_stage", "qk_mm", "qk", "rope_mul", "rope", "k_heads", "v_mm", "v_heads")
        s_scores, s_max, s_shifted, s_exp, s_sum, s_inv, s_inv_nat, s_invT_mm, s_invT = names(
            "scores", "max", "shifted", "exp", "sum", "inv", "inv_nat", "invT_mm", "invT")
        s_probsT_mm, s_probsT, s_attn_mm, s_attnT, s_proj = names(
            "probsT_mm", "probsT", "attn_mm", "attnT", "proj")
        s_res, s_stats, s_mean, s_var, s_rstd, s_x, s_keep, s_xT_mm, s_xT = names(
            "res", "stats", "mean", "var", "rstd", "x", "keep", "xT_mm", "xT")
        s_x_hi, s_x_lo, s_mm1, s_h, s_h_hi, s_h_lo, s_mm2, s_yT, s_y_mm, s_mix = names(
            "x_hi", "x_lo", "mm1", "h", "h_hi", "h_lo", "mm2", "yT", "y_mm", "mix")
        s_gate_mm, s_gate_row, s_gate_tr, s_gate, s_gate_exp = names(
            "gate_mm", "gate_row", "gate_tr", "gate", "gate_exp")

        def A(name, rows=P):
            return pa[0:rows, PACK_A[name]]

        def W(name, rows=P):
            return pb[0:rows, PACK_B[name]]

        def tile(t, k):
            return t[:, bass.ds(k * P, P)]

        ident = A("ident")
        GATE_STEPS = {0: 11, 1: 5}

        class Layer:

            def __init__(self, name, a, n, kvT, causal, rope, bias, bo, scale):
                self.name, self.a, self.n, self.kvT = name, a, n, kvT
                self.causal, self.rope, self.bias, self.bo, self.scale = causal, rope, bias, bo, scale

            def w(self, name):
                return W(f"{self.name}_{name}")

        layer_B = Layer("B", 0, 1, ctxT, True, False, True, bo_B, HD ** -0.5)
        layer_D = Layer("D", 1, 3, xT, True, True, True, bo_D, HD ** -0.5)
        layer_E = Layer("E", 2, 4, ctxT, False, False, False, None, 1.0)

        class Ffn:

            def __init__(self, f, n, groups, b1, b2, func, first_block, first_group):
                self.f, self.n, self.func, self.b1, self.b2 = f, n, func, b1, b2
                self.blocks = [(g, e, i) for g, es in enumerate(groups) for e in es for i in range(FB)]
                self.groups = len(groups)
                self.last = {g: max(j for j, b in enumerate(self.blocks) if b[0] == g) for g in range(len(groups))}
                self.first = {g: min(j for j, b in enumerate(self.blocks) if b[0] == g) for g in range(len(groups))}
                self.first_block, self.first_group = first_block, first_group

            def block(self, c, j):
                return c * len(self.blocks) + (self.first_block + j + 1)

            def group(self, c, g):
                return c * self.groups + (self.first_group + g + 1)

            def block_before(self, c, j, buffers):
                return self.block(c, previous_user(j, buffers, len(self.blocks)))

            def group_before(self, c, g):
                if self.groups == 1:
                    return self.group(c, -1)
                return self.group(c, previous_user(g, 2, self.groups))

            def ended(self, j):
                return next((g for g, at in self.last.items() if at == j), None)

            def chunks(self, engine, step):
                first = 1 if self.first_block == 0 else 0
                for c in range(first):
                    step(c)
                with engine.Fori(first, NCH) as c:
                    step(c)

        ffn_C = Ffn(0, 2, [[0, 1], [2], [3], [4], [5]], "C_b1", "C_b2", ACT.Relu, 0, 0)
        ffn_F = Ffn(1, 5, [[6]], "F_b1", "F_b2", ACT.Gelu, NCH * len(ffn_C.blocks), NCH * ffn_C.groups)

        block = ctx.enter_context(nc.Block())

        @block.sync
        def _(sp):
            sp.dma_start(pa[:], pack_a).then_inc(s_pa, 16)
            sp.dma_start(xT[:], xT_in).then_inc(s_xT_in, 16)
            sp.dma_start(x_nat[:], x.rearrange("(t p) d -> p t d", p=P)).then_inc(s_x_in, 16)
            sp.dma_start(pb[:], pack_b).then_inc(s_pb, 16)
            sp.dma_start(mask_in, key_mask).then_inc(s_mask_in, 16)
            sp.dma_start(ctxT[:], ctxT_in).then_inc(s_ctx_in, 16)
            for k in range(T):
                after(sp, s_w_split, k - 1)
                sp.dma_start(w_raw[:, k % 2, :], w_experts[:, k * W_CHUNK:(k + 1) * W_CHUNK])\
                  .then_inc(s_w_in[k % 2], 16)
            for c in range(NCH):
                sp.wait_ge(s_x, 5 * T + (c + 1) * CH)
                sp.dma_start(out.rearrange("(t p) d -> p t d", p=P)[:, c * CH:(c + 1) * CH, :],
                             x_nat[:, c * CH:(c + 1) * CH, :]).then_inc(s_out, 16)
            sp.wait_ge(s_out, 16 * NCH)

        @block.tensor
        def _(pe):
            def prepare():
                pe.wait_ge(s_pb, 16)
                for i, lay in enumerate((layer_B, layer_D)):
                    mm = pe.matmul(ps_y[:, i * D:(i + 1) * D], lay.w("bv").broadcast_to([P, P]), lay.w("wo"),
                                   start=True, stop=True)
                mm.then_inc(s_bo_mm, 1)
                for k in range(S):
                    for b in range(BT):
                        mm = pe.matmul(ps_scores[b * S:(b + 1) * S, k * H:(k + 1) * H],
                                       W("buckets", BUCKETS)[:, S - 1 - k:2 * S - 1 - k], W("rel_bias", BUCKETS),
                                       start=True, stop=True)
                mm.then_inc(s_bias_mm, 1)

            def linear_attention():
                pe.wait_ge(s_pa, 16)

                def step(k, kk):
                    p, q = kk % 2, (kk + 1) % 2
                    if active(kk, 0):
                        pe.wait_ge(s_x_stage, k + 1)
                        after(pe, s_lin_q, k)
                        pe.matmul(ps_qk[:, 0:P], A("wq_lin"), x_stage[:, p, :], start=True, stop=True)
                        after(pe, s_lin_kv, k)
                        pe.matmul(ps_vo[:, 0:2 * D], x_stage[:, p, :], A("wkv_lin"), start=True, stop=True)\
                          .then_inc(s_lin_proj, 1)
                    if active(kk, 1):
                        if kk == 1:
                            pe.wait_ge(s_const, 1)
                        pe.wait_ge(s_lin_phi, k)
                        after(pe, s_lin_masked, k - 1)
                        for b in range(BT):
                            rows = slice(b * S, (b + 1) * S)
                            mm = pe.matmul(ps_scores[:, b * 512:b * 512 + D + 1], phi[rows, q, D:2 * D],
                                           z[rows, q, 2 * D:3 * D + 1], start=True, stop=True)
                        mm.then_inc(s_lin_state, 1)
                    if active(kk, 3):
                        pe.wait_ge(s_x, k - 2)
                        after(pe, s_xT, k - 3)
                        pe.transpose(ps_tr[:, 0:P], x_new[:, q, :], ident).then_inc(s_xT_mm, 1)
                    if active(kk, 2):
                        pe.wait_ge(s_lin_masked, k - 1)
                        after(pe, s_lin_norm, k - 2)
                        for b in range(BT):
                            mm = pe.matmul(ps_y[b * S:(b + 1) * S, 0:D + H], phi[:, p, b * S:(b + 1) * S],
                                           kv_masked[:, p, b, :], start=True, stop=True)
                        mm.then_inc(s_lin_out, 1)
                sweep(pe, step)

            def softmax_attention(lay):
                pe.wait_ge(s_xT, lay.n * T)
                if lay.a == 0:
                    pe.wait_ge(s_ctx_in, 16)
                    pe.wait_ge(s_prep, 1)

                def project(weight, columns, k, source):
                    return pe.matmul(ps_qk[:, columns], lay.w(weight), tile(source, k), start=True, stop=True)

                def step(k, kk):
                    p, q = kk % 2, (kk + 1) % 2
                    u = k + lay.a * T
                    w = k + lay.n * T
                    if active(kk, 0):
                        after(pe, s_qk, u)
                        project("wq", slice(0, P), k, xT)
                        mm = project("wk", slice(P, 2 * P), k, lay.kvT)
                        if lay.rope:
                            project("wq_turned", slice(2 * P, 3 * P), k, xT)
                            mm = project("wk_turned", slice(3 * P, 4 * P), k, xT)
                        mm.then_inc(s_qk_mm, 1)
                    if active(kk, 3):
                        pe.wait_ge(s_attnT, u - 2)
                        pe.wait_ge(s_res, u + (T - 3))
                        pe.matmul(ps_y[:, 0:D], attnT[:, q, :], lay.w("wo"), start=True, stop=True)\
                          .then_inc(s_proj, 1)
                    if active(kk, 2):
                        pe.wait_ge(s_exp, u - 1)
                        for half in range(2):
                            after(pe, s_probsT, (u - 3) * 2 + half + 1)
                            for pair in range(half * H // 4, (half + 1) * H // 4):
                                mm = pe.transpose(ps_probsT[:, pair * P:(pair + 1) * P],
                                                  probs[:, p, 2 * pair:2 * pair + 2, :], ident)
                            mm.then_inc(s_probsT_mm, 1)
                    if active(kk, 1):
                        pe.wait_ge(s_kv_stage, u)
                        after(pe, s_attnT, u - 2)
                        for b in range(BT):
                            mm = pe.matmul(ps_vo[:, b * D:(b + 1) * D], kv_stage[:, q, b, :, :], lay.w("wv"),
                                           start=True, stop=True)
                        mm.then_inc(s_v_mm, 1)
                        pe.wait_ge(s_k_heads, u)
                        after(pe, s_shifted, u - 1)
                        for half in range(2):
                            cols = slice(half * 512, (half + 1) * 512)
                            whole = ps_scores[:, cols].rearrange("p (h k) -> p h k", k=S)
                            some = slice(half * H // 2, (half + 1) * H // 2)
                            if lay.causal:
                                pe.matmul(whole, id16[:], causal[:].unsqueeze(1).broadcast_to([P, H // 2, S]),
                                          start=True, stop=False, skip_group_check=True)
                            else:
                                pe.matmul(whole, select[:], key_neg[:, k - 1, :].unsqueeze(1)
                                          .broadcast_to([BT, H // 2, S]),
                                          start=True, stop=False, skip_group_check=True)
                                pe.matmul(ps_scores[:, cols], ident, rel_bias[:, some, :],
                                          start=False, stop=False, skip_group_check=True)
                            for b in range(BT):
                                mm = pe.matmul(ps_scores[b * S:(b + 1) * S, cols], qk[:, q, b * S:(b + 1) * S],
                                               k_heads[:, q, b, some, :],
                                               start=False, stop=True, skip_group_check=True)
                        mm.then_inc(s_scores, 1)
                    if active(kk, 3):
                        pe.wait_ge(s_x, w - 2)
                        after(pe, s_invT, u - 2)
                        pe.transpose(ps_tr[:, 0:P], x_new[:, q, :], ident).then_inc(s_xT_mm, 1)
                    if active(kk, 2):
                        pe.wait_ge(s_inv_nat, u - 1)
                        after(pe, s_invT, u - 2)
                        pe.transpose(ps_tr[:, P:2 * P], inv_nat[:, :, :], ident).then_inc(s_invT_mm, 1)
                        pe.wait_ge(s_v_heads, u if active(kk, 1) else u - 1)
                        pe.wait_ge(s_probsT, (u - 1) * 2)
                        for b in range(BT):
                            for odd in range(2):
                                for strip in range(4):
                                    rows = slice(32 * strip, 32 * strip + 32)
                                    mm = pe.matmul(ps_vo[rows, 2 * D + b * S:2 * D + (b + 1) * S],
                                                   v_heads[:, p, b, odd, rows],
                                                   probsT[:, p, 2 * strip + odd, b * S:(b + 1) * S],
                                                   start=(odd == 0), stop=(odd == 1), skip_group_check=True)
                        mm.then_inc(s_attn_mm, 1)
                sweep(pe, step)

            def gate(ffn, weight, experts):
                for c in range(NCH):
                    if c >= 2:
                        pe.wait_ge(s_gate_row, ffn.f * NCH + c - 1)
                    pe.matmul(ps_probsT[0:experts, (c % 2) * N:(c % 2 + 1) * N], W(weight),
                              xT[:, c * N:(c + 1) * N], start=True, stop=True).then_inc(s_gate_mm, 1)
                pe.wait_ge(s_gate_row, (ffn.f + 1) * NCH)
                for t in range(T):
                    mm = pe.transpose(ps_y[:, t * experts:(t + 1) * experts], logitsT[0:experts, t * P:(t + 1) * P],
                                      ident[0:experts, 0:experts])
                mm.then_inc(s_gate_tr, 1)

            def feed_forward(ffn):
                h_bank = [ps_probsT[:, 0:512], ps_probsT[:, 512:1024], ps_qk[:]]
                y_bank = [ps_tr[:], ps_tr[:]]
                t_bank = [ps_vo[:], ps_scores[:, 0:512]]
                pe.wait_ge(s_xT, ffn.n * T)
                pe.wait_ge(s_w_split, T)

                def step(c):
                    pe.wait_ge(s_x_lo, c + (ffn.f * NCH + 1))
                    blocks = ffn.blocks
                    for j in range(len(blocks) + 2):
                        if j < len(blocks):
                            g, e, i = blocks[j]
                            after(pe, s_h, ffn.block_before(c, j, 3))
                            for n, (w, v) in enumerate(((w_hi, x_hi), (w_hi, x_lo), (w_lo, x_hi))):
                                mm = pe.matmul(h_bank[j % 3], w[:, w1_block(e, i)], v[:, bass.ds(c * N, N)],
                                               start=(n == 0), stop=(n == 2))
                            mm.then_inc(s_mm1, 1)
                        if 1 <= j <= len(blocks):
                            g, e, i = blocks[j - 1]
                            first = ffn.first[g] == j - 1
                            pe.wait_ge(s_h_lo, ffn.block(c, j - 1))
                            if first:
                                after(pe, s_yT, ffn.group(c, g - 1))
                                if g == 0 and ffn.f == 0:
                                    after(pe, s_xT, CH * c + ffn.n * T)
                            q = (j - 1) % 2
                            for n, (w, v) in enumerate(((w_hi, h_hi), (w_hi, h_lo), (w_lo, h_hi))):
                                mm = pe.matmul(y_bank[g % 2], w[:, w2_block(e, i)], v[:, q, :],
                                               start=(first and n == 0), stop=(ffn.last[g] == j - 1 and n == 2))
                            mm.then_inc(s_mm2, 1)
                        if j >= 2 and ffn.ended(j - 2) is not None:
                            g = ffn.ended(j - 2)
                            pe.wait_ge(s_yT, ffn.group(c, g))
                            after(pe, s_mix, ffn.group_before(c, g))
                            for t in range(CH):
                                mm = pe.transpose(t_bank[g % 2][:, t * P:(t + 1) * P],
                                                  yT[:, g % 2, t * P:(t + 1) * P], ident)
                            mm.then_inc(s_y_mm, 1)
                    if ffn.f == 0:
                        pe.wait_ge(s_x, CH * c + (ffn.n * T + CH))
                        for t in range(CH):
                            mm = pe.transpose(ps_tr[:, t * P:(t + 1) * P], x_new[:, t, :], ident)
                        mm.then_inc(s_xT_mm, CH)
                ffn.chunks(pe, step)

            prepare()
            linear_attention()
            softmax_attention(layer_B)
            pe.wait_ge(s_xT, 2 * T)
            gate(ffn_C, "C_gate", NE)
            feed_forward(ffn_C)
            softmax_attention(layer_D)
            softmax_attention(layer_E)
            pe.wait_ge(s_xT, 5 * T)
            gate(ffn_F, "F_gate", NR1)
            feed_forward(ffn_F)

        @block.scalar
        def _(act):
            act.wait_ge(s_pa, 16)

            def linear_attention():
                def step(k, kk):
                    p, q = kk % 2, (kk + 1) % 2
                    if active(kk, 0):
                        pe_done = k + 1
                        act.wait_ge(s_lin_proj, pe_done)
                        act.activation(z[:, p, 0:D], ps_qk[:, 0:P], ACT.Identity, bias=A("bq_lin"))\
                           .then_inc(s_lin_q, 1)
                    if active(kk, 3):
                        act.wait_ge(s_xT_mm, k - 2)
                        act.copy(tile(xT, k - 3), ps_tr[:, 0:P]).then_inc(s_xT, 1)
                    if active(kk, 0):
                        act.wait_ge(s_lin_q, k + 1)
                        act.wait_ge(s_lin_kv, k + 1)
                        after(act, s_lin_phi, k - 1)
                        act.activation(r_z[:, p, :], z[:, p, 0:2 * D], ACT.Relu)
                        act.activation(e_z[:, p, :], z[:, p, 0:2 * D], ACT.Exp).then_inc(s_lin_exp, 1)
                sweep(act, step)

            def softmax_attention(lay):
                if lay.a == 0:
                    act.wait_ge(s_pb, 16)

                def step(k, kk):
                    p, q = kk % 2, (kk + 1) % 2
                    u, w = k + lay.a * T, k + lay.n * T
                    if active(kk, 0):
                        act.wait_ge(s_qk_mm, u + 1)
                        if lay.rope:
                            after(act, s_rope_mul, k - 1)
                            for i, b in enumerate(("bq", "bk", "bq_turned", "bk_turned")):
                                last = act.activation(qk_raw[:, p, i * P:(i + 1) * P], ps_qk[:, i * P:(i + 1) * P],
                                                      ACT.Identity, bias=lay.w(b))
                        else:
                            after(act, s_scores, u - 1)
                            after(act, s_k_heads, u - 1)
                            if lay.bias:
                                act.activation(qk[:, p, 0:P], ps_qk[:, 0:P], ACT.Identity, bias=lay.w("bq"))
                                last = act.activation(qk[:, p, P:2 * P], ps_qk[:, P:2 * P], ACT.Identity,
                                                      bias=lay.w("bk"))
                            else:
                                last = act.copy(qk[:, p, :], ps_qk[:, 0:2 * P])
                        last.then_inc(s_qk, 1)
                    if active(kk, 2):
                        after(act, s_attn_mm, u - 3)
                        for half in range(2):
                            act.wait_ge(s_probsT_mm, (u - 2) * 2 + half + 1)
                            act.copy(probsT[:, p, half * H // 4:(half + 1) * H // 4, :],
                                     ps_probsT[:, half * 512:(half + 1) * 512]).then_inc(s_probsT, 1)
                    if active(kk, 3):
                        act.wait_ge(s_xT_mm, w - 2)
                        if active(kk, 2):
                            act.wait_ge(s_invT_mm, u - 1)
                        act.copy(tile(xT, k - 3), ps_tr[:, 0:P]).then_inc(s_xT, 1)
                    if active(kk, 2):
                        act.wait_ge(s_invT_mm, u - 1)
                        after(act, s_attnT, u - 3)
                        act.copy(invT[:, p, :], ps_tr[:, P:2 * P]).then_inc(s_invT, 1)
                    if active(kk, 1):
                        act.wait_ge(s_shifted, u)
                        after(act, s_probsT_mm, (u - 2) * 2)
                        after(act, s_sum, u - 2)
                        act.activation(probs[:, q, :, :], shifted[:], ACT.Exp, scale=lay.scale).then_inc(s_exp, 1)
                sweep(act, step)

            def gate(ffn, experts):
                for c in range(NCH):
                    act.wait_ge(s_gate_mm, ffn.f * NCH + c + 1)
                    dst, src = logitsT[0:experts, c * N:(c + 1) * N], ps_probsT[0:experts, (c % 2) * N:(c % 2 + 1) * N]
                    if ffn.f == 0:
                        last = act.activation(dst, src, ACT.Identity, bias=W("C_gate_bias", experts))
                    else:
                        last = act.copy(dst, src)
                    last.then_inc(s_gate_row, 1)
                for c in range(NCH):
                    act.copy(x_hi[:, c * N:(c + 1) * N], xT[:, c * N:(c + 1) * N]).then_inc(s_x_hi, 1)
                act.wait_ge(s_gate, GATE_STEPS[0] * ffn.f + 2)
                act.activation(gates["g_exp"][:, :, 0:experts], gates["g_shifted"][:, :, 0:experts], ACT.Exp)\
                   .then_inc(s_gate_exp, 1)

            def feed_forward(ffn):
                h_bank = [ps_probsT[:, 0:512], ps_probsT[:, 512:1024], ps_qk[:]]

                def step(c):
                    for j in range(len(ffn.blocks) + 1):
                        if j < len(ffn.blocks):
                            act.wait_ge(s_mm1, ffn.block(c, j))
                            after(act, s_h_lo, ffn.block_before(c, j, 2))
                            g, e, i = ffn.blocks[j]
                            act.activation(h[:, j % 2, :], h_bank[j % 3], ffn.func, bias=W(ffn.b1)[:, j:j + 1])\
                               .then_inc(s_h, 1)
                        if j >= 1 and ffn.ended(j - 1) is not None:
                            g = ffn.ended(j - 1)
                            act.wait_ge(s_mm2, ffn.block(c, j - 1))
                            after(act, s_y_mm, ffn.group_before(c, g))
                            if ffn.f == 0 and g == 0:
                                last = act.activation(yT[:, 0, :], ps_tr[:], ACT.Identity, bias=b2_shared[:],
                                                      scale=1.0 / NS)
                            else:
                                col = g + 1 if ffn.f == 0 else 0
                                last = act.activation(yT[:, g % 2, :], ps_tr[:], ACT.Identity,
                                                      bias=W(ffn.b2)[:, col:col + 1])
                            last.then_inc(s_yT, 1)
                    if ffn.f == 0:
                        act.wait_ge(s_xT_mm, CH * c + (ffn.n * T + CH))
                        act.copy(xT[:, bass.ds(c * N, N)], ps_tr[:]).then_inc(s_xT, CH)
                ffn.chunks(act, step)

            linear_attention()
            softmax_attention(layer_B)
            gate(ffn_C, NE)
            feed_forward(ffn_C)
            softmax_attention(layer_D)
            softmax_attention(layer_E)
            gate(ffn_F, NR1)
            feed_forward(ffn_F)

        @block.vector
        def _(dve):
            def norm_statistics(i):
                dve.bn_stats(stats[:, i, :], y[:, i, :]).then_inc(s_stats, 1)

            def norm_variance(i, w):
                dve.bn_aggr(mean_var[:, i, :], stats[:, i, :]).then_inc(s_mean, 1)
                dve.wait_ge(s_mean, w + 1)
                dve.tensor_scalar(var_eps[:, i, :], mean_var[:, i, 1:2], EPS, None, ALU.add).then_inc(s_var, 1)

            def norm_apply(i, w, buffers, dst=None):
                dve.wait_ge(s_rstd, w + 1)
                if dst is None:
                    after(dve, s_xT_mm, w - buffers + 1)
                    after(dve, s_keep, w - buffers + 1)
                    dst = x_new[:, i, :]
                dve.tensor_scalar(dst, y[:, i, :], mean_var[:, i, 0:1], rstd[:, i, :], ALU.subtract, ALU.mult)\
                   .then_inc(s_x, 1)

            def prepare():
                dve.memset(z[:, :, 3 * D:3 * D + 1], 1.0).then_inc(s_ones, 1)
                dve.wait_ge(s_pa, 16)
                dve.wait_ge(s_pb, 16)
                dve.wait_ge(s_bo_mm, 1)
                dve.tensor_tensor(bo_B[:], ps_y[:, 0:D], W("B_bo"), ALU.add)
                dve.tensor_tensor(bo_D[:], ps_y[:, D:2 * D], W("D_bo"), ALU.add)
                dve.tensor_tensor(b2_shared[:], W("C_b2")[:, 0:1], W("C_b2")[:, 1:2], ALU.add).then_inc(s_ones, 1)
                dve.wait_ge(s_ones, 2)
                dve.tensor_scalar(b2_shared[:], b2_shared[:], 1.0 / NS, None, ALU.mult)
                dve.tensor_copy(id16[:], ident)
                dve.tensor_copy(causal[:], W("causal"))
                dve.tensor_copy(select[:], W("select", BT))
                dve.wait_ge(s_mask_in, 16)
                dve.tensor_scalar(key_neg[:], mask_in, -NEG, NEG, ALU.mult, ALU.add).then_inc(s_prep, 1)
                dve.wait_ge(s_bias_mm, 1)
                dve.tensor_copy(rel_bias[:].rearrange("p h k -> p k h"),
                                ps_scores[:].rearrange("p (k h) -> p k h", h=H)).then_inc(s_const, 1)

            def linear_attention():
                dve.wait_ge(s_pa, 16)
                dve.wait_ge(s_x_in, 16)

                def step(k, kk):
                    p, q = kk % 2, (kk + 1) % 2
                    if active(kk, 0):
                        dve.wait_ge(s_lin_proj, k + 1)
                        after(dve, s_lin_state, k - 1)
                        dve.tensor_tensor(z[:, p, D:3 * D], ps_vo[:, 0:2 * D], A("bkv_lin"), ALU.add)\
                           .then_inc(s_lin_kv, 1)
                    if active(kk, 1):
                        dve.wait_ge(s_lin_state, k)
                        after(dve, s_lin_out, k - 2)
                        both = ps_scores[:].rearrange("p (b c) -> p b c", b=BT)
                        dve.tensor_tensor(kv_masked[:, q, :, 0:D], both[:, :, 0:D],
                                          A("block_mask").unsqueeze(1).broadcast_to([P, BT, D]), ALU.mult)
                        dve.tensor_tensor(kv_masked[:, q, :, D:D + H],
                                          both[:, :, D:D + 1].broadcast_to([P, BT, H]),
                                          A("head_mask").unsqueeze(1).broadcast_to([P, BT, H]), ALU.mult)\
                           .then_inc(s_lin_masked, 1)
                    if active(kk, 2):
                        dve.wait_ge(s_lin_out, k - 1)
                        dve.tensor_scalar(den[:], ps_y[:, D:D + H], 1e-6, None, ALU.add).then_inc(s_lin_den, 1)
                        dve.wait_ge(s_lin_den, k - 1)
                        dve.reciprocal(den_inv[:], den[:]).then_inc(s_lin_inv, 1)
                        dve.wait_ge(s_lin_inv, k - 1)
                        dve.tensor_tensor(o_lin[:].rearrange("p (h m) -> p h m", h=H),
                                          ps_y[:, 0:D].rearrange("p (h m) -> p h m", h=H),
                                          den_inv[:].unsqueeze(2).broadcast_to([P, H, HD]), ALU.mult)\
                           .then_inc(s_lin_norm, 1)
                        dve.wait_ge(s_lin_norm, k - 1)
                        dve.tensor_tensor(y[:, p, :], o_lin[:], x_nat[:, k - 2, :], ALU.add).then_inc(s_res, 1)
                        dve.wait_ge(s_res, k - 1)
                        norm_statistics(p)
                        dve.wait_ge(s_stats, k - 1)
                    if active(kk, 0):
                        dve.wait_ge(s_lin_exp, k + 1)
                        after(dve, s_lin_out, k - 1)
                        dve.scalar_tensor_tensor(phi[:, p, :], e_z[:, p, :], 1.0, r_z[:, p, :], ALU.min, ALU.add)\
                           .then_inc(s_lin_phi, 1)
                    if active(kk, 2):
                        norm_variance(p, k - 2)
                        norm_apply(p, k - 2, 2)
                sweep(dve, step)

            def softmax_attention(lay):
                def step(k, kk):
                    p, q = kk % 2, (kk + 1) % 2
                    u, w = k + lay.a * T, k + lay.n * T
                    if active(kk, 2):
                        dve.wait_ge(s_exp, u - 1)
                        dve.tensor_reduce(row_sum[:], probs[:, p, :, :], AX.X, ALU.add).then_inc(s_sum, 1)
                    if lay.rope and active(kk, 0):
                        dve.wait_ge(s_qk, u + 1)
                        by = lambda name: W(name).unsqueeze(1).broadcast_to([P, 2 * BT, S])
                        parts = qk_raw[:, p, :].rearrange("p (i s) -> p i s", s=S)
                        dve.tensor_tensor(straight[:, p, :].rearrange("p (i s) -> p i s", s=S),
                                          parts[:, 0:2 * BT, :], by("cos"), ALU.mult)
                        dve.tensor_tensor(turned[:, p, :].rearrange("p (i s) -> p i s", s=S),
                                          parts[:, 2 * BT:4 * BT, :], by("sin"), ALU.mult).then_inc(s_rope_mul, 1)
                    if active(kk, 2):
                        dve.wait_ge(s_sum, u - 1)
                        dve.reciprocal(row_inv[:], row_sum[:]).then_inc(s_inv, 1)
                    if lay.rope and active(kk, 0):
                        dve.wait_ge(s_rope_mul, k + 1)
                        after(dve, s_scores, u - 1)
                        after(dve, s_k_heads, u - 1)
                        dve.tensor_tensor(qk[:, p, :], straight[:, p, :], turned[:, p, :], ALU.add)\
                           .then_inc(s_rope, 1)
                    if active(kk, 2):
                        dve.wait_ge(s_inv, u - 1)
                        after(dve, s_invT_mm, u - 2)
                        dve.tensor_copy(inv_nat[:], row_inv[:].unsqueeze(2).broadcast_to([P, H, HD]))\
                           .then_inc(s_inv_nat, 1)
                    if active(kk, 3):
                        dve.wait_ge(s_proj, u - 2)
                        dve.wait_ge(s_keep, w - T - 2)
                        dve.tensor_tensor(y[:, q, :], ps_y[:, 0:D], x_nat[:, k - 3, :], ALU.add).then_inc(s_res, 1)
                        dve.wait_ge(s_res, u + (T - 2))
                        norm_statistics(q)
                    if active(kk, 1):
                        dve.wait_ge(s_v_mm, u)
                        after(dve, s_attn_mm, u - 2)
                    if active(kk, 3):
                        dve.wait_ge(s_stats, w - 2)
                    if active(kk, 1):
                        dve.tensor_tensor(
                            v_heads[:, q, :, :, :],
                            ps_vo[:, 0:2 * D].rearrange("p (b d) -> p b d", b=BT).unsqueeze(2)
                            .broadcast_to([P, BT, 2, D]),
                            W("value_mask").rearrange("p (o d) -> p o d", o=2).unsqueeze(1)
                            .broadcast_to([P, BT, 2, D]), ALU.mult).then_inc(s_v_heads, 1)
                    if active(kk, 3):
                        norm_variance(q, w - 3)
                        norm_apply(q, w - 3, 2)
                    if active(kk, 1):
                        scores = ps_scores[:].rearrange("p (h k) -> p h k", h=H)
                        dve.wait_ge(s_scores, u)
                        dve.tensor_reduce(row_max[:], scores, AX.X, ALU.max).then_inc(s_max, 1)
                        dve.wait_ge(s_max, u)
                        after(dve, s_exp, u - 1)
                        dve.tensor_tensor(shifted[:], scores, row_max[:].unsqueeze(2).broadcast_to([P, H, S]),
                                          ALU.subtract).then_inc(s_shifted, 1)
                    if active(kk, 2):
                        dve.wait_ge(s_attn_mm, u - 1)
                        dve.wait_ge(s_invT, u - 1)
                        after(dve, s_proj, u - 3)
                        dve.tensor_tensor(attnT[:, p, :], ps_vo[:, 2 * D:3 * D], invT[:, p, :], ALU.mult)\
                           .then_inc(s_attnT, 1)
                sweep(dve, step)

            def gate(ffn, experts):
                count = [GATE_STEPS[0] * ffn.f]

                def link(instruction):
                    count[0] += 1
                    instruction.then_inc(s_gate, 1)
                    dve.wait_ge(s_gate, count[0])

                g = {n: t[:, :, 0:experts] for n, t in gates.items()}
                over = lambda t: t[:].unsqueeze(2).broadcast_to([P, T, experts])
                for c in range(NCH):
                    dve.wait_ge(s_x_hi, ffn.f * NCH + c + 1)
                    cols = slice(c * N, (c + 1) * N)
                    dve.tensor_tensor(x_lo[:, cols], xT[:, cols], x_hi[:, cols].bitcast(F32), ALU.subtract)\
                       .then_inc(s_x_lo, 1)
                dve.wait_ge(s_gate_tr, ffn.f + 1)
                logits = ps_y[:, 0:T * experts].rearrange("p (t e) -> p t e", e=experts)
                link(dve.tensor_reduce(g_max[:], logits, AX.X, ALU.max))
                link(dve.tensor_tensor(g["g_shifted"], logits, over(g_max), ALU.subtract))
                dve.wait_ge(s_gate_exp, ffn.f + 1)
                link(dve.tensor_reduce(g_sum[:], g["g_exp"], AX.X, ALU.add))
                link(dve.reciprocal(g_inv[:], g_sum[:]))
                link(dve.tensor_tensor(g["g_probs"], g["g_exp"], over(g_inv), ALU.mult))
                if ffn.f == 0:
                    probs_e = g["g_probs"].unsqueeze(3).broadcast_to([P, T, NE, NE])
                    probs_j = g["g_probs"].unsqueeze(2).broadcast_to([P, T, NE, NE])
                    lower = W("lower").rearrange("p (e j) -> p e j", e=NE).unsqueeze(1).broadcast_to([P, T, NE, NE])
                    link(dve.tensor_tensor(g_above, probs_j, probs_e, ALU.is_gt))
                    link(dve.tensor_tensor(g_equal, probs_j, probs_e, ALU.is_equal))
                    link(dve.tensor_tensor(g_tied, g_equal, lower, ALU.mult))
                    link(dve.tensor_tensor(g_before, g_above, g_tied, ALU.add))
                    link(dve.tensor_reduce(g["g_rank"], g_before, AX.X, ALU.add))
                    link(dve.scalar_tensor_tensor(g["g_weights"], g["g_rank"], 2.0, g["g_probs"], ALU.is_lt,
                                                  ALU.mult))
                assert count[0] == GATE_STEPS[0] * ffn.f + GATE_STEPS[ffn.f]

            def feed_forward(ffn):
                t_bank = [ps_vo[:], ps_scores[:, 0:512]]
                weights = gates["g_weights"] if ffn.f == 0 else gates["g_probs"]

                def step(c):
                    for j in range(len(ffn.blocks) + 2):
                        if j < len(ffn.blocks):
                            dve.wait_ge(s_h, ffn.block(c, j))
                            after(dve, s_mm2, ffn.block_before(c, j, 2))
                            dve.tensor_copy(h_hi[:, j % 2, :], h[:, j % 2, :]).then_inc(s_h_hi, 1)
                            dve.wait_ge(s_h_hi, ffn.block(c, j))
                            dve.tensor_tensor(h_lo[:, j % 2, :], h[:, j % 2, :], h_hi[:, j % 2, :].bitcast(F32),
                                              ALU.subtract).then_inc(s_h_lo, 1)
                        if j >= 2 and ffn.ended(j - 2) is not None:
                            g = ffn.ended(j - 2)
                            dve.wait_ge(s_y_mm, ffn.group(c, g))
                            after(dve, s_mix, ffn.group(c, g - 1))
                            bank = t_bank[g % 2]
                            if g == 0:
                                dve.wait_ge(s_keep, CH * c + ((ffn.n - 1) * T + CH))
                            if ffn.f == 0 and g == 0:
                                dve.tensor_tensor(y[:].rearrange("p t d -> p (t d)"), bank,
                                                  x_nat[:, bass.ds(c * CH, CH), :].rearrange("p t d -> p (t d)"),
                                                  ALU.add).then_inc(s_mix, 1)
                                continue
                            e = g - 1 if ffn.f == 0 else NR1 - 1
                            for t in range(CH):
                                before = y[:, t, :] if ffn.f == 0 else x_nat[:, c * CH + t, :]
                                last = dve.scalar_tensor_tensor(
                                    y[:, t, :], bank[:, t * P:(t + 1) * P],
                                    weights[:, c * CH + t, e:e + 1], before, ALU.mult, ALU.add)
                            last.then_inc(s_mix, 1)
                    dve.wait_ge(s_mix, ffn.group(c, ffn.groups - 1))
                    w = CH * c + ffn.n * T
                    dst = lambda t: x_nat[:, c * CH + t, :] if ffn.f else None
                    norm_statistics(0)
                    for t in range(CH):
                        dve.wait_ge(s_stats, w + (t + 1))
                        if t + 1 < CH:
                            norm_statistics(t + 1)
                        else:
                            norm_apply(t - 1, w + (t - 1), CH, dst(t - 1))
                        norm_variance(t, w + t)
                        if 1 <= t < CH - 1:
                            norm_apply(t - 1, w + (t - 1), CH, dst(t - 1))
                    norm_apply(CH - 1, w + (CH - 1), CH, dst(CH - 1))
                ffn.chunks(dve, step)

            prepare()
            linear_attention()
            softmax_attention(layer_B)
            gate(ffn_C, NE)
            feed_forward(ffn_C)
            softmax_attention(layer_D)
            softmax_attention(layer_E)
            gate(ffn_F, NR1)
            feed_forward(ffn_F)

        @block.gpsimd
        def _(pool):
            def inverse_deviation(i, w):
                pool.wait_ge(s_var, w + 1)
                pool.tensor_tensor(rstd[:, i, :], var_eps[:, i, :], minus_half[:], ALU.pow).then_inc(s_rstd, 1)

            def keep(i, w, dst, bias):
                pool.wait_ge(s_x, w + 1)
                if bias is None:
                    last = pool.tensor_copy(dst, x_new[:, i, :])
                else:
                    last = pool.tensor_tensor(dst, x_new[:, i, :], bias[:], ALU.add)
                last.then_inc(s_keep, 1)

            def linear_attention():
                pool.wait_ge(s_xT_in, 16)

                def step(k, kk):
                    p, q = kk % 2, (kk + 1) % 2
                    if active(kk, 0):
                        after(pool, s_lin_proj, k - 1)
                        pool.tensor_copy(x_stage[:, p, :], tile(xT, k)).then_inc(s_x_stage, 1)
                    if active(kk, 2):
                        inverse_deviation(p, k - 2)
                    if active(kk, 0):
                        cols = bass.ds(k * W_CHUNK, W_CHUNK)
                        pool.wait_ge(s_w_in[p], 8 * (k - kk % 2) + 16)
                        pool.tensor_copy(w_hi[:, cols], w_raw[:, p, :]).then_inc(s_w_hi, 1)
                        pool.wait_ge(s_w_hi, k + 1)
                        pool.tensor_tensor(w_lo[:, cols], w_raw[:, p, :], w_hi[:, cols].bitcast(F32), ALU.subtract)\
                            .then_inc(s_w_split, 1)
                    if active(kk, 2):
                        keep(p, k - 2, x_nat[:, k - 2, :], bo_B)
                sweep(pool, step)

            def softmax_attention(lay):
                def step(k, kk):
                    p, q = kk % 2, (kk + 1) % 2
                    u, w = k + lay.a * T, k + lay.n * T

                    def k_to_heads(b):
                        return pool.tensor_tensor(
                            k_heads[:, p, b, :, :],
                            qk[:, p, P + b * S:P + (b + 1) * S].unsqueeze(1).broadcast_to([P, H, S]),
                            A("head_mask").unsqueeze(2).broadcast_to([P, H, S]), ALU.mult)

                    if active(kk, 0):
                        if lay.kvT is xT:
                            pool.wait_ge(s_xT, w - T + 1)
                        after(pool, s_v_mm, u - 1)
                        pool.tensor_copy(kv_stage[:, p, :, :, :],
                                         tile(lay.kvT, k).rearrange("p (b s) -> p b s", b=BT).unsqueeze(2)
                                         .broadcast_to([P, BT, 2, S])).then_inc(s_kv_stage, 1)
                        pool.wait_ge(s_rope if lay.rope else s_qk, k + 1 if lay.rope else u + 1)
                        after(pool, s_scores, u - 1)
                        k_to_heads(0)
                    if active(kk, 3):
                        inverse_deviation(q, w - 3)
                    if active(kk, 0):
                        k_to_heads(1).then_inc(s_k_heads, 1)
                    if active(kk, 3):
                        keep(q, w - 3, x_nat[:, k - 3, :], None)
                sweep(pool, step)

            def feed_forward(ffn):
                def step(c):
                    w = CH * c + ffn.n * T
                    for t in range(CH):
                        inverse_deviation(t, w + t)
                    if ffn.f == 0:
                        for t in range(CH):
                            keep(t, w + t, x_nat[:, c * CH + t, :], bo_D)
                ffn.chunks(pool, step)

            pool.memset(minus_half[:], -0.5).then_inc(s_half, 1)
            pool.wait_ge(s_half, 1)
            linear_attention()
            pool.wait_ge(s_ctx_in, 16)
            pool.wait_ge(s_prep, 1)
            softmax_attention(layer_B)
            feed_forward(ffn_C)
            softmax_attention(layer_D)
            softmax_attention(layer_E)
            feed_forward(ffn_F)


def constants():
    f32 = np.float32
    feature, head = np.arange(D), np.arange(D) // HD
    row = np.arange(P)
    out = {"ident": np.eye(P, dtype=f32),
           "head_mask": (head[:, None] == np.arange(H)[None, :]).astype(f32),
           "block_mask": (head[:, None] == head[None, :]).astype(f32)}
    keep = (head[None, None, :] % 2 == (row // S)[:, None, None]) &            ((head // 2)[None, None, :] % 2 == np.arange(2)[None, :, None])
    out["value_mask"] = keep.astype(f32).reshape(P, 2 * D)
    half = HD // 2
    theta = np.power(f32(1250.0), (f32(-2.0) * np.arange(half, dtype=f32) / f32(HD)).astype(f32)).astype(f32)
    angle = (np.arange(1, S + 1, dtype=f32)[None, :] * np.tile(theta, 2)[feature % HD][:, None]).astype(f32)
    out["cos"] = np.cos(angle).astype(f32)
    out["sin"] = (np.sin(angle) * np.where(feature % HD < half, -1.0, 1.0)[:, None]).astype(f32)
    e = np.arange(NE)
    out["lower"] = np.broadcast_to((e[None, :] < e[:, None]).astype(f32).reshape(1, -1), (P, NE * NE))
    distance = (S - 1 - np.arange(P))
    nb, exact = BUCKETS // 2, BUCKETS // 4
    size = np.abs(distance)
    large = exact + (np.log(np.maximum(size, 1).astype(f32) / exact) / np.log(128 / exact) * (nb - exact))        .astype(f32).astype(np.int32)
    bucket = (distance > 0) * nb + np.where(size < exact, size, np.minimum(large, nb - 1))
    hot = np.zeros((P, P), f32)
    hot[bucket, np.arange(P)] = 1.0
    out["buckets"] = hot
    out["causal"] = np.where(np.arange(S)[None, :] > (row % S)[:, None], NEG, 0.0).astype(f32)
    out["select"] = (row[None, :] // S == np.arange(BT)[:, None]).astype(f32)
    return out


def arrays(inputs):
    i = {n: np.asarray(a) for n, a in inputs.items()}

    def column(a):
        return np.asarray(a, np.float32).reshape(-1, P).T

    def rows(a):
        return np.broadcast_to(a.reshape(1, -1), (P, a.size))

    turned = np.arange(D) ^ (HD // 2)
    part = constants()
    part["wq_lin"] = i["L0_attn_W_qkv"][:, 0:D]
    part["wkv_lin"] = i["L0_attn_W_qkv"][:, D:3 * D]
    part["bq_lin"] = column(i["L0_attn_b_qkv"][0:D])
    part["bkv_lin"] = rows(i["L0_attn_b_qkv"][D:3 * D])
    for n in "qkvo":
        part[f"B_w{n}"] = i[f"L0_xattn_W{n}"]
        part[f"D_w{n}"] = i[f"L1_attn_W{n}"].T
        part[f"E_w{n}"] = i[f"L1_xattn_W{n}"].T
        if n != "o":
            part[f"B_b{n}"] = column(i[f"L0_xattn_b{n}"])
            part[f"D_b{n}"] = column(i[f"L1_attn_b{n}"])
    for n in "qk":
        part[f"D_w{n}_turned"] = part[f"D_w{n}"][:, turned]
        part[f"D_b{n}_turned"] = part[f"D_b{n}"][turned]
    part["B_bo"] = rows(i["L0_xattn_bo"])
    part["D_bo"] = rows(i["L1_attn_bo"])
    part["C_b1"] = np.concatenate([column(i["L0_ffn_sb1"]), column(i["L0_ffn_rb1"])], 1)
    part["C_b2"] = np.concatenate([column(i["L0_ffn_sb2"]), column(i["L0_ffn_rb2"])], 1)
    part["F_b1"] = column(i["L1_ffn_b1"][NR1 - 1])
    part["F_b2"] = column(i["L1_ffn_b2"][NR1 - 1])
    part["C_gate"] = i["L0_ffn_gate_w"]
    part["C_gate_bias"] = i["L0_ffn_gate_b"].reshape(NE, 1)
    part["F_gate"] = i["L1_ffn_Wr"].T
    part["rel_bias"] = i["L1_xattn_rel_bias"].T

    def pack(columns, width):
        out = np.zeros((P, width), np.float32)
        for name, where in columns.items():
            out[0:part[name].shape[0], where] = part[name]
        return out

    experts = [(i["L0_ffn_sw1"][e], i["L0_ffn_sw2"][e]) for e in range(NS)]
    experts += [(i["L0_ffn_rw1"][e], i["L0_ffn_rw2"][e]) for e in range(NE)]
    experts += [(i["L1_ffn_W1"][NR1 - 1], i["L1_ffn_W2"][NR1 - 1])]
    w_experts = np.concatenate(
        [a for w1, w2 in experts for a in (w1, w2.reshape(FB, P, D).transpose(1, 0, 2).reshape(P, F))], 1)
    return {"x": i["x"].reshape(B * S, D), "xT": i["x"].reshape(B * S, D).T, "ctxT": i["ctx_1024"].reshape(B * S, D).T,
            "pack_a": pack(PACK_A, WIDTH_A), "pack_b": pack(PACK_B, WIDTH_B), "w_experts": w_experts,
            "key_mask": i["mask_Bx1x1xS2_bk0"].reshape(T, BT, S).transpose(1, 0, 2).astype(np.int32)}


def kernel(**inputs):
    import concourse.bacc as bacc
    from concourse.bass_utils import run_bass_kernel_spmd

    nc = bacc.Bacc("TRN2", target_bir_lowering=False, num_devices=1)
    given, args = {}, []
    for name, a in arrays(inputs).items():
        a = np.ascontiguousarray(a)
        given[f"in_{name}"] = a
        args.append(nc.dram_tensor(f"in_{name}", a.shape, mybir.dt.from_np(a.dtype), kind="ExternalInput").ap())
    result = nc.dram_tensor("result", (B * S, D), F32, kind="ExternalOutput").ap()
    build(nc, *args, result)
    r = run_bass_kernel_spmd(nc, [given], core_ids=[0])
    return r.results[0]["result"].reshape(B, S, D)
```

```python
from contextlib import ExitStack

import concourse.bass as bass
import numpy as np
from concourse import mybir

ALU = mybir.AluOpType
ACT = mybir.ActivationFunctionType
AX = mybir.AxisListType
F32 = mybir.dt.float32
F32R = mybir.dt.float32r
BF16 = mybir.dt.bfloat16

B, S, D, H = 32, 64, 128, 16
HD = D // H
P = 128
BT = P // S
T = B * S // P
CH = 4
NCH = T // CH
N = CH * P
F = 512
FB = F // P
NS, NE = 2, 4
NR1 = 8
BUCKETS = 32
EPS = 1e-5
NEG = -1e30
PAIRS = T // 2
H_BUFS = 4
LAG = 3

def _columns(widths):
    at, out = 0, {}
    for name, width in widths:
        out[name] = slice(at, at + width)
        at += width
    return out, at


PACK_A, WIDTH_A = _columns([
    ("wq_lin", D), ("wkv_lin", 2 * D), ("bkv_lin", 2 * D), ("bq_lin", 1),
    ("ident", P), ("head_mask", H), ("block_mask", D), ("B_wo", D), ("B_bo", D), ("B_bv", 1)])
PACK_B, WIDTH_B = _columns([
    ("B_wq", D), ("B_wk", D), ("B_wv", D),
    ("D_wq", D), ("D_wk", D), ("D_wq_turned", D), ("D_wk_turned", D), ("D_wv", D), ("D_wo", D), ("D_bo", D),
    ("E_wq", D), ("E_wk", D), ("E_wv", D), ("E_wo", D),
    ("B_bq", 1), ("B_bk", 1),
    ("D_bq", 1), ("D_bk", 1), ("D_bq_turned", 1), ("D_bk_turned", 1), ("D_bv", 1),
    ("C_b1", (NS + NE) * FB), ("F_b1", FB), ("C_b2", NS + NE), ("F_b2", 1),
    ("C_gate", NE), ("F_gate", NR1), ("C_gate_bias", 1),
    ("value_mask", 2 * D), ("cos", S), ("sin", S), ("lower", NE * NE),
    ("rel_bias", H), ("buckets", P), ("causal", S), ("select", P)])
EXPERT_COLS = 2 * F
W_COLS = (NS + NE + 1) * EXPERT_COLS
W_CHUNK = W_COLS // PAIRS


def w1_block(expert, f):
    at = expert * EXPERT_COLS + f * P
    return slice(at, at + P)


def w2_block(expert, f):
    at = expert * EXPERT_COLS + F + f * P
    return slice(at, at + P)


def after(engine, semaphore, count):
    if not isinstance(count, int) or count > 0:
        engine.wait_ge(semaphore, count)


def sweep(engine, layers, tiles, depth, stages):
    def step(n, k, kk):
        for behind, stage in stages:
            if 0 <= kk - behind < tiles:
                stage(layers[n], k - behind, (kk - behind) % 2)
            elif kk - behind < 0 and n > 0:
                stage(layers[n - 1], tiles + kk - behind, (kk - behind) % 2)

    peeled = depth + 2 - depth % 2
    for n in range(len(layers)):
        for k in range(peeled):
            step(n, k, k)
        with engine.Fori(0, (tiles - peeled) // 2) as i:
            step(n, 2 * i + peeled, peeled)
            step(n, 2 * i + (peeled + 1), peeled + 1)
    for k in range(tiles, tiles + depth):
        step(len(layers) - 1, k, k)


class Layer:

    def __init__(self, name, a, n, own, causal, rope, scale):
        self.name, self.a, self.n, self.own, self.causal, self.rope, self.scale = name, a, n, own, causal, rope, scale
        self.bias = name in "BD"

    def u(self, t):
        return t + self.a * T

    def w(self, t):
        return t + self.n * T


class Ffn:

    def __init__(self, f, n, groups, b1, b2, func, first_block, first_group, h_banks):
        self.f, self.n, self.func, self.b1, self.b2, self.h_banks = f, n, func, b1, b2, h_banks
        self.blocks = [(g, e, i) for g, es in enumerate(groups) for e in es for i in range(FB)]
        self.nb, self.ng = len(self.blocks), len(groups)
        self.last = {max(j for j, b in enumerate(self.blocks) if b[0] == g): g for g in range(self.ng)}
        self.first = {min(j for j, b in enumerate(self.blocks) if b[0] == g): g for g in range(self.ng)}
        self.first_block, self.first_group = first_block, first_group

    def block(self, c, j):
        return c * self.nb + (self.first_block + j + 1)

    def half(self, c, j):
        return c * (self.nb // 2) + ((self.first_block + j) // 2 + 1)

    def group(self, c, g):
        return c * self.ng + (self.first_group + g + 1)

    def group_before(self, c, g):
        if g >= 2:
            return self.group(c, g - 2)
        return self.group(c, max(x for x in range(self.ng) if x % 2 == g % 2) - self.ng)

    def at_gate(self, c, j):
        return isinstance(c, int) and c == 0 and j == min(4, self.nb - 1)

    def w(self, c):
        return CH * c + self.n * T

    def chunks(self, engine, slot):
        furthest = LAG + 5
        peeled = -(-furthest // self.nb)

        def run(c, j, static):
            def at(behind):
                back, jj = 0, j - behind
                while jj < 0:
                    back, jj = back + 1, jj + self.nb
                if static and not 0 <= c - back < NCH:
                    return None
                return c - back, jj
            slot(at)

        for c in range(peeled):
            for j in range(self.nb):
                run(c, j, True)
        with engine.Fori(peeled, NCH) as c:
            for j in range(self.nb):
                run(c, j, False)
        for j in range(furthest + 1):
            run(NCH + j // self.nb, j % self.nb, True)


def build(nc, x, xT_in, ctxT_in, pack_a, pack_b, w_experts, key_mask, out):
    with ExitStack() as ctx:
        def sb(name, shape, dt=F32):
            return ctx.enter_context(nc.sbuf_tensor(name, shape, dt))

        def bank(name, banks=1):
            return ctx.enter_context(nc.psum_tensor(name, [P, 512 * banks], F32))

        def sem(name):
            return ctx.enter_context(nc.semaphore(name))

        x_nat = sb("x_nat", [P, T, D])
        xT = sb("xT", [P, T * P])
        pa = sb("pa", [P, WIDTH_A])
        pb = sb("pb", [P, WIDTH_B])
        w_hi = sb("w_hi", [P, W_COLS], F32R)
        w_lo = sb("w_lo", [P, W_COLS], F32R)
        id16 = sb("id16", [P, P], BF16)
        causal = sb("causal", [P, S], BF16)
        select = sb("select", [BT, P], BF16)
        key_neg = sb("key_neg", [BT, T, S], BF16)
        rel_hi = sb("rel_hi", [P, H, S], F32R)
        rel_lo = sb("rel_lo", [P, H, S], F32R)
        ident_r = sb("ident_r", [P, P], F32R)
        bo_B = sb("bo_B", [P, D])
        bo_D = sb("bo_D", [P, D])
        b2_shared = sb("b2_shared", [P, 1])
        minus_half = sb("minus_half", [P, 2])
        v_ones = sb("v_ones", [P, 2, 2, D + 1])
        den = sb("den", [P, 2, H])
        den_inv = sb("den_inv", [P, 2, H])
        o_lin = sb("o_lin", [P, 2, D])
        kv_stage = sb("kv_stage", [P, 2, BT, 2, S])
        qk = sb("qk", [P, 2, 2 * P])
        qk_raw = sb("qk_raw", [P, 2, 4 * P])
        turned = sb("turned", [P, 2 * P])
        straight = sb("straight", [P, 2 * P])
        k_heads = sb("k_heads", [P, 2, BT, H, S])
        v_heads = sb("v_heads", [P, 2, BT, 2, D])
        row_max = sb("row_max", [P, H])
        shifted = sb("shifted", [P, H, S])
        probs = sb("probs", [P, 2, H, S])
        probsT = sb("probsT", [P, 2, H // 2, P])
        sum_inv = sb("sum_inv", [P, P])
        attnT = sb("attnT", [P, 2, P])
        r_z, e_z = (k_heads[:, 0, b, :, :].rearrange("p (i h) s -> p i (h s)", i=2) for b in range(BT))
        mask_in = k_heads[0:BT, 1, 0, :, :].bitcast(mybir.dt.int32)
        z = qk_raw
        phi = shifted[:].rearrange("p (i h) s -> p i (h s)", i=2)
        room = probsT[:].rearrange("p i a b -> p (i a b)")
        x_stage = room[:, 0:4 * P].rearrange("p (i c) -> p i c", i=2)
        kv_masked = room[:, 4 * P:4 * P + 4 * BT * (D + H)]\
            .rearrange("p (i j b c) -> p i j b c", i=2, j=2, b=BT)
        w_raw = probs[:].rearrange("p i h s -> p (i h s)")[:, 0:2 * W_CHUNK].rearrange("p (i c) -> p i c", i=2)
        y = sb("y", [P, CH, D])
        x_new = sb("x_new", [P, CH, D])
        stats = sb("stats", [P, CH, 6])
        mean_var = sb("mean_var", [P, CH, 2])
        var_eps = sb("var_eps", [P, CH, 1])
        rstd = sb("rstd", [P, CH, 1])
        x_hi = sb("x_hi", [P, T * P], F32R)
        x_lo = sb("x_lo", [P, T * P], F32R)
        h = probsT[:].rearrange("p i (j a) b -> p (i j) (a b)", j=2)
        h_hi = sb("h_hi", [P, H_BUFS, N], F32R)
        h_lo = sb("h_lo", [P, H_BUFS, N], F32R)
        yT = probs[:, 0, :, :].rearrange("p (i a) b -> p i (a b)", i=2)
        logitsT = k_heads[0:NR1, 0, :, :, :].rearrange("p b h s -> p (b h s)")
        gates = {n: sb(n, [P, T, NR1]) for n in ("g_shifted", "g_exp", "g_probs", "g_rank", "g_weights")}
        g_max = sb("g_max", [P, T])
        g_sum = sb("g_sum", [P, T])
        g_inv = sb("g_inv", [P, T])
        g_above, g_equal, g_tied, g_before = (
            shifted[:, i * H // 4:(i + 1) * H // 4, :].rearrange("p a (b e j) -> p (a b) e j", e=NE, j=NE)
            for i in range(4))

        ps_scores = bank("ps_scores", 2)
        ps_probsT = bank("ps_probsT", 2)
        ps_qk = bank("ps_qk")
        ps_tr = bank("ps_tr")
        ps_vo = bank("ps_vo")
        ps_y = bank("ps_y")
        scores0, scores1 = ps_scores[:, 0:512], ps_scores[:, 512:1024]
        h_bank = [ps_probsT[:, 0:512], ps_probsT[:, 512:1024], ps_qk[:]]
        y_bank = [ps_tr[:], scores1]
        t_bank = [ps_vo[:], scores0]

        def names(*which):
            return [sem(f"s_{n}") for n in which]

        s_pa, s_pb, s_x_in, s_mask_in, s_out = names("pa", "pb", "x_in", "mask_in", "out")
        s_w_in, s_x_stage, s_kv_stage = ([sem(f"s_{n}{i}") for i in range(2)] for n in ("w_in", "x_stage", "kv_stage"))
        s_bias_mm, s_bo_mm, s_bo, s_bo_D_mm, s_prep, s_half, s_ones, s_zeros, s_rel_hi, s_rel_bias = names(
            "bias_mm", "bo_mm", "bo", "bo_D_mm", "prep", "half", "ones", "zeros", "rel_hi", "rel_bias")
        s_w_hi, s_w_split, s_lin_proj, s_lin_q, s_lin_kv, s_lin_exp, s_lin_phi = names(
            "w_hi", "w_split", "lin_proj", "lin_q", "lin_kv", "lin_exp", "lin_phi")
        s_lin_state, s_lin_masked, s_lin_out, s_lin_den, s_lin_inv, s_lin_norm, s_lin_res = names(
            "lin_state", "lin_masked", "lin_out", "lin_den", "lin_inv", "lin_norm", "lin_res")
        s_qk_mm, s_qk, s_rope_mul, s_rope, s_k_heads, s_v_mm, s_v_heads = names(
            "qk_mm", "qk", "rope_mul", "rope", "k_heads", "v_mm", "v_heads")
        s_scores, s_max, s_shifted, s_exp, s_sum_inv = names("scores", "max", "shifted", "exp", "sum_inv")
        s_probsT_mm, s_probsT, s_attn_mm, s_attnT, s_proj, s_res = names(
            "probsT_mm", "probsT", "attn_mm", "attnT", "proj", "res")
        s_stats, s_mean, s_var, s_rstd, s_x, s_keep, s_xT_mm, s_xT = names(
            "stats", "mean", "var", "rstd", "x", "keep", "xT_mm", "xT")
        s_x_hi, s_x_lo, s_mm1, s_h, s_h_hi, s_h_lo_even, s_h_lo_odd, s_mm2 = names(
            "x_hi", "x_lo", "mm1", "h", "h_hi", "h_lo_even", "h_lo_odd", "mm2")
        s_yT, s_y_mm, s_mix = names("yT", "y_mm", "mix")
        s_gate_mm, s_gate_row, s_gate_tr, s_gate, s_gate_exp = names(
            "gate_mm", "gate_row", "gate_tr", "gate", "gate_exp")

        def A(name, rows=P):
            return pa[0:rows, PACK_A[name]]

        def W(name, rows=P):
            return pb[0:rows, PACK_B[name]]

        def weight(lay, name):
            name = f"{lay.name}_{name}"
            return A(name) if name in PACK_A else W(name)

        def tile(a, t, tiles=1):
            return a[:, bass.ds(t * P * tiles, P * tiles)]

        def landed(t, p):
            return 8 * (t - p) + 16

        ident = A("ident")
        GATE_STEPS = [11, 5]
        lin = None
        layer_B = Layer("B", 0, 1, False, True, False, HD ** -0.5)
        layer_D = Layer("D", 1, 3, True, True, True, HD ** -0.5)
        layer_E = Layer("E", 2, 4, False, False, False, 1.0)
        ffn_C = Ffn(0, 2, [[0, 1], [2], [3], [4], [5]], "C_b1", "C_b2", ACT.Relu, 0, 0, 3)
        ffn_F = Ffn(1, 5, [[6]], "F_b1", "F_b2", ACT.Gelu, NCH * ffn_C.nb, NCH * ffn_C.ng, 2)
        TURN, STATS, NORM, TURN_X = LAG + 1, LAG + 2, LAG + 3, LAG + 5

        block = ctx.enter_context(nc.Block())

        @block.sync
        def _(sp):
            def load_pair(t, p):
                after(sp, s_lin_proj, t - 1)
                sp.dma_start(x_stage[:, p, :], tile(xT_in, t, 2)).then_inc(s_x_stage[p], 16)

            def load_weights(t, p):
                after(sp, s_w_split, t - 1)
                sp.dma_start(w_raw[:, p, :], w_experts[:, bass.ds(t * W_CHUNK, W_CHUNK)]).then_inc(s_w_in[p], 16)

            sp.dma_start(pa[:], pack_a).then_inc(s_pa, 16)
            load_pair(0, 0)
            load_pair(1, 1)
            sp.dma_start(x_nat[:], x.rearrange("(t p) d -> p t d", p=P)).then_inc(s_x_in, 16)
            load_weights(0, 0)
            load_weights(1, 1)
            sp.dma_start(pb[:], pack_b).then_inc(s_pb, 16)
            sp.dma_start(mask_in, key_mask).then_inc(s_mask_in, 16)
            for t in range(2, PAIRS):
                load_pair(t, t % 2)
                load_weights(t, t % 2)
            for c in range(NCH):
                sp.wait_ge(s_x, ffn_F.w(c) + CH)
                sp.dma_start(out.rearrange("(t p) d -> p t d", p=P)[:, c * CH:(c + 1) * CH, :],
                             x_nat[:, c * CH:(c + 1) * CH, :]).then_inc(s_out, 16)
            sp.wait_ge(s_out, 16 * NCH)

        @block.tensor
        def _(pe):
            def prepare_B():
                pe.matmul(ps_y[:, 0:D], A("B_bv").broadcast_to([P, P]), A("B_wo"), start=True, stop=True)\
                  .then_inc(s_bo_mm, 1)
                pe.wait_ge(s_bo, 1)

            def prepare_DE():
                pe.wait_ge(s_pb, 16)
                pe.wait_ge(s_lin_norm, PAIRS)
                pe.matmul(ps_y[:, 0:D], W("D_bv").broadcast_to([P, P]), W("D_wo"), start=True, stop=True)\
                  .then_inc(s_bo_D_mm, 1)
                pe.wait_ge(s_lin_masked, PAIRS)
                for k in range(S):
                    for b in range(BT):
                        mm = pe.matmul(ps_scores[b * S:(b + 1) * S, k * H:(k + 1) * H],
                                       W("buckets", BUCKETS)[:, S - 1 - k:2 * S - 1 - k], W("rel_bias", BUCKETS),
                                       start=True, stop=True)
                mm.then_inc(s_bias_mm, 1)

            def lin_proj(_, t, p):
                pe.wait_ge(s_x_stage[p], landed(t, p))
                after(pe, s_lin_q, t)
                pe.matmul(ps_qk[:, 0:2 * P], A("wq_lin"), x_stage[:, p, :], start=True, stop=True)
                after(pe, s_lin_kv, t)
                for i in range(2):
                    mm = pe.matmul(ps_vo[:, i * 2 * D:(i + 1) * 2 * D], x_stage[:, p, i * P:(i + 1) * P],
                                   A("wkv_lin"), start=True, stop=True)
                mm.then_inc(s_lin_proj, 1)

            def lin_state(_, t, p):
                pe.wait_ge(s_lin_phi, t + 1)
                after(pe, s_lin_masked, t)
                for i in range(2):
                    for b in range(BT):
                        rows = slice(b * S, (b + 1) * S)
                        mm = pe.matmul(ps_scores[:, b * 512 + i * (D + 1):b * 512 + (i + 1) * (D + 1)],
                                       phi[rows, p, (2 + i) * P:(3 + i) * P], v_ones[rows, p, i, :],
                                       start=True, stop=True)
                mm.then_inc(s_lin_state, 1)

            def lin_out(_, t, p):
                pe.wait_ge(s_lin_masked, t + 1)
                after(pe, s_lin_norm, t)
                for i in range(2):
                    for b in range(BT):
                        mm = pe.matmul(ps_y[b * S:(b + 1) * S, i * (D + H):(i + 1) * (D + H)],
                                       phi[:, p, i * P + b * S:i * P + (b + 1) * S], kv_masked[:, p, i, b, :],
                                       start=True, stop=True)
                mm.then_inc(s_lin_out, 1)

            def lin_turn(_, t, p):
                pe.wait_ge(s_x, 2 * t + 2)
                after(pe, s_xT, 2 * t)
                for i in range(2):
                    mm = pe.transpose(ps_tr[:, i * P:(i + 1) * P], x_new[:, 2 * p + i, :], ident)
                mm.then_inc(s_xT_mm, 2)

            def project_qk(lay, t, p):
                u = lay.u(t)
                if lay is layer_B:
                    pe.wait_ge(s_lin_q, PAIRS)
                if lay is layer_D:
                    pe.wait_ge(s_h, NCH * ffn_C.nb)
                after(pe, s_qk, u)
                pe.wait_ge(s_kv_stage[p], 2 * landed(u, p))
                pe.wait_ge(s_xT, lay.w(t) - (T - 1))
                tokens = kv_stage[:, p, :, 0, :]

                def project(name, i, source):
                    return pe.matmul(ps_qk[:, i * P:(i + 1) * P], weight(lay, name), source, start=True, stop=True)

                mm = project("wq", 0, tile(xT, t))
                mm = project("wk", 1, tokens)
                if lay.rope:
                    project("wq_turned", 2, tile(xT, t))
                    mm = project("wk_turned", 3, tokens)
                mm.then_inc(s_qk_mm, 1)

            def project_v(lay, t, p):
                pe.wait_ge(s_xT, lay.w(t) - 4)
                if lay is not layer_E and isinstance(t, int) and t == 0:
                    pe.wait_ge(s_xT, lay.w(0))
                if lay is layer_D and isinstance(t, int) and t == 0:
                    pe.wait_ge(s_yT, NCH * ffn_C.ng)
                after(pe, s_v_heads, lay.u(t))
                for b in range(BT):
                    mm = pe.matmul(ps_tr[:, b * D:(b + 1) * D], kv_stage[:, p, b, :, :], weight(lay, "wv"),
                                   start=True, stop=True)
                mm.then_inc(s_v_mm, 1)

            def project_out(lay, t, p):
                u = lay.u(t)
                pe.wait_ge(s_attnT, u + 1)
                if lay is layer_B:
                    pe.wait_ge(s_prep, 1)
                after(pe, s_res, u)
                pe.matmul(ps_y[:, 0:D], attnT[:, p, :], weight(lay, "wo"), start=True, stop=True)\
                  .then_inc(s_proj, 1)

            def scores(lay, t, p):
                u = lay.u(t)
                if lay is layer_B:
                    pe.wait_ge(s_rel_bias, 1)
                if lay is layer_D:
                    pe.wait_ge(s_yT, NCH * ffn_C.ng)
                pe.wait_ge(s_k_heads, u + 1)
                after(pe, s_shifted, u)
                for half in range(2):
                    cols = slice(half * 512, (half + 1) * 512)
                    whole = ps_scores[:, cols].rearrange("p (h k) -> p h k", k=S)
                    some = slice(half * H // 2, (half + 1) * H // 2)
                    if lay.causal:
                        pe.matmul(whole, id16[:], causal[:].unsqueeze(1).broadcast_to([P, H // 2, S]),
                                  start=True, stop=False, skip_group_check=True)
                    else:
                        pe.matmul(whole, select[:], key_neg[:, t, :].unsqueeze(1).broadcast_to([BT, H // 2, S]),
                                  start=True, stop=False, skip_group_check=True)
                        for part in (rel_hi, rel_lo):
                            pe.matmul(ps_scores[:, cols], ident_r[:], part[:, some, :],
                                      start=False, stop=False, skip_group_check=True)
                    for b in range(BT):
                        mm = pe.matmul(ps_scores[b * S:(b + 1) * S, cols], qk[:, p, b * S:(b + 1) * S],
                                       k_heads[:, p, b, some, :], start=False, stop=True, skip_group_check=True)
                mm.then_inc(s_scores, 1)

            def turn_probs(lay, t, p):
                u = lay.u(t)
                pe.wait_ge(s_exp, u + 1)
                for half in range(2):
                    after(pe, s_probsT, 2 * u - 1 + half)
                    for pair in range(half * H // 4, (half + 1) * H // 4):
                        mm = pe.transpose(ps_probsT[:, pair * P:(pair + 1) * P],
                                          probs[:, p, 2 * pair:2 * pair + 2, :], ident)
                    mm.then_inc(s_probsT_mm, 1)

            def attend(lay, t, p):
                u = lay.u(t)
                pe.wait_ge(s_v_heads, u + 1)
                if lay is layer_B:
                    pe.wait_ge(s_lin_kv, PAIRS)
                if lay is layer_D:
                    pe.wait_ge(s_mix, NCH * ffn_C.ng)
                after(pe, s_attnT, u)
                pe.wait_ge(s_probsT, 2 * u + 2)
                for b in range(BT):
                    for odd in range(2):
                        for strip in range(4):
                            rows = slice(32 * strip, 32 * strip + 32)
                            pe.matmul(ps_vo[rows, 2 * D + b * S:2 * D + (b + 1) * S], v_heads[:, p, b, odd, rows],
                                      probsT[:, p, 2 * strip + odd, b * S:(b + 1) * S],
                                      start=(odd == 0), stop=(odd == 1), skip_group_check=True)
                for odd in range(2):
                    for strip in range(4):
                        rows = slice(32 * strip, 32 * strip + 32)
                        mm = pe.matmul(ps_vo[rows, 3 * D:4 * D], W("value_mask")[:, odd * D:odd * D + 32],
                                       probsT[:, p, 2 * strip + odd, :],
                                       start=(odd == 0), stop=(odd == 1), skip_group_check=True)
                mm.then_inc(s_attn_mm, 1)

            def turn_x(lay, t, p):
                w = lay.w(t)
                pe.wait_ge(s_x, w + 1)
                pe.wait_ge(s_xT, w)
                some = min(t + 5, T) if isinstance(t, int) and lay is not layer_D else t + 5
                pe.wait_ge(s_v_heads, lay.u(some))
                pe.transpose(ps_tr[:, BT * D:BT * D + P], x_new[:, p, :], ident).then_inc(s_xT_mm, 1)

            def gate(ffn, name, experts):
                for c in range(NCH):
                    pe.wait_ge(s_xT, ffn.w(c) - T + CH)
                    if c == 0 and ffn.f:
                        pe.wait_ge(s_res, 3 * T)
                        pe.wait_ge(s_attnT, 3 * T)
                    elif c == 0:
                        pe.wait_ge(s_res, T)
                        pe.wait_ge(s_attnT, T)
                    after(pe, s_gate_row, ffn.f * NCH + c - 1)
                    pe.matmul((ps_y, ps_vo)[c % 2][0:experts, :], W(name), xT[:, c * N:(c + 1) * N],
                              start=True, stop=True).then_inc(s_gate_mm, 1)
                pe.wait_ge(s_gate_row, (ffn.f + 1) * NCH)
                for t in range(T):
                    mm = pe.transpose(ps_y[:, t * experts:(t + 1) * experts], logitsT[0:experts, t * P:(t + 1) * P],
                                      ident[0:experts, 0:experts])
                mm.then_inc(s_gate_tr, 1)

            def feed_forward(ffn, gate_name, experts):
                pe.wait_ge(s_w_split, PAIRS)
                pe.wait_ge(s_probsT, 2 * (T if ffn.f == 0 else 3 * T))
                pe.wait_ge(s_qk, T if ffn.f == 0 else 3 * T)

                def slot(at):
                    if (now := at(0)) is not None:
                        c, j = now
                        g, e, i = ffn.blocks[j]
                        pe.wait_ge(s_x_lo, c + (ffn.f * NCH + 1))
                        after(pe, s_h, ffn.block(c, j) - ffn.h_banks)
                        for n, (w, v) in enumerate(((w_hi, x_hi), (w_hi, x_lo), (w_lo, x_hi))):
                            mm = pe.matmul(h_bank[j % ffn.h_banks], w[:, w1_block(e, i)], v[:, bass.ds(c * N, N)],
                                           start=(n == 0), stop=(n == 2))
                        mm.then_inc(s_mm1, 1)
                        if ffn.at_gate(c, j):
                            gate(ffn, gate_name, experts)
                    if (then := at(LAG)) is not None:
                        c, j = then
                        g, e, i = ffn.blocks[j]
                        pe.wait_ge(s_h_lo_odd if j % 2 else s_h_lo_even, ffn.half(c, j))
                        pe.wait_ge(s_h_hi, ffn.block(c, j))
                        if j in ffn.first:
                            after(pe, s_yT, ffn.group_before(c, g))
                            if ffn.first_group + g < 2 and isinstance(c, int) and c == 0:
                                pe.wait_ge(s_xT, ffn.n * T)
                                pe.wait_ge(s_shifted, T)
                            if ffn.f and isinstance(c, int) and c == 0:
                                pe.wait_ge(s_xT, ffn.n * T)
                        for n, (w, v) in enumerate(((w_hi, h_hi), (w_hi, h_lo), (w_lo, h_hi))):
                            mm = pe.matmul(y_bank[g % 2], w[:, w2_block(e, i)], v[:, j % H_BUFS, :],
                                           start=(j in ffn.first and n == 0), stop=(j in ffn.last and n == 2))
                        mm.then_inc(s_mm2, 1)
                    if (then := at(TURN)) is not None and then[1] in ffn.last:
                        c, g = then[0], ffn.last[then[1]]
                        pe.wait_ge(s_yT, ffn.group(c, g))
                        after(pe, s_mix, ffn.group_before(c, g))
                        if isinstance(c, int) and c == 0:
                            pe.wait_ge(s_gate_row, (ffn.f + 1) * NCH)
                            pe.wait_ge(s_shifted, T if ffn.f == 0 else 3 * T)
                        for t in range(CH):
                            mm = pe.transpose(t_bank[g % 2][:, t * P:(t + 1) * P],
                                              yT[:, g % 2, t * P:(t + 1) * P], ident)
                        mm.then_inc(s_y_mm, 1)
                    if ffn.f == 0 and (then := at(TURN_X)) is not None and then[1] == ffn.nb - 1:
                        c = then[0]
                        pe.wait_ge(s_x, ffn.w(c) + CH)
                        pe.wait_ge(s_xT, ffn.w(c))
                        pe.wait_ge(s_gate, GATE_STEPS[0])
                        for t in range(CH):
                            mm = pe.transpose(ps_y[:, t * P:(t + 1) * P], x_new[:, t, :], ident)
                        mm.then_inc(s_xT_mm, CH)
                ffn.chunks(pe, slot)

            pe.wait_ge(s_pa, 16)
            prepare_B()
            sweep(pe, [lin], PAIRS, 3, [(0, lin_proj), (1, lin_state), (3, lin_turn), (2, lin_out)])
            prepare_DE()
            attention = [(1, project_qk), (2, project_v), (2, scores), (6, turn_x), (3, turn_probs),
                         (4, project_out), (3, attend)]
            sweep(pe, [layer_B], T, 6, attention)
            feed_forward(ffn_C, "C_gate", NE)
            sweep(pe, [layer_D, layer_E], T, 6, attention)
            feed_forward(ffn_F, "F_gate", NR1)

        @block.scalar
        def _(act):
            def lin_q(_, t, p):
                act.wait_ge(s_lin_proj, t + 1)
                act.activation(z[:, p, 0:2 * P], ps_qk[:, 0:2 * P], ACT.Identity, bias=A("bq_lin"))\
                   .then_inc(s_lin_q, 1)

            def lin_exp(_, t, p):
                act.wait_ge(s_lin_q, t + 1)
                act.wait_ge(s_lin_kv, t + 1)
                after(act, s_lin_phi, t - 1)
                act.activation(r_z[:, p, :], z[:, p, :], ACT.Relu)
                act.activation(e_z[:, p, :], z[:, p, :], ACT.Exp).then_inc(s_lin_exp, 1)

            def round_weights(_, t, p):
                act.wait_ge(s_w_in[p], landed(t, p))
                act.copy(w_hi[:, bass.ds(t * W_CHUNK, W_CHUNK)], w_raw[:, p, :]).then_inc(s_w_hi, 1)

            def lin_turn(_, t, p):
                act.wait_ge(s_xT_mm, 2 * t + 2)
                act.copy(tile(xT, t, 2), ps_tr[:, 0:2 * P]).then_inc(s_xT, 2)

            def load_tokens(lay, t, p):
                if lay.own:
                    act.wait_ge(s_xT, lay.w(t) - (T - 1))
                after(act, s_v_mm, lay.u(t) - 1)
                source = xT if lay.own else ctxT_in
                for copy in range(2):
                    act.dma_start(kv_stage[:, p, :, copy, :], tile(source, t).rearrange("p (b s) -> p b s", b=BT))\
                      .then_inc(s_kv_stage[p], 16)

            def take_qk(lay, t, p):
                u = lay.u(t)
                if lay is layer_B:
                    act.wait_ge(s_pb, 16)
                act.wait_ge(s_qk_mm, u + 1)
                if lay.rope:
                    after(act, s_rope_mul, t - 1)
                    for i, b in enumerate(("bq", "bk", "bq_turned", "bk_turned")):
                        last = act.activation(qk_raw[:, p, i * P:(i + 1) * P], ps_qk[:, i * P:(i + 1) * P],
                                              ACT.Identity, bias=weight(lay, b))
                else:
                    after(act, s_scores, u - 1)
                    after(act, s_k_heads, u - 1)
                    if lay.bias:
                        act.activation(qk[:, p, 0:P], ps_qk[:, 0:P], ACT.Identity, bias=weight(lay, "bq"))
                        last = act.activation(qk[:, p, P:2 * P], ps_qk[:, P:2 * P], ACT.Identity,
                                              bias=weight(lay, "bk"))
                    else:
                        last = act.copy(qk[:, p, :], ps_qk[:, 0:2 * P])
                last.then_inc(s_qk, 1)

            def take_v(lay, t, p):
                u = lay.u(t)
                act.wait_ge(s_v_mm, u + 1)
                after(act, s_attn_mm, u - 1)
                if lay is layer_B:
                    act.wait_ge(s_zeros, 1)
                for half in range(2):
                    rows = slice(half * S, (half + 1) * S)
                    for b in range(BT):
                        src = ps_tr[rows, b * D:(b + 1) * D]\
                            .rearrange("p (g o h m) -> p g o h m", o=2, h=2, m=HD)[:, :, :, half, :]
                        dst = v_heads[rows, p, b, :, :]\
                            .rearrange("p c (g o h m) -> p c g o h m", o=2, h=2, m=HD)
                        for odd in range(2):
                            last = act.copy(dst[:, odd, :, odd, half, :], src[:, :, odd, :])
                last.then_inc(s_v_heads, 1)

            def keep_x(lay, t, p):
                act.wait_ge(s_x, lay.w(t) + 1)
                act.copy(x_nat[:, t, :], x_new[:, p, :]).then_inc(s_keep, 1)

            def take_probsT(lay, t, p):
                u = lay.u(t)
                after(act, s_attn_mm, u - 1)
                for half in range(2):
                    act.wait_ge(s_probsT_mm, 2 * u + 1 + half)
                    act.copy(probsT[:, p, half * H // 4:(half + 1) * H // 4, :],
                             ps_probsT[:, half * 512:(half + 1) * 512]).then_inc(s_probsT, 1)

            def exponentiate(lay, t, p):
                u = lay.u(t)
                act.wait_ge(s_shifted, u + 1)
                after(act, s_probsT_mm, 2 * u - 2)
                act.activation(probs[:, p, :, :], shifted[:], ACT.Exp, scale=lay.scale).then_inc(s_exp, 1)

            def take_xT(lay, t, p):
                act.wait_ge(s_xT_mm, lay.w(t) + 1)
                act.copy(tile(xT, t), ps_tr[:, BT * D:BT * D + P]).then_inc(s_xT, 1)

            def gate(ffn, experts):
                for c in range(NCH):
                    act.wait_ge(s_gate_mm, ffn.f * NCH + c + 1)
                    dst, src = logitsT[0:experts, c * N:(c + 1) * N], (ps_y, ps_vo)[c % 2][0:experts, :]
                    if ffn.f == 0:
                        last = act.activation(dst, src, ACT.Identity, bias=W("C_gate_bias", experts))
                    else:
                        last = act.copy(dst, src)
                    last.then_inc(s_gate_row, 1)
                for c in range(1, NCH):
                    round_x(ffn, c)
                act.wait_ge(s_gate, GATE_STEPS[0] * ffn.f + 2)
                act.activation(gates["g_exp"][:, :, 0:experts], gates["g_shifted"][:, :, 0:experts], ACT.Exp)\
                   .then_inc(s_gate_exp, 1)

            def round_x(ffn, c):
                act.wait_ge(s_xT, ffn.w(c) - T + CH)
                act.copy(x_hi[:, c * N:(c + 1) * N], xT[:, c * N:(c + 1) * N]).then_inc(s_x_hi, 1)

            def feed_forward(ffn, experts):
                round_x(ffn, 0)
                act.wait_ge(s_attn_mm, T if ffn.f == 0 else 3 * T)

                def slot(at):
                    if (now := at(0)) is not None:
                        c, j = now
                        act.wait_ge(s_mm1, ffn.block(c, j))
                        after(act, s_h_hi, ffn.block(c, j) - H_BUFS)
                        after(act, s_h_lo_odd if j % 2 else s_h_lo_even, ffn.half(c, j) - H_BUFS // 2)
                        act.activation(h[:, j % H_BUFS, :], h_bank[j % ffn.h_banks], ffn.func,
                                       bias=W(ffn.b1)[:, j:j + 1]).then_inc(s_h, 1)
                        if ffn.at_gate(c, j):
                            gate(ffn, experts)
                    if (then := at(LAG)) is not None and then[1] in ffn.last:
                        c, g = then[0], ffn.last[then[1]]
                        act.wait_ge(s_mm2, ffn.block(*then))
                        after(act, s_y_mm, ffn.group_before(c, g))
                        if ffn.f == 0 and g == 0:
                            last = act.activation(yT[:, 0, :], y_bank[0], ACT.Identity, bias=b2_shared[:],
                                                  scale=1.0 / NS)
                        else:
                            col = g + 1 if ffn.f == 0 else 0
                            last = act.activation(yT[:, g % 2, :], y_bank[g % 2], ACT.Identity,
                                                  bias=W(ffn.b2)[:, col:col + 1])
                        last.then_inc(s_yT, 1)
                    if ffn.f == 0 and (then := at(TURN_X)) is not None and then[1] == ffn.nb - 1:
                        c = then[0]
                        act.wait_ge(s_xT_mm, ffn.w(c) + CH)
                        act.copy(xT[:, bass.ds(c * N, N)], ps_y[:]).then_inc(s_xT, CH)
                ffn.chunks(act, slot)

            act.wait_ge(s_pa, 16)
            sweep(act, [lin], PAIRS, 3, [(0, lin_q), (3, lin_turn), (0, lin_exp), (0, round_weights)])
            attention = [(1, take_qk), (0, load_tokens), (2, take_v), (6, take_xT), (3, take_probsT),
                         (2, exponentiate), (6, keep_x)]
            sweep(act, [layer_B], T, 6, attention)
            feed_forward(ffn_C, NE)
            sweep(act, [layer_D, layer_E], T, 6, attention)
            feed_forward(ffn_F, NR1)

        @block.vector
        def _(dve):
            def norm_statistics(i):
                dve.bn_stats(stats[:, i, :], y[:, i, :]).then_inc(s_stats, 1)

            def norm_variance(first, w, tiles=1):
                for i in range(first, first + tiles):
                    last = dve.bn_aggr(mean_var[:, i, :], stats[:, i, :])
                last.then_inc(s_mean, tiles)
                dve.wait_ge(s_mean, w + tiles)
                some = slice(first, first + tiles)
                dve.tensor_scalar(var_eps[:, some, :], mean_var[:, some, 1:2], EPS, None, ALU.add)\
                   .then_inc(s_var, tiles)

            def norm_apply(i, w, buffers, dst=None):
                dve.wait_ge(s_rstd, w + 1)
                if dst is None:
                    after(dve, s_xT_mm, w - (buffers - 1))
                    after(dve, s_keep, w - (buffers - 1))
                    dst = x_new[:, i, :]
                dve.tensor_scalar(dst, y[:, i, :], mean_var[:, i, 0:1], rstd[:, i, :], ALU.subtract, ALU.mult)\
                   .then_inc(s_x, 1)

            def prepare_B():
                dve.memset(v_ones[:, :, :, D:D + 1], 1.0).then_inc(s_ones, 1)
                dve.wait_ge(s_bo_mm, 1)
                dve.tensor_tensor(bo_B[:], ps_y[:, 0:D], A("B_bo"), ALU.add).then_inc(s_bo, 1)

            def prepare_DE():
                dve.wait_ge(s_pb, 16)
                dve.tensor_copy(id16[:], ident)
                dve.tensor_copy(ident_r[:], ident)
                dve.tensor_copy(causal[:], W("causal"))
                dve.tensor_copy(select[:], W("select", BT))
                dve.tensor_tensor(b2_shared[:], W("C_b2")[:, 0:1], W("C_b2")[:, 1:2], ALU.add).then_inc(s_ones, 1)
                dve.wait_ge(s_mask_in, 16)
                dve.tensor_scalar(key_neg[:], mask_in, -NEG, NEG, ALU.mult, ALU.add)
                dve.wait_ge(s_ones, 2)
                dve.tensor_scalar(b2_shared[:], b2_shared[:], 1.0 / NS, None, ALU.mult)
                dve.wait_ge(s_bo_D_mm, 1)
                dve.tensor_tensor(bo_D[:], ps_y[:, 0:D], W("D_bo"), ALU.add).then_inc(s_prep, 1)
                dve.wait_ge(s_bias_mm, 1)
                bias = ps_scores[:].rearrange("p (k h) -> p k h", h=H)
                upper, lower = (r[:].rearrange("p h k -> p k h") for r in (rel_hi, rel_lo))
                dve.tensor_copy(upper, bias).then_inc(s_rel_hi, 1)
                dve.wait_ge(s_rel_hi, 1)
                dve.tensor_tensor(lower, bias, upper.bitcast(F32), ALU.subtract).then_inc(s_rel_bias, 1)

            def lin_kv(_, t, p):
                dve.wait_ge(s_lin_proj, t + 1)
                after(dve, s_lin_exp, t - 1)
                after(dve, s_lin_state, t - 1)
                both = ps_vo[:].rearrange("p (i c) -> p i c", i=2)
                bias = A("bkv_lin").rearrange("p (i d) -> p i d", i=2)
                dve.tensor_tensor(z[:, p, 2 * P:4 * P].rearrange("p (i d) -> p i d", i=2), both[:, :, 0:D],
                                  bias[:, 0:1, :].broadcast_to([P, 2, D]), ALU.add)
                dve.tensor_tensor(v_ones[:, p, :, 0:D], both[:, :, D:2 * D],
                                  bias[:, 1:2, :].broadcast_to([P, 2, D]), ALU.add).then_inc(s_lin_kv, 1)

            def lin_masked(_, t, p):
                dve.wait_ge(s_lin_state, t + 1)
                after(dve, s_lin_out, t - 1)
                for b in range(BT):
                    state = ps_scores[:, b * 512:b * 512 + 2 * (D + 1)].rearrange("p (i c) -> p i c", i=2)
                    dve.tensor_tensor(kv_masked[:, p, :, b, 0:D], state[:, :, 0:D],
                                      A("block_mask").unsqueeze(1).broadcast_to([P, 2, D]), ALU.mult)
                    last = dve.tensor_tensor(kv_masked[:, p, :, b, D:D + H],
                                             state[:, :, D:D + 1].broadcast_to([P, 2, H]),
                                             A("head_mask").unsqueeze(1).broadcast_to([P, 2, H]), ALU.mult)
                last.then_inc(s_lin_masked, 1)

            def lin_out(_, t, p):
                dve.wait_ge(s_lin_out, t + 1)
                both = ps_y[:, 0:2 * (D + H)].rearrange("p (i c) -> p i c", i=2)
                dve.tensor_scalar(den[:], both[:, :, D:D + H], 1e-6, None, ALU.add).then_inc(s_lin_den, 1)
                dve.wait_ge(s_lin_den, t + 1)
                dve.reciprocal(den_inv[:], den[:]).then_inc(s_lin_inv, 1)
                dve.wait_ge(s_lin_inv, t + 1)
                dve.tensor_tensor(o_lin[:].rearrange("p i (h m) -> p i h m", h=H),
                                  both[:, :, 0:D].rearrange("p i (h m) -> p i h m", h=H),
                                  den_inv[:].unsqueeze(3).broadcast_to([P, 2, H, HD]), ALU.mult)\
                   .then_inc(s_lin_norm, 1)
                dve.wait_ge(s_lin_norm, t + 1)
                dve.tensor_tensor(y[:, 2 * p:2 * p + 2, :], o_lin[:], x_nat[:, bass.ds(2 * t, 2), :], ALU.add)\
                   .then_inc(s_lin_res, 1)
                dve.wait_ge(s_lin_res, t + 1)
                norm_statistics(2 * p)
                norm_statistics(2 * p + 1)
                dve.wait_ge(s_stats, 2 * t + 2)

            def lin_phi(_, t, p):
                dve.wait_ge(s_lin_exp, t + 1)
                after(dve, s_lin_out, t - 1)
                dve.scalar_tensor_tensor(phi[:, p, :], e_z[:, p, :], 1.0, r_z[:, p, :], ALU.min, ALU.add)\
                   .then_inc(s_lin_phi, 1)

            def lin_norm_variance(_, t, p):
                norm_variance(2 * p, 2 * t, 2)

            def lin_norm_apply(_, t, p):
                for i in range(2):
                    norm_apply(2 * p + i, 2 * t + i, CH)

            def rotate(lay, t, p):
                if not lay.rope:
                    return
                dve.wait_ge(s_qk, lay.u(t) + 1)
                after(dve, s_rope, t)
                by = lambda name: W(name).unsqueeze(1).broadcast_to([P, 2 * BT, S])
                parts = qk_raw[:, p, :].rearrange("p (i s) -> p i s", s=S)
                dve.tensor_tensor(straight[:].rearrange("p (i s) -> p i s", s=S), parts[:, 0:2 * BT, :],
                                  by("cos"), ALU.mult)
                dve.tensor_tensor(turned[:].rearrange("p (i s) -> p i s", s=S), parts[:, 2 * BT:4 * BT, :],
                                  by("sin"), ALU.mult).then_inc(s_rope_mul, 1)
                dve.wait_ge(s_rope_mul, t + 1)
                after(dve, s_scores, lay.u(t) - 1)
                after(dve, s_k_heads, lay.u(t) - 1)
                dve.tensor_tensor(qk[:, p, :], straight[:], turned[:], ALU.add).then_inc(s_rope, 1)

            def invert_sums(lay, t, p):
                dve.wait_ge(s_attn_mm, lay.u(t) + 1)
                dve.reciprocal(sum_inv[:], ps_vo[:, 3 * D:4 * D]).then_inc(s_sum_inv, 1)

            def normalize_heads(lay, t, p):
                u = lay.u(t)
                dve.wait_ge(s_sum_inv, u + 1)
                after(dve, s_proj, u - 1)
                dve.tensor_tensor(attnT[:, p, :], ps_vo[:, 2 * D:3 * D], sum_inv[:], ALU.mult)\
                   .then_inc(s_attnT, 1)

            def add_residual(lay, t, p):
                u = lay.u(t)
                dve.wait_ge(s_proj, u + 1)
                dve.wait_ge(s_keep, lay.w(t) - (T - 1))
                dve.tensor_tensor(y[:, p, :], ps_y[:, 0:D], x_nat[:, t, :], ALU.add).then_inc(s_res, 1)
                dve.wait_ge(s_res, u + 1)
                norm_statistics(p)

            def find_max(lay, t, p):
                u = lay.u(t)
                dve.wait_ge(s_scores, u + 1)
                dve.tensor_reduce(row_max[:], ps_scores[:].rearrange("p (h k) -> p h k", h=H), AX.X, ALU.max)\
                   .then_inc(s_max, 1)

            def shift(lay, t, p):
                u = lay.u(t)
                dve.wait_ge(s_max, u + 1)
                after(dve, s_exp, u)
                dve.tensor_tensor(shifted[:], ps_scores[:].rearrange("p (h k) -> p h k", h=H),
                                  row_max[:].unsqueeze(2).broadcast_to([P, H, S]), ALU.subtract)\
                   .then_inc(s_shifted, 1)

            def wait_statistics(lay, t, p):
                dve.wait_ge(s_stats, lay.w(t) + 1)

            def attention_variance(lay, t, p):
                norm_variance(p, lay.w(t))

            def attention_norm(lay, t, p):
                norm_apply(p, lay.w(t), 2)

            def gate(ffn, experts):
                count = [GATE_STEPS[0] * ffn.f]

                def link(instruction):
                    count[0] += 1
                    instruction.then_inc(s_gate, 1)
                    dve.wait_ge(s_gate, count[0])

                g = {n: t[:, :, 0:experts] for n, t in gates.items()}
                over = lambda t: t[:].unsqueeze(2).broadcast_to([P, T, experts])
                for c in range(1, NCH):
                    split_x(ffn, c)
                dve.wait_ge(s_gate_tr, ffn.f + 1)
                logits = ps_y[:, 0:T * experts].rearrange("p (t e) -> p t e", e=experts)
                link(dve.tensor_reduce(g_max[:], logits, AX.X, ALU.max))
                link(dve.tensor_tensor(g["g_shifted"], logits, over(g_max), ALU.subtract))
                dve.wait_ge(s_gate_exp, ffn.f + 1)
                link(dve.tensor_reduce(g_sum[:], g["g_exp"], AX.X, ALU.add))
                link(dve.reciprocal(g_inv[:], g_sum[:]))
                link(dve.tensor_tensor(g["g_probs"], g["g_exp"], over(g_inv), ALU.mult))
                if ffn.f == 0:
                    probs_e = g["g_probs"].unsqueeze(3).broadcast_to([P, T, NE, NE])
                    probs_j = g["g_probs"].unsqueeze(2).broadcast_to([P, T, NE, NE])
                    lower = W("lower").rearrange("p (e j) -> p e j", e=NE).unsqueeze(1).broadcast_to([P, T, NE, NE])
                    link(dve.tensor_tensor(g_above, probs_j, probs_e, ALU.is_gt))
                    link(dve.tensor_tensor(g_equal, probs_j, probs_e, ALU.is_equal))
                    link(dve.tensor_tensor(g_tied, g_equal, lower, ALU.mult))
                    link(dve.tensor_tensor(g_before, g_above, g_tied, ALU.add))
                    link(dve.tensor_reduce(g["g_rank"], g_before, AX.X, ALU.add))
                    link(dve.scalar_tensor_tensor(g["g_weights"], g["g_rank"], 2.0, g["g_probs"], ALU.is_lt,
                                                  ALU.mult))
                assert count[0] == GATE_STEPS[0] * ffn.f + GATE_STEPS[ffn.f]

            def split_x(ffn, c):
                dve.wait_ge(s_x_hi, ffn.f * NCH + c + 1)
                cols = slice(c * N, (c + 1) * N)
                dve.tensor_tensor(x_lo[:, cols], xT[:, cols], x_hi[:, cols].bitcast(F32), ALU.subtract)\
                   .then_inc(s_x_lo, 1)

            def mix(ffn, c, g):
                dve.wait_ge(s_y_mm, ffn.group(c, g))
                after(dve, s_mix, ffn.group(c, g - 1))
                bank = t_bank[g % 2]
                if g == 0:
                    dve.wait_ge(s_keep, ffn.w(c) - (T - CH))
                    dve.wait_ge(s_x, ffn.w(c))
                if ffn.f == 0 and g == 0:
                    dve.tensor_tensor(y[:].rearrange("p t d -> p (t d)"), bank,
                                      x_nat[:, bass.ds(c * CH, CH), :].rearrange("p t d -> p (t d)"), ALU.add)\
                       .then_inc(s_mix, 1)
                    return
                e, weights = (g - 1, gates["g_weights"]) if ffn.f == 0 else (NR1 - 1, gates["g_probs"])
                for t in range(CH):
                    before = y[:, t, :] if ffn.f == 0 else x_nat[:, c * CH + t, :]
                    last = dve.scalar_tensor_tensor(y[:, t, :], bank[:, t * P:(t + 1) * P],
                                                    weights[:, c * CH + t, e:e + 1], before, ALU.mult, ALU.add)
                last.then_inc(s_mix, 1)

            def feed_forward(ffn, experts):
                split_x(ffn, 0)

                def slot(at):
                    if (now := at(0)) is not None:
                        c, j = now
                        dve.wait_ge(s_h, ffn.block(c, j))
                        after(dve, s_mm2, ffn.block(c, j) - H_BUFS)
                        dve.tensor_copy(h_hi[:, j % H_BUFS, :], h[:, j % H_BUFS, :]).then_inc(s_h_hi, 1)
                        if j % 2 == 0:
                            dve.wait_ge(s_h_hi, ffn.block(c, j))
                            dve.tensor_tensor(h_lo[:, j % H_BUFS, :], h[:, j % H_BUFS, :],
                                              h_hi[:, j % H_BUFS, :].bitcast(F32), ALU.subtract)\
                               .then_inc(s_h_lo_even, 1)
                        if ffn.at_gate(c, j):
                            gate(ffn, experts)
                    if (then := at(TURN)) is not None and then[1] in ffn.last:
                        mix(ffn, then[0], ffn.last[then[1]])
                    if (then := at(STATS)) is not None and then[1] == ffn.nb - 1:
                        c = then[0]
                        dve.wait_ge(s_mix, ffn.group(c, ffn.ng - 1))
                        for t in range(CH):
                            norm_statistics(t)
                        dve.wait_ge(s_stats, ffn.w(c) + CH)
                    if (then := at(NORM)) is not None and then[1] == ffn.nb - 1:
                        norm_variance(0, ffn.w(then[0]), CH)
                    if (then := at(NORM + 1)) is not None and then[1] == ffn.nb - 1:
                        c = then[0]
                        for t in range(CH):
                            norm_apply(t, ffn.w(c) + t, CH, x_nat[:, c * CH + t, :] if ffn.f else None)
                ffn.chunks(dve, slot)

            dve.wait_ge(s_pa, 16)
            prepare_B()
            dve.wait_ge(s_x_in, 16)
            sweep(dve, [lin], PAIRS, 3, [(0, lin_kv), (1, lin_masked), (2, lin_out), (0, lin_phi),
                                      (2, lin_norm_variance), (2, lin_norm_apply)])
            prepare_DE()
            attention = [(5, add_residual), (5, wait_statistics), (4, invert_sums), (5, attention_variance),
                         (4, normalize_heads), (1, rotate), (2, find_max), (2, shift), (5, attention_norm)]
            sweep(dve, [layer_B], T, 6, attention)
            feed_forward(ffn_C, NE)
            sweep(dve, [layer_D, layer_E], T, 6, attention)
            feed_forward(ffn_F, NR1)

        @block.gpsimd
        def _(pool):
            def inverse_deviation(first, w, tiles=1):
                some = slice(first, first + tiles)
                pool.wait_ge(s_var, w + tiles)
                pool.tensor_tensor(rstd[:, some, 0], var_eps[:, some, 0],
                                   minus_half[:, 0:1].broadcast_to([P, tiles]), ALU.pow).then_inc(s_rstd, tiles)

            def keep(i, w, dst, bias):
                pool.wait_ge(s_x, w + 1)
                pool.tensor_tensor(dst, x_new[:, i, :], bias[:], ALU.add).then_inc(s_keep, 1)

            def split_weights(_, t, p):
                cols = bass.ds(t * W_CHUNK, W_CHUNK)
                pool.wait_ge(s_w_hi, t + 1)
                pool.tensor_tensor(w_lo[:, cols], w_raw[:, p, :], w_hi[:, cols].bitcast(F32), ALU.subtract)\
                    .then_inc(s_w_split, 1)

            def lin_deviation(_, t, p):
                inverse_deviation(2 * p, 2 * t, 2)

            def lin_keep(_, t, p):
                for i in range(2):
                    keep(2 * p + i, 2 * t + i, x_nat[:, 2 * t + i, :], bo_B)

            def k_to_heads(lay, t, p, b):
                return pool.tensor_tensor(
                    k_heads[:, p, b, :, :],
                    qk[:, p, P + b * S:P + (b + 1) * S].unsqueeze(1).broadcast_to([P, H, S]),
                    A("head_mask").unsqueeze(2).broadcast_to([P, H, S]), ALU.mult)

            def first_batch(lay, t, p):
                pool.wait_ge(s_rope if lay.rope else s_qk, t + 1 if lay.rope else lay.u(t) + 1)
                after(pool, s_scores, lay.u(t) - 1)
                k_to_heads(lay, t, p, 0)

            def second_batch(lay, t, p):
                k_to_heads(lay, t, p, 1).then_inc(s_k_heads, 1)

            def deviation(lay, t, p):
                inverse_deviation(p, lay.w(t))

            def feed_forward(ffn):
                def slot(at):
                    if (now := at(0)) is not None and now[1] % 2:
                        c, j = now
                        pool.wait_ge(s_h_hi, ffn.block(c, j))
                        after(pool, s_mm2, ffn.block(c, j) - H_BUFS)
                        pool.tensor_tensor(h_lo[:, j % H_BUFS, :], h[:, j % H_BUFS, :],
                                           h_hi[:, j % H_BUFS, :].bitcast(F32), ALU.subtract)\
                            .then_inc(s_h_lo_odd, 1)
                    if (then := at(NORM)) is not None and then[1] == ffn.nb - 1:
                        inverse_deviation(0, ffn.w(then[0]), CH)
                    if ffn.f == 0 and (then := at(NORM + 2)) is not None and then[1] == ffn.nb - 1:
                        c = then[0]
                        for t in range(CH):
                            keep(t, ffn.w(c) + t, x_nat[:, c * CH + t, :], bo_D)
                ffn.chunks(pool, slot)

            pool.memset(v_heads[:], 0.0).then_inc(s_zeros, 1)
            pool.memset(minus_half[:], -0.5).then_inc(s_half, 1)
            pool.wait_ge(s_half, 1)
            pool.wait_ge(s_bo, 1)
            sweep(pool, [lin], PAIRS, 3, [(0, split_weights), (2, lin_deviation), (2, lin_keep)])
            pool.wait_ge(s_rel_bias, 1)
            attention = [(1, first_batch), (5, deviation), (1, second_batch)]
            sweep(pool, [layer_B], T, 6, attention)
            feed_forward(ffn_C)
            sweep(pool, [layer_D, layer_E], T, 6, attention)
            feed_forward(ffn_F)


def constants():
    f32 = np.float32
    feature, head = np.arange(D), np.arange(D) // HD
    row = np.arange(P)
    out = {"ident": np.eye(P, dtype=f32),
           "head_mask": (head[:, None] == np.arange(H)[None, :]).astype(f32),
           "block_mask": (head[:, None] == head[None, :]).astype(f32)}
    keep = (head[None, None, :] % 2 == (row // S)[:, None, None]) & \
        ((head // 2)[None, None, :] % 2 == np.arange(2)[None, :, None])
    out["value_mask"] = keep.astype(f32).reshape(P, 2 * D)
    half = HD // 2
    theta = np.power(f32(1250.0), (f32(-2.0) * np.arange(half, dtype=f32) / f32(HD)).astype(f32)).astype(f32)
    angle = (np.arange(1, S + 1, dtype=f32)[None, :] * np.tile(theta, 2)[feature % HD][:, None]).astype(f32)
    out["cos"] = np.cos(angle).astype(f32)
    out["sin"] = (np.sin(angle) * np.where(feature % HD < half, -1.0, 1.0)[:, None]).astype(f32)
    e = np.arange(NE)
    out["lower"] = np.broadcast_to((e[None, :] < e[:, None]).astype(f32).reshape(1, -1), (P, NE * NE))
    distance = (S - 1 - np.arange(P))
    nb, exact = BUCKETS // 2, BUCKETS // 4
    size = np.abs(distance)
    large = exact + (np.log(np.maximum(size, 1).astype(f32) / exact) / np.log(128 / exact) * (nb - exact))\
        .astype(f32).astype(np.int32)
    bucket = (distance > 0) * nb + np.where(size < exact, size, np.minimum(large, nb - 1))
    hot = np.zeros((P, P), f32)
    hot[bucket, np.arange(P)] = 1.0
    out["buckets"] = hot
    out["causal"] = np.where(np.arange(S)[None, :] > (row % S)[:, None], NEG, 0.0).astype(f32)
    out["select"] = (row[None, :] // S == np.arange(BT)[:, None]).astype(f32)
    return out


def arrays(inputs):
    i = {n: np.asarray(a) for n, a in inputs.items()}

    def column(a):
        return np.asarray(a, np.float32).reshape(-1, P).T

    def rows(a):
        return np.broadcast_to(a.reshape(1, -1), (P, a.size))

    turned = np.arange(D) ^ (HD // 2)
    part = constants()
    part["wq_lin"] = i["L0_attn_W_qkv"][:, 0:D]
    part["wkv_lin"] = i["L0_attn_W_qkv"][:, D:3 * D]
    part["bq_lin"] = column(i["L0_attn_b_qkv"][0:D])
    part["bkv_lin"] = rows(i["L0_attn_b_qkv"][D:3 * D])
    for n in "qkvo":
        part[f"B_w{n}"] = i[f"L0_xattn_W{n}"]
        part[f"D_w{n}"] = i[f"L1_attn_W{n}"].T
        part[f"E_w{n}"] = i[f"L1_xattn_W{n}"].T
        if n != "o":
            part[f"B_b{n}"] = column(i[f"L0_xattn_b{n}"])
            part[f"D_b{n}"] = column(i[f"L1_attn_b{n}"])
    for n in "qk":
        part[f"D_w{n}_turned"] = part[f"D_w{n}"][:, turned]
        part[f"D_b{n}_turned"] = part[f"D_b{n}"][turned]
    part["B_bo"] = rows(i["L0_xattn_bo"])
    part["D_bo"] = rows(i["L1_attn_bo"])
    part["C_b1"] = np.concatenate([column(i["L0_ffn_sb1"]), column(i["L0_ffn_rb1"])], 1)
    part["C_b2"] = np.concatenate([column(i["L0_ffn_sb2"]), column(i["L0_ffn_rb2"])], 1)
    part["F_b1"] = column(i["L1_ffn_b1"][NR1 - 1])
    part["F_b2"] = column(i["L1_ffn_b2"][NR1 - 1])
    part["C_gate"] = i["L0_ffn_gate_w"]
    part["C_gate_bias"] = i["L0_ffn_gate_b"].reshape(NE, 1)
    part["F_gate"] = i["L1_ffn_Wr"].T
    part["rel_bias"] = i["L1_xattn_rel_bias"].T

    def pack(columns, width):
        out = np.zeros((P, width), np.float32)
        for name, where in columns.items():
            out[0:part[name].shape[0], where] = part[name]
        return out

    experts = [(i["L0_ffn_sw1"][e], i["L0_ffn_sw2"][e]) for e in range(NS)]
    experts += [(i["L0_ffn_rw1"][e], i["L0_ffn_rw2"][e]) for e in range(NE)]
    experts += [(i["L1_ffn_W1"][NR1 - 1], i["L1_ffn_W2"][NR1 - 1])]
    w_experts = np.concatenate(
        [a for w1, w2 in experts for a in (w1, w2.reshape(FB, P, D).transpose(1, 0, 2).reshape(P, F))], 1)
    return {"x": i["x"].reshape(B * S, D), "xT": i["x"].reshape(B * S, D).T, "ctxT": i["ctx_1024"].reshape(B * S, D).T,
            "pack_a": pack(PACK_A, WIDTH_A), "pack_b": pack(PACK_B, WIDTH_B), "w_experts": w_experts,
            "key_mask": i["mask_Bx1x1xS2_bk0"].reshape(T, BT, S).transpose(1, 0, 2).astype(np.int32)}


def kernel(**inputs):
    import concourse.bacc as bacc
    from concourse.bass_utils import run_bass_kernel_spmd

    nc = bacc.Bacc("TRN2", target_bir_lowering=False, num_devices=1)
    given, args = {}, []
    for name, a in arrays(inputs).items():
        a = np.ascontiguousarray(a)
        given[f"in_{name}"] = a
        args.append(nc.dram_tensor(f"in_{name}", a.shape, mybir.dt.from_np(a.dtype), kind="ExternalInput").ap())
    result = nc.dram_tensor("result", (B * S, D), F32, kind="ExternalOutput").ap()
    build(nc, *args, result)
    r = run_bass_kernel_spmd(nc, [given], core_ids=[0])
    return r.results[0]["result"].reshape(B, S, D)
```

```python
from contextlib import ExitStack

import concourse.bass as bass
import numpy as np
from concourse import mybir

ALU = mybir.AluOpType
ACT = mybir.ActivationFunctionType
AX = mybir.AxisListType
F32 = mybir.dt.float32
F32R = mybir.dt.float32r
BF16 = mybir.dt.bfloat16

B, S, D, H = 32, 64, 128, 16
HD = D // H
P = 128
BT = P // S
T = B * S // P
CH = 4
NCH = T // CH
N = CH * P
F = 512
FB = F // P
NS, NE = 2, 4
NR1 = 8
BUCKETS = 32
KEYS = P // BUCKETS
EPS = 1e-5
NEG = -1e30
PAIRS = T // 2
H_BUFS = 4
LAG = 3

def _columns(widths):
    at, out = 0, {}
    for name, width in widths:
        out[name] = slice(at, at + width)
        at += width
    return out, at


PACK_A, WIDTH_A = _columns([
    ("wq_lin", D), ("wkv_lin", 2 * D), ("bkv_lin", 2 * D), ("bq_lin", 1),
    ("ident", P), ("head_mask", H), ("block_mask", D), ("B_wo", D), ("B_bo", D), ("B_bv", 1)])
PACK_B, WIDTH_B = _columns([
    ("B_wq", D), ("B_wk", D), ("B_wv_parity", D),
    ("D_wq", D), ("D_wk", D), ("D_wq_turned", D), ("D_wk_turned", D), ("D_wv_parity", D), ("D_wo", D), ("D_bo", D),
    ("E_wq", D), ("E_wk", D), ("E_wv_parity", D), ("E_wo", D),
    ("B_bq", 1), ("B_bk", 1),
    ("D_bq", 1), ("D_bk", 1), ("D_bq_turned", 1), ("D_bk_turned", 1), ("D_bv", 1),
    ("C_b1", (NS + NE) * FB), ("F_b1", FB), ("C_b2", NS + NE), ("F_b2", 1),
    ("C_gate", NE), ("F_gate", NR1), ("C_gate_bias", 1),
    ("value_mask", 2 * D), ("cos", S), ("sin", S), ("lower", NE * NE),
    ("rel_bias", KEYS * H), ("buckets", P), ("causal", S), ("select", P)])
EXPERT_COLS = 2 * F
W_COLS = (NS + NE + 1) * EXPERT_COLS
W_CHUNK = W_COLS // PAIRS


def w1_block(expert, f):
    at = expert * EXPERT_COLS + f * P
    return slice(at, at + P)


def w2_block(expert, f):
    at = expert * EXPERT_COLS + F + f * P
    return slice(at, at + P)


def after(engine, semaphore, count):
    if not isinstance(count, int) or count > 0:
        engine.wait_ge(semaphore, count)


def open_sweep(layer, steps, stages):
    for k in range(steps):
        for behind, stage in stages:
            if k >= behind:
                stage(layer, k - behind, (k - behind) % 2)


def sweep(engine, layers, tiles, depth, stages, opened=0, before={}):
    def step(n, k, kk):
        for behind, stage in stages:
            if 0 <= kk - behind < tiles:
                stage(layers[n], k - behind, (kk - behind) % 2)
            elif kk - behind < 0 and n > 0:
                stage(layers[n - 1], tiles + kk - behind, (kk - behind) % 2)

    peeled = depth + 2 - depth % 2
    for n in range(len(layers)):
        for k in range(opened if n == 0 else 0, peeled):
            step(n, k, k)
        with engine.Fori(0, (tiles - peeled) // 2) as i:
            step(n, 2 * i + peeled, peeled)
            step(n, 2 * i + (peeled + 1), peeled + 1)
    for k in range(tiles, tiles + depth):
        if k in before:
            before[k]()
        step(len(layers) - 1, k, k)


class Layer:

    def __init__(self, name, a, n, own, causal, rope, scale):
        self.name, self.a, self.n, self.own, self.causal, self.rope, self.scale = name, a, n, own, causal, rope, scale
        self.bias = name in "BD"

    def u(self, t):
        return t + self.a * T

    def w(self, t):
        return t + self.n * T


class Ffn:

    def __init__(self, f, n, groups, name, experts, func, first_block, first_group, h_banks):
        self.f, self.n, self.experts, self.func, self.h_banks = f, n, experts, func, h_banks
        self.b1, self.b2, self.gate = f"{name}_b1", f"{name}_b2", f"{name}_gate"
        self.blocks = [(g, e, i) for g, es in enumerate(groups) for e in es for i in range(FB)]
        self.nb, self.ng = len(self.blocks), len(groups)
        self.last = {max(j for j, b in enumerate(self.blocks) if b[0] == g): g for g in range(self.ng)}
        self.first = {min(j for j, b in enumerate(self.blocks) if b[0] == g): g for g in range(self.ng)}
        self.first_block, self.first_group = first_block, first_group

    def block(self, c, j):
        return c * self.nb + (self.first_block + j + 1)

    def half(self, c, j):
        return c * (self.nb // 2) + ((self.first_block + j) // 2 + 1)

    def group(self, c, g):
        return c * self.ng + (self.first_group + g + 1)

    def group_before(self, c, g):
        if g >= 2:
            return self.group(c, g - 2)
        return self.group(c, max(x for x in range(self.ng) if x % 2 == g % 2) - self.ng)

    def number(self, c, j):
        return c * self.nb + j if isinstance(c, int) else None

    def y_bank(self, g):
        return 2 if self.ng > 1 and g == self.ng - 1 else g % 2

    def w(self, c):
        return CH * c + self.n * T

    def chunks(self, engine, slot, before={}):
        furthest = LAG + (8 if self.f == 0 else 4)
        peeled = -(-furthest // self.nb)
        if NCH - peeled < 3:
            peeled = NCH

        def run(c, j, static):
            def at(behind):
                back, jj = 0, j - behind
                while jj < 0:
                    back, jj = back + 1, jj + self.nb
                if static and not 0 <= c - back < NCH:
                    return None
                return c - back, jj
            slot(at)

        for c in range(peeled):
            for j in range(self.nb):
                run(c, j, True)
        if peeled < NCH:
            with engine.Fori(peeled, NCH) as c:
                for j in range(self.nb):
                    run(c, j, False)
        for j in range(furthest + 1):
            if j in before:
                before[j]()
            run(NCH + j // self.nb, j % self.nb, True)


def build(nc, x, xT_in, ctxT_in, pack_a, pack_b, w_experts, key_mask, out):
    with ExitStack() as ctx:
        def sb(name, shape, dt=F32):
            return ctx.enter_context(nc.sbuf_tensor(name, shape, dt))

        def bank(name, banks=1):
            return ctx.enter_context(nc.psum_tensor(name, [P, 512 * banks], F32))

        def sem(name):
            return ctx.enter_context(nc.semaphore(name))

        x_nat = sb("x_nat", [P, T, D])
        xT = sb("xT", [P, T * P])
        pa = sb("pa", [P, WIDTH_A])
        pb = sb("pb", [P, WIDTH_B])
        w_hi = sb("w_hi", [P, W_COLS], F32R)
        w_lo = sb("w_lo", [P, W_COLS], F32R)
        id16 = sb("id16", [P, P], BF16)
        causal = sb("causal", [P, S], BF16)
        select = sb("select", [BT, P], BF16)
        key_neg = sb("key_neg", [BT, T, S], BF16)
        rel_hi = sb("rel_hi", [P, H, S], F32R)
        rel_lo = sb("rel_lo", [P, H, S], F32R)
        ident_r = sb("ident_r", [P, P], F32R)
        bo_B = sb("bo_B", [P, D])
        bo_D = sb("bo_D", [P, D])
        b2_shared = sb("b2_shared", [P, 1])
        minus_half = sb("minus_half", [P, 2])
        table_warm = sb("table_warm", [P, 2])
        v_ones = sb("v_ones", [P, 2, 2, D + 1])
        den = sb("den", [P, 2, H])
        den_inv = sb("den_inv", [P, 2, H])
        o_lin = sb("o_lin", [P, 2, D])
        kv_stage = sb("kv_stage", [P, 2, P])
        qk = sb("qk", [P, 2, 2 * P])
        qk_raw = sb("qk_raw", [P, 2, 4 * P])
        turned = sb("turned", [P, 2 * P])
        straight = sb("straight", [P, 2 * P])
        k_heads = sb("k_heads", [P, 2, BT, H, S])
        v_heads = sb("v_heads", [P, 2, BT, 2, D])
        row_max = sb("row_max", [P, H])
        shifted = sb("shifted", [P, H, S])
        probs = sb("probs", [P, 2, H, S])
        probsT = sb("probsT", [P, 2, H // 2, P])
        sum_inv = sb("sum_inv", [P, P])
        attnT = sb("attnT", [P, 2, P])
        r_z, e_z = (k_heads[:, 0, b, :, :].rearrange("p (i h) s -> p i (h s)", i=2) for b in range(BT))
        mask_in = k_heads[0:BT, 1, 0, :, :].bitcast(mybir.dt.int32)
        z = qk_raw
        phi = shifted[:].rearrange("p (i h) s -> p i (h s)", i=2)
        room = probsT[:].rearrange("p i a b -> p (i a b)")
        x_stage = room[:, 0:4 * P].rearrange("p (i c) -> p i c", i=2)
        kv_masked = room[:, 4 * P:4 * P + 4 * BT * (D + H)]\
            .rearrange("p (i j b c) -> p i j b c", i=2, j=2, b=BT)
        w_raw = probs[:].rearrange("p i h s -> p (i h s)")[:, 0:2 * W_CHUNK].rearrange("p (i c) -> p i c", i=2)
        y = sb("y", [P, CH, D])
        x_new = sb("x_new", [P, CH, D])
        stats = sb("stats", [P, CH, 6])
        mean_var = sb("mean_var", [P, CH, 2])
        var_eps = sb("var_eps", [P, CH, 1])
        rstd = sb("rstd", [P, CH, 1])
        x_hi = sb("x_hi", [P, T * P], F32R)
        x_lo = sb("x_lo", [P, T * P], F32R)
        h = probsT[:].rearrange("p i (j a) b -> p (i j) (a b)", j=2)
        h_hi = sb("h_hi", [P, H_BUFS, N], F32R)
        h_lo = sb("h_lo", [P, H_BUFS, N], F32R)
        yT = probs[:, 0, :, :].rearrange("p (i a) b -> p i (a b)", i=2)
        logitsT = k_heads[0:NR1, 0, :, :, :].rearrange("p b h s -> p (b h s)")
        gates = {n: sb(n, [P, T, NR1]) for n in ("g_shifted", "g_exp", "g_probs", "g_rank", "g_weights")}
        g_max = sb("g_max", [P, T])
        g_sum = sb("g_sum", [P, T])
        g_inv = sb("g_inv", [P, T])
        g_above, g_equal, g_tied, g_before = (
            shifted[:, i * H // 4:(i + 1) * H // 4, :].rearrange("p a (b e j) -> p (a b) e j", e=NE, j=NE)
            for i in range(4))

        ps_scores = bank("ps_scores", 2)
        ps_probsT = bank("ps_probsT", 2)
        ps_qk = bank("ps_qk")
        ps_tr = bank("ps_tr")
        ps_vo = bank("ps_vo")
        ps_y = bank("ps_y")
        scores0, scores1 = ps_scores[:, 0:512], ps_scores[:, 512:1024]
        h_bank = [ps_probsT[:, 0:512], ps_probsT[:, 512:1024], ps_qk[:]]
        y_bank = [ps_tr[:], scores1, ps_y[:]]
        t_bank = [ps_vo[:], scores0]

        def names(*which):
            return [sem(f"s_{n}") for n in which]

        s_pa, s_pb, s_x_in, s_mask_in, s_out = names("pa", "pb", "x_in", "mask_in", "out")
        s_w_in, s_x_stage, s_kv_stage = ([sem(f"s_{n}{i}") for i in range(2)] for n in ("w_in", "x_stage", "kv_stage"))
        s_bias_mm, s_bo_mm, s_bo, s_bo_D_mm, s_bo_D, s_half, s_ones, s_zeros, s_rel_hi, s_rel_bias = names(
            "bias_mm", "bo_mm", "bo", "bo_D_mm", "bo_D", "half", "ones", "zeros", "rel_hi", "rel_bias")
        s_w_hi, s_w_split, s_lin_proj, s_lin_q, s_lin_kv, s_lin_exp, s_lin_phi = names(
            "w_hi", "w_split", "lin_proj", "lin_q", "lin_kv", "lin_exp", "lin_phi")
        s_lin_state, s_lin_masked, s_lin_out, s_lin_den, s_lin_inv, s_lin_norm, s_lin_res = names(
            "lin_state", "lin_masked", "lin_out", "lin_den", "lin_inv", "lin_norm", "lin_res")
        s_qk_mm, s_qk, s_rope_mul, s_rope, s_k_heads, s_v_mm, s_v_heads = names(
            "qk_mm", "qk", "rope_mul", "rope", "k_heads", "v_mm", "v_heads")
        s_scores, s_max, s_shifted, s_exp, s_sum_inv = names("scores", "max", "shifted", "exp", "sum_inv")
        s_probsT_mm, s_probsT, s_attn_mm, s_attnT, s_proj, s_res = names(
            "probsT_mm", "probsT", "attn_mm", "attnT", "proj", "res")
        s_stats, s_mean, s_var, s_rstd, s_x, s_keep, s_xT_mm, s_xT = names(
            "stats", "mean", "var", "rstd", "x", "keep", "xT_mm", "xT")
        s_x_hi, s_x_lo, s_mm1, s_h, s_mm2, s_h_lo_even, s_h_lo_odd = names(
            "x_hi", "x_lo", "mm1", "h", "mm2", "h_lo_even", "h_lo_odd")
        s_h_hi = names("h_hi_even", "h_hi_odd")
        s_yT, s_y_mm, s_mix = names("yT", "y_mm", "mix")
        s_gate_mm, s_gate_row, s_gate_tr, s_gate, s_gate_exp = names(
            "gate_mm", "gate_row", "gate_tr", "gate", "gate_exp")

        def A(name, rows=P):
            return pa[0:rows, PACK_A[name]]

        def W(name, rows=P):
            return pb[0:rows, PACK_B[name]]

        def weight(lay, name):
            name = f"{lay.name}_{name}"
            return A(name) if name in PACK_A else W(name)

        def tile(a, t, tiles=1):
            return a[:, bass.ds(t * P * tiles, P * tiles)]

        def landed(t, p):
            return 8 * (t - p) + 16

        ident = A("ident")
        GATE_STEPS = [11, 5]
        lin = None
        layer_B = Layer("B", 0, 1, False, True, False, HD ** -0.5)
        layer_D = Layer("D", 1, 3, True, True, True, HD ** -0.5)
        layer_E = Layer("E", 2, 4, False, False, False, 1.0)
        ffn_C = Ffn(0, 2, [[0, 1], [2], [3], [4], [5]], "C", NE, ACT.Relu, 0, 0, 3)
        ffn_F = Ffn(1, 5, [[6]], "F", NR1, ACT.Gelu, NCH * ffn_C.nb, NCH * ffn_C.ng, 2)
        TURN, STATS, NORM, TURN_X = LAG + 1, LAG + 2, LAG + 3, LAG + 8

        block = ctx.enter_context(nc.Block())

        @block.sync
        def _(sp):
            def load_pair(t, p):
                after(sp, s_lin_proj, t - 1)
                sp.dma_start(x_stage[:, p, :], tile(xT_in, t, 2)).then_inc(s_x_stage[p], 16)

            def load_weights(t, p):
                after(sp, s_w_split, t - 1)
                sp.dma_start(w_raw[:, p, :], w_experts[:, bass.ds(t * W_CHUNK, W_CHUNK)]).then_inc(s_w_in[p], 16)

            sp.dma_start(pa[:], pack_a).then_inc(s_pa, 16)
            load_pair(0, 0)
            load_pair(1, 1)
            sp.dma_start(x_nat[:], x.rearrange("(t p) d -> p t d", p=P)).then_inc(s_x_in, 16)
            load_weights(0, 0)
            load_weights(1, 1)
            sp.dma_start(pb[:], pack_b).then_inc(s_pb, 16)
            sp.dma_start(mask_in, key_mask).then_inc(s_mask_in, 16)
            for t in range(2, PAIRS):
                load_pair(t, t % 2)
                load_weights(t, t % 2)
            for c in range(NCH):
                sp.wait_ge(s_x, ffn_F.w(c) + CH)
                sp.dma_start(out.rearrange("(t p) d -> p t d", p=P)[:, c * CH:(c + 1) * CH, :],
                             x_nat[:, c * CH:(c + 1) * CH, :]).then_inc(s_out, 16)
            sp.wait_ge(s_out, 16 * NCH)

        @block.tensor
        def _(pe):
            def prepare_B():
                pe.matmul(ps_y[:, 0:D], A("B_bv").broadcast_to([P, P]), A("B_wo"), start=True, stop=True)\
                  .then_inc(s_bo_mm, 1)
                pe.wait_ge(s_bo, 1)

            def prepare_DE():
                pe.wait_ge(s_pb, 16)
                pe.matmul(ps_probsT[:, 0:D], W("D_bv").broadcast_to([P, P]), W("D_wo"), start=True, stop=True)\
                  .then_inc(s_bo_D_mm, 1)
                pe.wait_ge(s_lin_masked, PAIRS)
                for k in range(0, S, KEYS):
                    for b in range(BT):
                        mm = pe.matmul(ps_scores[b * S:(b + 1) * S, k * H:(k + KEYS) * H],
                                       W("buckets")[:, S - 1 - k:2 * S - 1 - k], W("rel_bias"),
                                       start=True, stop=True)
                mm.then_inc(s_bias_mm, 1)

            def lin_proj(_, t, p):
                pe.wait_ge(s_x_stage[p], landed(t, p))
                after(pe, s_lin_q, t)
                pe.matmul(ps_qk[:, 0:2 * P], A("wq_lin"), x_stage[:, p, :], start=True, stop=True)
                after(pe, s_lin_kv, t)
                for i in range(2):
                    mm = pe.matmul(ps_vo[:, i * 2 * D:(i + 1) * 2 * D], x_stage[:, p, i * P:(i + 1) * P],
                                   A("wkv_lin"), start=True, stop=True)
                mm.then_inc(s_lin_proj, 1)

            def lin_state(_, t, p):
                pe.wait_ge(s_lin_phi, t + 1)
                after(pe, s_lin_masked, t)
                for i in range(2):
                    for b in range(BT):
                        rows = slice(b * S, (b + 1) * S)
                        mm = pe.matmul(ps_scores[:, b * 512 + i * (D + 1):b * 512 + (i + 1) * (D + 1)],
                                       phi[rows, p, (2 + i) * P:(3 + i) * P], v_ones[rows, p, i, :],
                                       start=True, stop=True)
                mm.then_inc(s_lin_state, 1)

            def lin_out(_, t, p):
                pe.wait_ge(s_lin_masked, t + 1)
                after(pe, s_lin_norm, t)
                for i in range(2):
                    for b in range(BT):
                        mm = pe.matmul(ps_y[b * S:(b + 1) * S, i * (D + H):(i + 1) * (D + H)],
                                       phi[:, p, i * P + b * S:i * P + (b + 1) * S], kv_masked[:, p, i, b, :],
                                       start=True, stop=True)
                mm.then_inc(s_lin_out, 1)

            def lin_turn(_, t, p):
                pe.wait_ge(s_x, 2 * t + 2)
                after(pe, s_xT, 2 * t)
                for i in range(2):
                    mm = pe.transpose(ps_tr[:, i * P:(i + 1) * P], x_new[:, 2 * p + i, :], ident)
                mm.then_inc(s_xT_mm, 2)

            def project_qk(lay, t, p):
                u = lay.u(t)
                if lay is layer_B:
                    pe.wait_ge(s_lin_q, PAIRS)
                if lay is layer_D:
                    pe.wait_ge(s_h, NCH * ffn_C.nb)
                after(pe, s_qk, u)
                pe.wait_ge(s_kv_stage[p], landed(u, p))
                pe.wait_ge(s_xT, lay.w(t) - (T - 1))
                tokens = kv_stage[:, p, :]

                def project(name, i, source):
                    return pe.matmul(ps_qk[:, i * P:(i + 1) * P], weight(lay, name), source, start=True, stop=True)

                mm = project("wq", 0, tile(xT, t))
                mm = project("wk", 1, tokens)
                if lay.rope:
                    project("wq_turned", 2, tile(xT, t))
                    mm = project("wk_turned", 3, tokens)
                mm.then_inc(s_qk_mm, 1)

            def project_v(lay, t, p):
                if lay is layer_B and isinstance(t, int) and t < 5:
                    pe.wait_ge(s_xT, T)
                elif lay is layer_D and isinstance(t, int) and t < 5:
                    pe.wait_ge(s_yT, NCH * ffn_C.ng)
                else:
                    pe.wait_ge(s_xT, lay.w(t) - 4)
                after(pe, s_v_heads, lay.u(t))
                for b in range(BT):
                    for odd in range(2):
                        mm = pe.matmul(ps_tr[odd * S:(odd + 1) * S, b * D // 2:(b + 1) * D // 2],
                                       kv_stage[:, p, b * S:(b + 1) * S],
                                       weight(lay, "wv_parity")[:, odd * D // 2:(odd + 1) * D // 2], start=True, stop=True)
                mm.then_inc(s_v_mm, 1)

            def project_out(lay, t, p):
                u = lay.u(t)
                pe.wait_ge(s_attnT, u + 1)
                if lay is layer_B:
                    pe.wait_ge(s_lin_norm, PAIRS)
                after(pe, s_res, u)
                pe.matmul(ps_y[:, 0:D], attnT[:, p, :], weight(lay, "wo"), start=True, stop=True)\
                  .then_inc(s_proj, 1)

            def scores(lay, t, p):
                u = lay.u(t)
                if lay is layer_B:
                    pe.wait_ge(s_rel_bias, 1)
                if lay is layer_D:
                    pe.wait_ge(s_yT, NCH * ffn_C.ng)
                pe.wait_ge(s_k_heads, u + 1)
                after(pe, s_shifted, u)
                for half in range(2):
                    cols = slice(half * 512, (half + 1) * 512)
                    whole = ps_scores[:, cols].rearrange("p (h k) -> p h k", k=S)
                    some = slice(half * H // 2, (half + 1) * H // 2)
                    if lay.causal:
                        pe.matmul(whole, id16[:], causal[:].unsqueeze(1).broadcast_to([P, H // 2, S]),
                                  start=True, stop=False, skip_group_check=True)
                    else:
                        pe.matmul(whole, select[:], key_neg[:, t, :].unsqueeze(1).broadcast_to([BT, H // 2, S]),
                                  start=True, stop=False, skip_group_check=True)
                        for part in (rel_hi, rel_lo):
                            pe.matmul(ps_scores[:, cols], ident_r[:], part[:, some, :],
                                      start=False, stop=False, skip_group_check=True)
                    for b in range(BT):
                        mm = pe.matmul(ps_scores[b * S:(b + 1) * S, cols], qk[:, p, b * S:(b + 1) * S],
                                       k_heads[:, p, b, some, :], start=False, stop=True, skip_group_check=True)
                mm.then_inc(s_scores, 1)

            def turn_probs(lay, t, p):
                u = lay.u(t)
                pe.wait_ge(s_exp, u + 1)
                if lay is layer_B:
                    pe.wait_ge(s_bo_D, 1)
                for half in range(2):
                    after(pe, s_probsT, 2 * u - 1 + half)
                    for i in range(H // 4):
                        pair = 2 * i + half
                        mm = pe.transpose(ps_probsT[:, half * 512 + i * P:half * 512 + (i + 1) * P],
                                          probs[:, p, 2 * pair:2 * pair + 2, :], ident)
                    mm.then_inc(s_probsT_mm, 1)

            def attend(lay, t, p):
                u = lay.u(t)
                pe.wait_ge(s_v_heads, u + 1)
                if lay is layer_B:
                    pe.wait_ge(s_lin_kv, PAIRS)
                if lay is layer_D:
                    pe.wait_ge(s_mix, NCH * ffn_C.ng)
                after(pe, s_attnT, u)
                for odd in range(2):
                    pe.wait_ge(s_probsT, 2 * u + 1 + odd)
                    for b in range(BT):
                        for strip in range(4):
                            rows = slice(32 * strip, 32 * strip + 32)
                            pe.matmul(ps_vo[rows, 2 * D + b * S:2 * D + (b + 1) * S], v_heads[:, p, b, odd, rows],
                                      probsT[:, p, odd * H // 4 + strip, b * S:(b + 1) * S],
                                      start=(odd == 0 and b == 0), stop=(odd == 1), skip_group_check=True)
                    for strip in range(4):
                        rows = slice(32 * strip, 32 * strip + 32)
                        mm = pe.matmul(ps_vo[rows, 3 * D:4 * D], W("value_mask")[:, odd * D:odd * D + 32],
                                       probsT[:, p, odd * H // 4 + strip, :],
                                       start=False, stop=(odd == 1), skip_group_check=True)
                mm.then_inc(s_attn_mm, 1)

            def turn_x(lay, t, p):
                w = lay.w(t)
                pe.wait_ge(s_x, w + 1)
                pe.wait_ge(s_xT, w)
                some = min(t + 5, T) if isinstance(t, int) and lay is not layer_D else t + 5
                pe.wait_ge(s_v_heads, lay.u(some))
                pe.transpose(ps_tr[:, D:D + P], x_new[:, p, :], ident).then_inc(s_xT_mm, 1)

            def gate(ffn, c, bank):
                pe.wait_ge(s_xT, ffn.w(c) - T + CH)
                pe.matmul(bank[0:ffn.experts, :], W(ffn.gate), xT[:, c * N:(c + 1) * N], start=True, stop=True)\
                  .then_inc(s_gate_mm, 1)

            def open_feed_forward(ffn):
                pe.wait_ge(s_probsT, 2 * (T if ffn.f == 0 else 3 * T))
                pe.wait_ge(s_qk, T if ffn.f == 0 else 3 * T)
                for c in range(NCH - 1):
                    gate(ffn, c, (ps_probsT[:, 0:512], ps_probsT[:, 512:1024], ps_qk)[c])

            def turn_gate(ffn):
                n = ffn.experts
                pe.wait_ge(s_gate_row, (ffn.f + 1) * NCH)
                for t in range(T):
                    mm = pe.transpose(ps_y[:, t * n:(t + 1) * n], logitsT[0:n, t * P:(t + 1) * P], ident[0:n, 0:n])
                mm.then_inc(s_gate_tr, 1)

            def feed_forward(ffn, before={}):
                pe.wait_ge(s_w_split, PAIRS)
                pe.wait_ge(s_gate_row, (ffn.f + 1) * NCH - 1)

                def slot(at):
                    if (now := at(0)) is not None:
                        c, j = now
                        g, e, i = ffn.blocks[j]
                        pe.wait_ge(s_x_lo, c + (ffn.f * NCH + 1))
                        after(pe, s_h, ffn.block(c, j) - ffn.h_banks)
                        for n, (w, v) in enumerate(((w_hi, x_hi), (w_hi, x_lo), (w_lo, x_hi))):
                            mm = pe.matmul(h_bank[j % ffn.h_banks], w[:, w1_block(e, i)], v[:, bass.ds(c * N, N)],
                                           start=(n == 0), stop=(n == 2))
                        mm.then_inc(s_mm1, 1)
                        if ffn.number(c, j) == 2:
                            pe.wait_ge(s_res, T if ffn.f == 0 else 3 * T)
                            gate(ffn, NCH - 1, ps_y)
                        if ffn.number(c, j) == 3:
                            turn_gate(ffn)
                    if (then := at(LAG)) is not None:
                        c, j = then
                        g, e, i = ffn.blocks[j]
                        pe.wait_ge(s_h_lo_odd if j % 2 else s_h_lo_even, ffn.half(c, j))
                        pe.wait_ge(s_h_hi[j % 2], ffn.half(c, j))
                        if j in ffn.first:
                            after(pe, s_yT, ffn.group(c, g) - min(2, ffn.ng))
                            if ffn.y_bank(g) == 2:
                                pe.wait_ge(s_xT, ffn.w(c))
                                if isinstance(c, int) and c == 0:
                                    pe.wait_ge(s_gate, 2)
                            if isinstance(c, int) and c == 0:
                                pe.wait_ge(s_xT, ffn.n * T)
                                pe.wait_ge(s_shifted, T if ffn.f == 0 else 3 * T)
                        for n, (w, v) in enumerate(((w_hi, h_hi), (w_hi, h_lo), (w_lo, h_hi))):
                            mm = pe.matmul(y_bank[ffn.y_bank(g)], w[:, w2_block(e, i)], v[:, j % H_BUFS, :],
                                           start=(j in ffn.first and n == 0), stop=(j in ffn.last and n == 2))
                        mm.then_inc(s_mm2, 1)
                    if (then := at(TURN)) is not None and then[1] in ffn.last:
                        c, g = then[0], ffn.last[then[1]]
                        pe.wait_ge(s_yT, ffn.group(c, g))
                        after(pe, s_mix, ffn.group_before(c, g))
                        if isinstance(c, int) and c == 0:
                            pe.wait_ge(s_attnT, T if ffn.f == 0 else 3 * T)
                            pe.wait_ge(s_shifted, T if ffn.f == 0 else 3 * T)
                        for t in range(CH):
                            mm = pe.transpose(t_bank[g % 2][:, t * P:(t + 1) * P],
                                              yT[:, g % 2, t * P:(t + 1) * P], ident)
                        mm.then_inc(s_y_mm, 1)
                    if ffn.f == 0 and (then := at(TURN_X)) is not None and then[1] == ffn.nb - 1:
                        c = then[0]
                        pe.wait_ge(s_x, ffn.w(c) + CH)
                        pe.wait_ge(s_yT, ffn.group(c, ffn.ng - 1))
                        for t in range(CH):
                            mm = pe.transpose(ps_y[:, t * P:(t + 1) * P], x_new[:, t, :], ident)
                        mm.then_inc(s_xT_mm, CH)
                ffn.chunks(pe, slot, before)

            pe.wait_ge(s_pa, 16)
            linear = [(2, lin_out), (3, lin_turn), (0, lin_proj), (1, lin_state)]
            open_sweep(lin, 1, linear)
            prepare_B()
            sweep(pe, [lin], PAIRS, 3, linear, opened=1, before={PAIRS + 2: prepare_DE})
            project_qk(layer_B, 0, 0)
            project_v(layer_B, 0, 0)
            attention = [(1, project_qk), (2, scores), (6, turn_x), (3, turn_probs), (1, project_v),
                         (4, project_out), (3, attend)]
            sweep(pe, [layer_B], T, 6, attention, opened=2, before={T + 4: lambda: open_feed_forward(ffn_C)})
            feed_forward(ffn_C, {LAG: lambda: open_sweep(layer_D, 2, attention)})
            sweep(pe, [layer_D, layer_E], T, 6, attention, opened=2, before={T + 4: lambda: open_feed_forward(ffn_F)})
            feed_forward(ffn_F)

        @block.scalar
        def _(act):
            def lin_q(_, t, p):
                act.wait_ge(s_lin_proj, t + 1)
                act.activation(z[:, p, 0:2 * P], ps_qk[:, 0:2 * P], ACT.Identity, bias=A("bq_lin"))\
                   .then_inc(s_lin_q, 1)

            def lin_exp(_, t, p):
                act.wait_ge(s_lin_q, t + 1)
                act.wait_ge(s_lin_kv, t + 1)
                after(act, s_lin_phi, t - 1)
                act.activation(r_z[:, p, :], z[:, p, :], ACT.Relu)
                act.activation(e_z[:, p, :], z[:, p, :], ACT.Exp).then_inc(s_lin_exp, 1)

            def round_weights(_, t, p):
                act.wait_ge(s_w_in[p], landed(t, p))
                act.copy(w_hi[:, bass.ds(t * W_CHUNK, W_CHUNK)], w_raw[:, p, :]).then_inc(s_w_hi, 1)

            def lin_turn(_, t, p):
                act.wait_ge(s_xT_mm, 2 * t + 2)
                act.copy(tile(xT, t, 2), ps_tr[:, 0:2 * P]).then_inc(s_xT, 2)

            def load_tokens(lay, t, p):
                if lay.own:
                    act.wait_ge(s_xT, lay.w(t) - (T - 1))
                after(act, s_v_mm, lay.u(t) - 1)
                source = xT if lay.own else ctxT_in
                act.dma_start(kv_stage[:, p, :], tile(source, t)).then_inc(s_kv_stage[p], 16)

            def take_qk(lay, t, p):
                u = lay.u(t)
                if lay is layer_B:
                    act.wait_ge(s_pb, 16)
                act.wait_ge(s_qk_mm, u + 1)
                if lay.rope:
                    after(act, s_rope_mul, t - 1)
                    for i, b in enumerate(("bq", "bk", "bq_turned", "bk_turned")):
                        last = act.activation(qk_raw[:, p, i * P:(i + 1) * P], ps_qk[:, i * P:(i + 1) * P],
                                              ACT.Identity, bias=weight(lay, b))
                else:
                    after(act, s_scores, u - 1)
                    after(act, s_k_heads, u - 1)
                    if lay.bias:
                        act.activation(qk[:, p, 0:P], ps_qk[:, 0:P], ACT.Identity, bias=weight(lay, "bq"))
                        last = act.activation(qk[:, p, P:2 * P], ps_qk[:, P:2 * P], ACT.Identity,
                                              bias=weight(lay, "bk"))
                    else:
                        last = act.copy(qk[:, p, :], ps_qk[:, 0:2 * P])
                last.then_inc(s_qk, 1)

            def take_v(lay, t, p):
                u = lay.u(t)
                act.wait_ge(s_v_mm, u + 1)
                after(act, s_attn_mm, u - 1)
                if lay is layer_B:
                    act.wait_ge(s_zeros, 1)
                for half in range(2):
                    rows = slice(half * S, (half + 1) * S)
                    src = ps_tr[rows, 0:D].rearrange("p (b g o m) -> p b g o m", b=BT, o=2, m=HD)
                    dst = v_heads[rows, p, :, :, :].rearrange("p b c (g o h m) -> p b c g o h m", o=2, h=2, m=HD)
                    for odd in range(2):
                        last = act.copy(dst[:, :, odd, :, odd, half, :], src[:, :, :, odd, :])
                last.then_inc(s_v_heads, 1)

            def keep_x(lay, t, p):
                act.wait_ge(s_x, lay.w(t) + 1)
                act.copy(x_nat[:, t, :], x_new[:, p, :]).then_inc(s_keep, 1)

            def take_probsT(lay, t, p):
                u = lay.u(t)
                after(act, s_attn_mm, u - 1)
                for half in range(2):
                    act.wait_ge(s_probsT_mm, 2 * u + 1 + half)
                    act.copy(probsT[:, p, half * H // 4:(half + 1) * H // 4, :],
                             ps_probsT[:, half * 512:(half + 1) * 512]).then_inc(s_probsT, 1)

            def exponentiate(lay, t, p):
                u = lay.u(t)
                act.wait_ge(s_shifted, u + 1)
                after(act, s_probsT_mm, 2 * u - 2)
                act.activation(probs[:, p, :, :], shifted[:], ACT.Exp, scale=lay.scale).then_inc(s_exp, 1)

            def take_xT(lay, t, p):
                act.wait_ge(s_xT_mm, lay.w(t) + 1)
                act.copy(tile(xT, t), ps_tr[:, D:D + P]).then_inc(s_xT, 1)

            def gate_row(ffn, c, bank):
                act.wait_ge(s_gate_mm, ffn.f * NCH + c + 1)
                n = ffn.experts
                dst = logitsT[0:n, c * N:(c + 1) * N]
                if ffn.f == 0:
                    last = act.activation(dst, bank[0:n, :], ACT.Identity, bias=W("C_gate_bias", n))
                else:
                    last = act.copy(dst, bank[0:n, :])
                last.then_inc(s_gate_row, 1)

            def exponentiate_gate(ffn):
                n = ffn.experts
                act.wait_ge(s_gate, GATE_STEPS[0] * ffn.f + 2)
                act.activation(gates["g_exp"][:, :, 0:n], gates["g_shifted"][:, :, 0:n], ACT.Exp)\
                   .then_inc(s_gate_exp, 1)

            def open_feed_forward(ffn):
                for c in range(NCH - 1):
                    gate_row(ffn, c, (ps_probsT[:, 0:512], ps_probsT[:, 512:1024], ps_qk)[c])
                round_x(ffn, 0)

            def round_x(ffn, c):
                act.wait_ge(s_xT, ffn.w(c) - T + CH)
                act.copy(x_hi[:, c * N:(c + 1) * N], xT[:, c * N:(c + 1) * N]).then_inc(s_x_hi, 1)

            def feed_forward(ffn, before={}):
                act.wait_ge(s_attn_mm, T if ffn.f == 0 else 3 * T)

                def slot(at):
                    if (now := at(0)) is not None:
                        c, j = now
                        act.wait_ge(s_mm1, ffn.block(c, j))
                        after(act, s_h_hi[j % 2], ffn.half(c, j) - H_BUFS // 2)
                        after(act, s_h_lo_odd if j % 2 else s_h_lo_even, ffn.half(c, j) - H_BUFS // 2)
                        act.activation(h[:, j % H_BUFS, :], h_bank[j % ffn.h_banks], ffn.func,
                                       bias=W(ffn.b1)[:, j:j + 1]).then_inc(s_h, 1)
                        if ffn.f and j % 2:
                            act.wait_ge(s_h, ffn.block(c, j))
                            after(act, s_mm2, ffn.block(c, j) - H_BUFS)
                            act.copy(h_hi[:, j % H_BUFS, :], h[:, j % H_BUFS, :]).then_inc(s_h_hi[1], 1)
                        if ffn.number(c, j) == 2:
                            gate_row(ffn, NCH - 1, ps_y)
                        if ffn.number(c, j) in (1, 3, 4):
                            round_x(ffn, {1: 1, 3: 2, 4: 3}[ffn.number(c, j)])
                        if ffn.number(c, j) == 5:
                            exponentiate_gate(ffn)
                    if (then := at(LAG)) is not None and then[1] in ffn.last:
                        c, g = then[0], ffn.last[then[1]]
                        act.wait_ge(s_mm2, ffn.block(*then))
                        after(act, s_y_mm, ffn.group_before(c, g))
                        if ffn.f == 0 and g == 0:
                            last = act.activation(yT[:, 0, :], y_bank[0], ACT.Identity, bias=b2_shared[:],
                                                  scale=1.0 / NS)
                        else:
                            col = g + 1 if ffn.f == 0 else 0
                            last = act.activation(yT[:, g % 2, :], y_bank[ffn.y_bank(g)], ACT.Identity,
                                                  bias=W(ffn.b2)[:, col:col + 1])
                        last.then_inc(s_yT, 1)
                    if ffn.f == 0 and (then := at(TURN_X)) is not None and then[1] == ffn.nb - 1:
                        c = then[0]
                        act.wait_ge(s_xT_mm, ffn.w(c) + CH)
                        act.copy(xT[:, bass.ds(c * N, N)], ps_y[:]).then_inc(s_xT, CH)
                ffn.chunks(act, slot, before)

            act.wait_ge(s_half, 1)
            act.activation(table_warm[:], minus_half[:], ACT.Exp)
            act.wait_ge(s_pa, 16)
            attention = [(1, take_qk), (2, take_v), (0, load_tokens), (6, take_xT), (3, take_probsT),
                         (2, exponentiate), (6, keep_x)]
            sweep(act, [lin], PAIRS, 3, [(3, lin_turn), (0, lin_q), (0, lin_exp), (0, round_weights)],
                  before={PAIRS: lambda: load_tokens(layer_B, 0, 0), PAIRS + 2: lambda: take_qk(layer_B, 0, 0)})
            load_tokens(layer_B, 1, 1)
            sweep(act, [layer_B], T, 6, attention, opened=2, before={T + 4: lambda: open_feed_forward(ffn_C)})
            feed_forward(ffn_C, {LAG: lambda: open_sweep(layer_D, 2, attention)})
            sweep(act, [layer_D, layer_E], T, 6, attention, opened=2, before={T + 4: lambda: open_feed_forward(ffn_F)})
            feed_forward(ffn_F)

        @block.vector
        def _(dve):
            def norm_statistics(i):
                dve.bn_stats(stats[:, i, :], y[:, i, :]).then_inc(s_stats, 1)

            def norm_variance(first, w, tiles=1):
                for i in range(first, first + tiles):
                    last = dve.bn_aggr(mean_var[:, i, :], stats[:, i, :])
                last.then_inc(s_mean, tiles)
                dve.wait_ge(s_mean, w + tiles)
                some = slice(first, first + tiles)
                dve.tensor_scalar(var_eps[:, some, :], mean_var[:, some, 1:2], EPS, None, ALU.add)\
                   .then_inc(s_var, tiles)

            def norm_apply(i, w, buffers, dst=None):
                dve.wait_ge(s_rstd, w + 1)
                if dst is None:
                    after(dve, s_xT_mm, w - (buffers - 1))
                    after(dve, s_keep, w - (buffers - 1))
                    dst = x_new[:, i, :]
                dve.tensor_scalar(dst, y[:, i, :], mean_var[:, i, 0:1], rstd[:, i, :], ALU.subtract, ALU.mult)\
                   .then_inc(s_x, 1)

            def prepare_B():
                dve.memset(v_ones[:, :, :, D:D + 1], 1.0).then_inc(s_ones, 1)
                dve.wait_ge(s_bo_mm, 1)
                dve.tensor_tensor(bo_B[:], ps_y[:, 0:D], A("B_bo"), ALU.add).then_inc(s_bo, 1)

            def prepare_DE():
                dve.wait_ge(s_pb, 16)
                dve.tensor_copy(id16[:], ident)
                dve.tensor_copy(ident_r[:], ident)
                dve.tensor_copy(causal[:], W("causal"))
                dve.tensor_copy(select[:], W("select", BT))
                dve.tensor_tensor(b2_shared[:], W("C_b2")[:, 0:1], W("C_b2")[:, 1:2], ALU.add).then_inc(s_ones, 1)
                dve.wait_ge(s_mask_in, 16)
                dve.tensor_scalar(key_neg[:], mask_in, -NEG, NEG, ALU.mult, ALU.add)
                dve.wait_ge(s_ones, 2)
                dve.tensor_scalar(b2_shared[:], b2_shared[:], 1.0 / NS, None, ALU.mult)
                dve.wait_ge(s_bo_D_mm, 1)
                dve.tensor_tensor(bo_D[:], ps_probsT[:, 0:D], W("D_bo"), ALU.add).then_inc(s_bo_D, 1)

            def split_bias():
                dve.wait_ge(s_bias_mm, 1)
                bias = ps_scores[:].rearrange("p (k h) -> p k h", h=H)
                upper, lower = (r[:].rearrange("p h k -> p k h") for r in (rel_hi, rel_lo))
                dve.tensor_copy(upper, bias).then_inc(s_rel_hi, 1)
                dve.wait_ge(s_rel_hi, 1)
                dve.tensor_tensor(lower, bias, upper.bitcast(F32), ALU.subtract).then_inc(s_rel_bias, 1)

            def lin_kv(_, t, p):
                dve.wait_ge(s_lin_proj, t + 1)
                after(dve, s_lin_exp, t - 1)
                after(dve, s_lin_state, t - 1)
                both = ps_vo[:].rearrange("p (i c) -> p i c", i=2)
                bias = A("bkv_lin").rearrange("p (i d) -> p i d", i=2)
                dve.tensor_tensor(z[:, p, 2 * P:4 * P].rearrange("p (i d) -> p i d", i=2), both[:, :, 0:D],
                                  bias[:, 0:1, :].broadcast_to([P, 2, D]), ALU.add)
                dve.tensor_tensor(v_ones[:, p, :, 0:D], both[:, :, D:2 * D],
                                  bias[:, 1:2, :].broadcast_to([P, 2, D]), ALU.add).then_inc(s_lin_kv, 1)

            def lin_masked(_, t, p):
                dve.wait_ge(s_lin_state, t + 1)
                after(dve, s_lin_out, t - 1)
                for b in range(BT):
                    state = ps_scores[:, b * 512:b * 512 + 2 * (D + 1)].rearrange("p (i c) -> p i c", i=2)
                    dve.tensor_tensor(kv_masked[:, p, :, b, 0:D], state[:, :, 0:D],
                                      A("block_mask").unsqueeze(1).broadcast_to([P, 2, D]), ALU.mult)
                    last = dve.tensor_tensor(kv_masked[:, p, :, b, D:D + H],
                                             state[:, :, D:D + 1].broadcast_to([P, 2, H]),
                                             A("head_mask").unsqueeze(1).broadcast_to([P, 2, H]), ALU.mult)
                last.then_inc(s_lin_masked, 1)

            def lin_out(_, t, p):
                dve.wait_ge(s_lin_out, t + 1)
                both = ps_y[:, 0:2 * (D + H)].rearrange("p (i c) -> p i c", i=2)
                dve.tensor_scalar(den[:], both[:, :, D:D + H], 1e-6, None, ALU.add).then_inc(s_lin_den, 1)
                dve.wait_ge(s_lin_den, t + 1)
                dve.reciprocal(den_inv[:], den[:]).then_inc(s_lin_inv, 1)
                dve.wait_ge(s_lin_inv, t + 1)
                dve.tensor_tensor(o_lin[:].rearrange("p i (h m) -> p i h m", h=H),
                                  both[:, :, 0:D].rearrange("p i (h m) -> p i h m", h=H),
                                  den_inv[:].unsqueeze(3).broadcast_to([P, 2, H, HD]), ALU.mult)\
                   .then_inc(s_lin_norm, 1)
                dve.wait_ge(s_lin_norm, t + 1)
                dve.tensor_tensor(y[:, 2 * p:2 * p + 2, :], o_lin[:], x_nat[:, bass.ds(2 * t, 2), :], ALU.add)\
                   .then_inc(s_lin_res, 1)
                dve.wait_ge(s_lin_res, t + 1)
                norm_statistics(2 * p)
                norm_statistics(2 * p + 1)
                dve.wait_ge(s_stats, 2 * t + 2)

            def lin_phi(_, t, p):
                dve.wait_ge(s_lin_exp, t + 1)
                after(dve, s_lin_out, t - 1)
                dve.scalar_tensor_tensor(phi[:, p, :], e_z[:, p, :], 1.0, r_z[:, p, :], ALU.min, ALU.add)\
                   .then_inc(s_lin_phi, 1)

            def lin_norm_variance(_, t, p):
                norm_variance(2 * p, 2 * t, 2)

            def lin_norm_apply(_, t, p):
                for i in range(2):
                    norm_apply(2 * p + i, 2 * t + i, CH)

            def rotate(lay, t, p):
                if not lay.rope:
                    return
                dve.wait_ge(s_qk, lay.u(t) + 1)
                after(dve, s_rope, t)
                by = lambda name: W(name).unsqueeze(1).broadcast_to([P, 2 * BT, S])
                parts = qk_raw[:, p, :].rearrange("p (i s) -> p i s", s=S)
                dve.tensor_tensor(straight[:].rearrange("p (i s) -> p i s", s=S), parts[:, 0:2 * BT, :],
                                  by("cos"), ALU.mult)
                dve.tensor_tensor(turned[:].rearrange("p (i s) -> p i s", s=S), parts[:, 2 * BT:4 * BT, :],
                                  by("sin"), ALU.mult).then_inc(s_rope_mul, 1)
                dve.wait_ge(s_rope_mul, t + 1)
                after(dve, s_scores, lay.u(t) - 1)
                after(dve, s_k_heads, lay.u(t) - 1)
                dve.tensor_tensor(qk[:, p, :], straight[:], turned[:], ALU.add).then_inc(s_rope, 1)

            def invert_sums(lay, t, p):
                dve.wait_ge(s_attn_mm, lay.u(t) + 1)
                dve.reciprocal(sum_inv[:], ps_vo[:, 3 * D:4 * D]).then_inc(s_sum_inv, 1)

            def normalize_heads(lay, t, p):
                u = lay.u(t)
                dve.wait_ge(s_sum_inv, u + 1)
                after(dve, s_proj, u - 1)
                dve.tensor_tensor(attnT[:, p, :], ps_vo[:, 2 * D:3 * D], sum_inv[:], ALU.mult)\
                   .then_inc(s_attnT, 1)

            def add_residual(lay, t, p):
                u = lay.u(t)
                dve.wait_ge(s_proj, u + 1)
                dve.wait_ge(s_keep, lay.w(t) - (T - 1))
                dve.tensor_tensor(y[:, p, :], ps_y[:, 0:D], x_nat[:, t, :], ALU.add).then_inc(s_res, 1)
                dve.wait_ge(s_res, u + 1)
                norm_statistics(p)

            def find_max(lay, t, p):
                u = lay.u(t)
                dve.wait_ge(s_scores, u + 1)
                dve.tensor_reduce(row_max[:], ps_scores[:].rearrange("p (h k) -> p h k", h=H), AX.X, ALU.max)\
                   .then_inc(s_max, 1)

            def shift(lay, t, p):
                u = lay.u(t)
                dve.wait_ge(s_max, u + 1)
                after(dve, s_exp, u)
                dve.tensor_tensor(shifted[:], ps_scores[:].rearrange("p (h k) -> p h k", h=H),
                                  row_max[:].unsqueeze(2).broadcast_to([P, H, S]), ALU.subtract)\
                   .then_inc(s_shifted, 1)

            def wait_statistics(lay, t, p):
                dve.wait_ge(s_stats, lay.w(t) + 1)

            def attention_variance(lay, t, p):
                norm_variance(p, lay.w(t))

            def attention_norm(lay, t, p):
                norm_apply(p, lay.w(t), 2)

            def gate_step(ffn, n):
                experts = ffn.experts
                g = {name: t[:, :, 0:experts] for name, t in gates.items()}
                over = lambda t: t[:].unsqueeze(2).broadcast_to([P, T, experts])
                logits = ps_y[:, 0:T * experts].rearrange("p (t e) -> p t e", e=experts)
                lower = W("lower").rearrange("p (e j) -> p e j", e=NE).unsqueeze(1).broadcast_to([P, T, NE, NE])
                by_e, by_j = (gates["g_probs"][:, :, 0:NE].unsqueeze(d).broadcast_to([P, T, NE, NE]) for d in (3, 2))
                steps = [
                    lambda: dve.tensor_reduce(g_max[:], logits, AX.X, ALU.max),
                    lambda: dve.tensor_tensor(g["g_shifted"], logits, over(g_max), ALU.subtract),
                    lambda: dve.tensor_reduce(g_sum[:], g["g_exp"], AX.X, ALU.add),
                    lambda: dve.reciprocal(g_inv[:], g_sum[:]),
                    lambda: dve.tensor_tensor(g["g_probs"], g["g_exp"], over(g_inv), ALU.mult),
                    lambda: dve.tensor_tensor(g_above, by_j, by_e, ALU.is_gt),
                    lambda: dve.tensor_tensor(g_equal, by_j, by_e, ALU.is_equal),
                    lambda: dve.tensor_tensor(g_tied, g_equal, lower, ALU.mult),
                    lambda: dve.tensor_tensor(g_before, g_above, g_tied, ALU.add),
                    lambda: dve.tensor_reduce(g["g_rank"], g_before, AX.X, ALU.add),
                    lambda: dve.scalar_tensor_tensor(g["g_weights"], g["g_rank"], 2.0, g["g_probs"], ALU.is_lt,
                                                     ALU.mult)]
                if n == 0:
                    dve.wait_ge(s_gate_tr, ffn.f + 1)
                if n == 2:
                    dve.wait_ge(s_gate_exp, ffn.f + 1)
                after(dve, s_gate, GATE_STEPS[0] * ffn.f + n)
                steps[n]().then_inc(s_gate, 1)

            def split_x(ffn, c):
                dve.wait_ge(s_x_hi, ffn.f * NCH + c + 1)
                cols = slice(c * N, (c + 1) * N)
                dve.tensor_tensor(x_lo[:, cols], xT[:, cols], x_hi[:, cols].bitcast(F32), ALU.subtract)\
                   .then_inc(s_x_lo, 1)

            def mix(ffn, c, g):
                dve.wait_ge(s_y_mm, ffn.group(c, g))
                after(dve, s_mix, ffn.group(c, g - 1))
                bank = t_bank[g % 2]
                if g == 0:
                    dve.wait_ge(s_keep, ffn.w(c) - (T - CH))
                    dve.wait_ge(s_x, ffn.w(c))
                if ffn.f == 0 and g == 0:
                    dve.tensor_tensor(y[:].rearrange("p t d -> p (t d)"), bank,
                                      x_nat[:, bass.ds(c * CH, CH), :].rearrange("p t d -> p (t d)"), ALU.add)\
                       .then_inc(s_mix, 1)
                    return
                e, weights = (g - 1, gates["g_weights"]) if ffn.f == 0 else (NR1 - 1, gates["g_probs"])
                if isinstance(c, int) and c == 0:
                    dve.wait_ge(s_gate, GATE_STEPS[0] * ffn.f + GATE_STEPS[ffn.f])
                for t in range(CH):
                    before = y[:, t, :] if ffn.f == 0 else x_nat[:, c * CH + t, :]
                    last = dve.scalar_tensor_tensor(y[:, t, :], bank[:, t * P:(t + 1) * P],
                                                    weights[:, c * CH + t, e:e + 1], before, ALU.mult, ALU.add)
                last.then_inc(s_mix, 1)

            def feed_forward(ffn, before={}):
                def slot(at):
                    if (now := at(0)) is not None:
                        c, j = now
                        if j % 2 == 0 or ffn.f == 0:
                            dve.wait_ge(s_h, ffn.block(c, j))
                            after(dve, s_mm2, ffn.block(c, j) - H_BUFS)
                            dve.tensor_copy(h_hi[:, j % H_BUFS, :], h[:, j % H_BUFS, :]).then_inc(s_h_hi[j % 2], 1)
                        if j % 2 == 0:
                            dve.wait_ge(s_h_hi[0], ffn.half(c, j))
                            dve.tensor_tensor(h_lo[:, j % H_BUFS, :], h[:, j % H_BUFS, :],
                                              h_hi[:, j % H_BUFS, :].bitcast(F32), ALU.subtract)\
                               .then_inc(s_h_lo_even, 1)
                        number = ffn.number(c, j)
                        if number in (1, 3, 5):
                            split_x(ffn, (number + 1) // 2)
                        if number is not None and 0 <= number - 4 <= GATE_STEPS[ffn.f] // 2:
                            for n in range(2 * (number - 4), min(2 * (number - 3), GATE_STEPS[ffn.f])):
                                gate_step(ffn, n)
                    if (then := at(TURN)) is not None and then[1] in ffn.last:
                        mix(ffn, then[0], ffn.last[then[1]])
                    if (then := at(STATS)) is not None and then[1] == ffn.nb - 1:
                        c = then[0]
                        dve.wait_ge(s_mix, ffn.group(c, ffn.ng - 1))
                        for t in range(CH):
                            norm_statistics(t)
                        dve.wait_ge(s_stats, ffn.w(c) + CH)
                    if (then := at(NORM)) is not None and then[1] == ffn.nb - 1:
                        norm_variance(0, ffn.w(then[0]), CH)
                    for behind, tiles in ((NORM + 2, (0, 1)), (NORM + 3, (2, 3))) if ffn.f == 0 else\
                            ((NORM + 1, range(CH)),):
                        if (then := at(behind)) is None or then[1] != ffn.nb - 1:
                            continue
                        c = then[0]
                        for t in tiles:
                            norm_apply(t, ffn.w(c) + t, CH, x_nat[:, c * CH + t, :] if ffn.f else None)
                ffn.chunks(dve, slot, before)

            dve.wait_ge(s_pa, 16)
            linear = [(1, lin_phi), (2, lin_out), (0, lin_kv), (2, lin_norm_variance), (1, lin_masked),
                      (2, lin_norm_apply)]
            open_sweep(lin, 1, linear)
            prepare_B()
            dve.wait_ge(s_x_in, 16)
            sweep(dve, [lin], PAIRS, 3, linear, opened=1, before={PAIRS + 2: prepare_DE})
            split_bias()
            attention = [(5, add_residual), (5, wait_statistics), (4, invert_sums), (5, attention_variance),
                         (4, normalize_heads), (1, rotate), (2, find_max), (2, shift), (5, attention_norm)]
            sweep(dve, [layer_B], T, 6, attention, opened=2, before={T + 5: lambda: split_x(ffn_C, 0)})
            feed_forward(ffn_C, {LAG + 3: lambda: open_sweep(layer_D, 2, attention)})
            sweep(dve, [layer_D, layer_E], T, 6, attention, opened=2, before={T + 5: lambda: split_x(ffn_F, 0)})
            feed_forward(ffn_F)

        @block.gpsimd
        def _(pool):
            def inverse_deviation(first, w, tiles=1):
                some = slice(first, first + tiles)
                pool.wait_ge(s_var, w + tiles)
                pool.tensor_tensor(rstd[:, some, 0], var_eps[:, some, 0],
                                   minus_half[:, 0:1].broadcast_to([P, tiles]), ALU.pow).then_inc(s_rstd, tiles)

            def keep(i, w, dst, bias):
                pool.wait_ge(s_x, w + 1)
                pool.tensor_tensor(dst, x_new[:, i, :], bias[:], ALU.add).then_inc(s_keep, 1)

            def split_weights(_, t, p):
                cols = bass.ds(t * W_CHUNK, W_CHUNK)
                pool.wait_ge(s_w_hi, t + 1)
                pool.tensor_tensor(w_lo[:, cols], w_raw[:, p, :], w_hi[:, cols].bitcast(F32), ALU.subtract)\
                    .then_inc(s_w_split, 1)

            def lin_deviation(_, t, p):
                inverse_deviation(2 * p, 2 * t, 2)

            def lin_keep(_, t, p):
                for i in range(2):
                    keep(2 * p + i, 2 * t + i, x_nat[:, 2 * t + i, :], bo_B)

            def k_to_heads(lay, t, p):
                pool.wait_ge(s_rope if lay.rope else s_qk, t + 1 if lay.rope else lay.u(t) + 1)
                after(pool, s_scores, lay.u(t) - 1)
                pool.tensor_tensor(
                    k_heads[:, p, :, :, :],
                    qk[:, p, P:2 * P].rearrange("p (b s) -> p b s", b=BT).unsqueeze(2).broadcast_to([P, BT, H, S]),
                    A("head_mask").unsqueeze(1).unsqueeze(3).broadcast_to([P, BT, H, S]), ALU.mult)\
                    .then_inc(s_k_heads, 1)

            def deviation(lay, t, p):
                inverse_deviation(p, lay.w(t))

            def feed_forward(ffn, before={}):
                def slot(at):
                    if (now := at(0)) is not None and now[1] % 2:
                        c, j = now
                        pool.wait_ge(s_h_hi[1], ffn.half(c, j))
                        after(pool, s_mm2, ffn.block(c, j) - H_BUFS)
                        pool.tensor_tensor(h_lo[:, j % H_BUFS, :], h[:, j % H_BUFS, :],
                                           h_hi[:, j % H_BUFS, :].bitcast(F32), ALU.subtract)\
                            .then_inc(s_h_lo_odd, 1)
                    if (then := at(NORM)) is not None and then[1] == ffn.nb - 1:
                        inverse_deviation(0, ffn.w(then[0]), CH)
                    for behind, tiles in ((NORM + 3, (0, 1)), (NORM + 5, (2, 3))) if ffn.f == 0 else ():
                        if (then := at(behind)) is None or then[1] != ffn.nb - 1:
                            continue
                        c = then[0]
                        for t in tiles:
                            keep(t, ffn.w(c) + t, x_nat[:, c * CH + t, :], bo_D)
                ffn.chunks(pool, slot, before)

            pool.memset(v_heads[:], 0.0).then_inc(s_zeros, 1)
            pool.memset(minus_half[:], -0.5).then_inc(s_half, 1)
            pool.wait_ge(s_half, 1)
            pool.wait_ge(s_bo, 1)
            sweep(pool, [lin], PAIRS, 3, [(1, split_weights), (2, lin_deviation), (2, lin_keep)])
            pool.wait_ge(s_bo_D, 1)
            attention = [(5, deviation), (1, k_to_heads)]
            sweep(pool, [layer_B], T, 6, attention)
            feed_forward(ffn_C, {LAG + 5: lambda: open_sweep(layer_D, 2, attention)})
            sweep(pool, [layer_D, layer_E], T, 6, attention, opened=2)
            feed_forward(ffn_F)


def constants():
    f32 = np.float32
    feature, head = np.arange(D), np.arange(D) // HD
    row = np.arange(P)
    out = {"ident": np.eye(P, dtype=f32),
           "head_mask": (head[:, None] == np.arange(H)[None, :]).astype(f32),
           "block_mask": (head[:, None] == head[None, :]).astype(f32)}
    keep = (head[None, None, :] % 2 == (row // S)[:, None, None]) & \
        ((head // 2)[None, None, :] % 2 == np.arange(2)[None, :, None])
    out["value_mask"] = keep.astype(f32).reshape(P, 2 * D)
    half = HD // 2
    theta = np.power(f32(1250.0), (f32(-2.0) * np.arange(half, dtype=f32) / f32(HD)).astype(f32)).astype(f32)
    angle = (np.arange(1, S + 1, dtype=f32)[None, :] * np.tile(theta, 2)[feature % HD][:, None]).astype(f32)
    out["cos"] = np.cos(angle).astype(f32)
    out["sin"] = (np.sin(angle) * np.where(feature % HD < half, -1.0, 1.0)[:, None]).astype(f32)
    e = np.arange(NE)
    out["lower"] = np.broadcast_to((e[None, :] < e[:, None]).astype(f32).reshape(1, -1), (P, NE * NE))
    distance = (S - 1 - np.arange(P))
    nb, exact = BUCKETS // 2, BUCKETS // 4
    size = np.abs(distance)
    large = exact + (np.log(np.maximum(size, 1).astype(f32) / exact) / np.log(128 / exact) * (nb - exact))\
        .astype(f32).astype(np.int32)
    bucket = (distance > 0) * nb + np.where(size < exact, size, np.minimum(large, nb - 1))
    hot = np.zeros((P, P), f32)
    for g in range(KEYS):
        m = np.arange(g, P)
        hot[g * BUCKETS + bucket[m - g], m] = 1.0
    out["buckets"] = hot
    out["causal"] = np.where(np.arange(S)[None, :] > (row % S)[:, None], NEG, 0.0).astype(f32)
    out["select"] = (row[None, :] // S == np.arange(BT)[:, None]).astype(f32)
    return out


def arrays(inputs):
    i = {n: np.asarray(a) for n, a in inputs.items()}

    def column(a):
        return np.asarray(a, np.float32).reshape(-1, P).T

    def rows(a):
        return np.broadcast_to(a.reshape(1, -1), (P, a.size))

    turned = np.arange(D) ^ (HD // 2)
    part = constants()
    part["wq_lin"] = i["L0_attn_W_qkv"][:, 0:D]
    part["wkv_lin"] = i["L0_attn_W_qkv"][:, D:3 * D]
    part["bq_lin"] = column(i["L0_attn_b_qkv"][0:D])
    part["bkv_lin"] = rows(i["L0_attn_b_qkv"][D:3 * D])
    heads = np.arange(D).reshape(H, HD)
    by_parity = np.concatenate([heads[0::2], heads[1::2]]).reshape(-1)
    for n in "qkvo":
        part[f"B_w{n}"] = i[f"L0_xattn_W{n}"]
        part[f"D_w{n}"] = i[f"L1_attn_W{n}"].T
        part[f"E_w{n}"] = i[f"L1_xattn_W{n}"].T
        if n != "o":
            part[f"B_b{n}"] = column(i[f"L0_xattn_b{n}"])
            part[f"D_b{n}"] = column(i[f"L1_attn_b{n}"])
    for layer in "BDE":
        part[f"{layer}_wv_parity"] = part[f"{layer}_wv"][:, by_parity]
    for n in "qk":
        part[f"D_w{n}_turned"] = part[f"D_w{n}"][:, turned]
        part[f"D_b{n}_turned"] = part[f"D_b{n}"][turned]
    part["B_bo"] = rows(i["L0_xattn_bo"])
    part["D_bo"] = rows(i["L1_attn_bo"])
    part["C_b1"] = np.concatenate([column(i["L0_ffn_sb1"]), column(i["L0_ffn_rb1"])], 1)
    part["C_b2"] = np.concatenate([column(i["L0_ffn_sb2"]), column(i["L0_ffn_rb2"])], 1)
    part["F_b1"] = column(i["L1_ffn_b1"][NR1 - 1])
    part["F_b2"] = column(i["L1_ffn_b2"][NR1 - 1])
    part["C_gate"] = i["L0_ffn_gate_w"]
    part["C_gate_bias"] = i["L0_ffn_gate_b"].reshape(NE, 1)
    part["F_gate"] = i["L1_ffn_Wr"].T
    part["rel_bias"] = np.zeros((P, KEYS * H), np.float32)
    for g in range(KEYS):
        part["rel_bias"][g * BUCKETS:(g + 1) * BUCKETS, g * H:(g + 1) * H] = i["L1_xattn_rel_bias"].T

    def pack(columns, width):
        out = np.zeros((P, width), np.float32)
        for name, where in columns.items():
            out[0:part[name].shape[0], where] = part[name]
        return out

    experts = [(i["L0_ffn_sw1"][e], i["L0_ffn_sw2"][e]) for e in range(NS)]
    experts += [(i["L0_ffn_rw1"][e], i["L0_ffn_rw2"][e]) for e in range(NE)]
    experts += [(i["L1_ffn_W1"][NR1 - 1], i["L1_ffn_W2"][NR1 - 1])]
    w_experts = np.concatenate(
        [a for w1, w2 in experts for a in (w1, w2.reshape(FB, P, D).transpose(1, 0, 2).reshape(P, F))], 1)
    return {"x": i["x"].reshape(B * S, D), "xT": i["x"].reshape(B * S, D).T, "ctxT": i["ctx_1024"].reshape(B * S, D).T,
            "pack_a": pack(PACK_A, WIDTH_A), "pack_b": pack(PACK_B, WIDTH_B), "w_experts": w_experts,
            "key_mask": i["mask_Bx1x1xS2_bk0"].reshape(T, BT, S).transpose(1, 0, 2).astype(np.int32)}


def kernel(**inputs):
    import concourse.bacc as bacc
    from concourse.bass_utils import run_bass_kernel_spmd

    nc = bacc.Bacc("TRN2", target_bir_lowering=False, num_devices=1)
    given, args = {}, []
    for name, a in arrays(inputs).items():
        a = np.ascontiguousarray(a)
        given[f"in_{name}"] = a
        args.append(nc.dram_tensor(f"in_{name}", a.shape, mybir.dt.from_np(a.dtype), kind="ExternalInput").ap())
    result = nc.dram_tensor("result", (B * S, D), F32, kind="ExternalOutput").ap()
    build(nc, *args, result)
    r = run_bass_kernel_spmd(nc, [given], core_ids=[0])
    return r.results[0]["result"].reshape(B, S, D)
```
